# Optimizing a Trainium2 kernel written in Bass

```python
import numpy as np
import jax
import jax.numpy as jnp

def _softmax(x, axis=-1):
    return jax.nn.softmax(x, axis=axis)

def _gelu(x):
    return jax.nn.gelu(x, approximate=True)

def _silu(x):
    return jax.nn.silu(x)

def _sigmoid(x):
    return jax.nn.sigmoid(x)

def _layernorm(x, axis=-1, eps=1e-05):
    m = jnp.mean(x, axis=axis, keepdims=True)
    v = jnp.var(x, axis=axis, keepdims=True)
    return (x - m) / jnp.sqrt(v + eps)

def _scatter_add(tgt, idx, src, axis=0):
    return tgt.at[idx].add(src)

def _segment_sum(src, seg, n):
    return jax.ops.segment_sum(src, seg, n)
kernel_name = 'mk_seq_preln_d2_jaxref_r8_13f654'

def setup_inputs(seed: int=0):
    np.random.seed(seed)
    _w = jnp.asarray

    def _L0_attn_setup():
        import jax, jax.numpy as jnp
        import numpy as np
        NUM_HEADS = 16
        key = jax.random.key(seed)
        ks = jax.random.split(key, 5)
        B, S, H = (2, 256, 128)
        scale = 0.02
        return {'x': jax.random.normal(ks[0], (B, S, H), dtype=jnp.float32), 'w_qkv': jax.random.normal(ks[1], (H, 3 * H), dtype=jnp.float32) * scale, 'b_qkv': jax.random.normal(ks[2], (3 * H,), dtype=jnp.float32) * scale, 'w_out': jax.random.normal(ks[3], (H, H), dtype=jnp.float32) * scale, 'b_out': jax.random.normal(ks[4], (H,), dtype=jnp.float32) * scale}
    _L0_attn_in = _L0_attn_setup()

    def _L0_ffn_setup():
        import jax, jax.numpy as jnp
        import numpy as np
        H = 128
        I = 256
        E = 32
        B, S = (4, 256)

        def _grouped_mm(a, w, group_sizes):
            return jax.lax.ragged_dot(a, w, group_sizes)

        def _swiglu(x, gw, uw, dw):
            return jax.nn.silu(x @ gw) * (x @ uw) @ dw
        key = jax.random.key(seed)
        ks = jax.random.split(key, 8)
        scale = 0.02
        inp = {'hidden_states': jax.random.normal(ks[0], (B, S, H), dtype=jnp.float32), 'gate_w': jax.random.normal(ks[1], (H, E), dtype=jnp.float32) * scale, 'shared_gate_w': jax.random.normal(ks[2], (H, I), dtype=jnp.float32) * scale, 'shared_up_w': jax.random.normal(ks[3], (H, I), dtype=jnp.float32) * scale, 'shared_down_w': jax.random.normal(ks[4], (I, H), dtype=jnp.float32) * scale, 'routed_gate_w': jax.random.normal(ks[5], (E, H, I), dtype=jnp.float32) * scale, 'routed_up_w': jax.random.normal(ks[6], (E, H, I), dtype=jnp.float32) * scale, 'routed_down_w': jax.random.normal(ks[7], (E, I, H), dtype=jnp.float32) * scale}
        return inp
    _L0_ffn_in = _L0_ffn_setup()

    def _L1_attn_setup():
        import jax, jax.numpy as jnp
        import numpy as np
        import math
        B, N, DIM = (4, 512, 128)
        HEADS, DHEAD, NRF = (16, 64, 64)
        STAB = 1e-06

        def _phi(t, RF):
            return jax.nn.relu(jnp.einsum('bhnd,hdr->bhnr', t, RF))
        key = jax.random.key(seed)
        k1, k2, k3, k4 = jax.random.split(key, 4)
        x = jax.random.normal(k1, (B, N, DIM), dtype=jnp.float32)
        W_qkv = jax.random.normal(k2, (DIM, 3 * HEADS * DHEAD), dtype=jnp.float32) * (1.0 / math.sqrt(DIM))
        RF = jax.random.normal(k3, (HEADS, DHEAD, NRF), dtype=jnp.float32) / math.sqrt(NRF)
        W_out = jax.random.normal(k4, (HEADS * DHEAD, DIM), dtype=jnp.float32) * (1.0 / math.sqrt(HEADS * DHEAD))
        b_out = jnp.zeros((DIM,), dtype=jnp.float32)
        return {'x': x, 'W_qkv': W_qkv, 'RF': RF, 'W_out': W_out, 'b_out': b_out}
    _L1_attn_in = _L1_attn_setup()

    def _L1_ffn_setup():
        import jax, jax.numpy as jnp
        import numpy as np
        HIDDEN = 128
        N_ROUTED = 16
        N_SHARED = 2
        TOP_K = 2
        MID_R = HIDDEN // 4
        MID_S = HIDDEN // 2
        key = jax.random.key(seed)
        ks = jax.random.split(key, 8)
        s = 0.02
        return {'x': jax.random.normal(ks[0], (2, 128, HIDDEN), dtype=jnp.float32), 'router_w': jax.random.normal(ks[1], (HIDDEN, N_ROUTED), dtype=jnp.float32) * s, 'wg_r': jax.random.normal(ks[2], (N_ROUTED, HIDDEN, MID_R), dtype=jnp.float32) * s, 'wu_r': jax.random.normal(ks[3], (N_ROUTED, HIDDEN, MID_R), dtype=jnp.float32) * s, 'wd_r': jax.random.normal(ks[4], (N_ROUTED, MID_R, HIDDEN), dtype=jnp.float32) * s, 'wg_s': jax.random.normal(ks[5], (N_SHARED, HIDDEN, MID_S), dtype=jnp.float32) * s, 'wu_s': jax.random.normal(ks[6], (N_SHARED, HIDDEN, MID_S), dtype=jnp.float32) * s, 'wd_s': jax.random.normal(ks[7], (N_SHARED, MID_S, HIDDEN), dtype=jnp.float32) * s}
    _L1_ffn_in = _L1_ffn_setup()
    _d = {'L0_attn_x': _L0_attn_in['x'], 'L0_attn_w_qkv': _L0_attn_in['w_qkv'], 'L0_attn_b_qkv': _L0_attn_in['b_qkv'], 'L0_attn_w_out': _L0_attn_in['w_out'], 'L0_attn_b_out': _L0_attn_in['b_out'], 'L0_ffn_gate_w': _L0_ffn_in['gate_w'], 'L0_ffn_shared_gate_w': _L0_ffn_in['shared_gate_w'], 'L0_ffn_shared_up_w': _L0_ffn_in['shared_up_w'], 'L0_ffn_shared_down_w': _L0_ffn_in['shared_down_w'], 'L0_ffn_routed_gate_w': _L0_ffn_in['routed_gate_w'], 'L0_ffn_routed_up_w': _L0_ffn_in['routed_up_w'], 'L0_ffn_routed_down_w': _L0_ffn_in['routed_down_w'], 'L1_attn_W_qkv': _L1_attn_in['W_qkv'], 'L1_attn_RF': _L1_attn_in['RF'], 'L1_attn_W_out': _L1_attn_in['W_out'], 'L1_attn_b_out': _L1_attn_in['b_out'], 'L1_ffn_router_w': _L1_ffn_in['router_w'], 'L1_ffn_wg_r': _L1_ffn_in['wg_r'], 'L1_ffn_wu_r': _L1_ffn_in['wu_r'], 'L1_ffn_wd_r': _L1_ffn_in['wd_r'], 'L1_ffn_wg_s': _L1_ffn_in['wg_s'], 'L1_ffn_wu_s': _L1_ffn_in['wu_s'], 'L1_ffn_wd_s': _L1_ffn_in['wd_s']}
    _x0 = _d['L0_attn_x']
    _d['L0_attn_x'] = jax.random.normal(jax.random.fold_in(jax.random.key(seed), 1), (16, 512, 128), dtype=_x0.dtype)
    del _x0
    return _d

def reference(L0_attn_x, L0_attn_w_qkv, L0_attn_b_qkv, L0_attn_w_out, L0_attn_b_out, L0_ffn_gate_w, L0_ffn_shared_gate_w, L0_ffn_shared_up_w, L0_ffn_shared_down_w, L0_ffn_routed_gate_w, L0_ffn_routed_up_w, L0_ffn_routed_down_w, L1_attn_W_qkv, L1_attn_RF, L1_attn_W_out, L1_attn_b_out, L1_ffn_router_w, L1_ffn_wg_r, L1_ffn_wu_r, L1_ffn_wd_r, L1_ffn_wg_s, L1_ffn_wu_s, L1_ffn_wd_s):

    def _L0_attn_ref(x, w_qkv, b_qkv, w_out, b_out):
        import jax, jax.numpy as jnp
        import numpy as np
        NUM_HEADS = 16
        B, S, H = x.shape
        nh = NUM_HEADS
        hd = H // nh
        attn_scale = 1.0 / np.sqrt(hd).astype(np.float32)
        qkv = x @ w_qkv + b_qkv
        q, k, v = jnp.split(qkv, 3, axis=-1)
        to_heads = lambda t: t.reshape(B, S, nh, hd).transpose(0, 2, 1, 3)
        q, k, v = (to_heads(q), to_heads(k), to_heads(v))
        scores = jnp.einsum('bhid,bhjd->bhij', q, k) * attn_scale
        i = jnp.arange(S)[:, None]
        j = jnp.arange(S)[None, :]
        scores = jnp.where(j >= i, scores, -jnp.inf)
        attn = jax.nn.softmax(scores, axis=-1)
        out = jnp.einsum('bhij,bhjd->bhid', attn, v)
        out = out.transpose(0, 2, 1, 3).reshape(B, S, H)
        return out @ w_out + b_out

    def _L0_ffn_ref(hidden_states, gate_w, shared_gate_w, shared_up_w, shared_down_w, routed_gate_w, routed_up_w, routed_down_w):
        import jax, jax.numpy as jnp
        import numpy as np
        H = 128
        I = 256
        E = 32
        B, S = (4, 256)

        def _grouped_mm(a, w, group_sizes):
            return jax.lax.ragged_dot(a, w, group_sizes)

        def _swiglu(x, gw, uw, dw):
            return jax.nn.silu(x @ gw) * (x @ uw) @ dw
        b, s, h = hidden_states.shape
        x = hidden_states.reshape(-1, h)
        shared_out = _swiglu(x, shared_gate_w, shared_up_w, shared_down_w)
        logits = x @ gate_w
        topk_ids = jnp.argmax(logits, axis=-1)
        topk_val = jnp.max(logits, axis=-1)
        scores = jax.nn.sigmoid(topk_val)[:, None]
        xs = x * scores
        tokens_per_expert = jnp.zeros((E,), jnp.int32).at[topk_ids].add(1)
        order = jnp.argsort(topk_ids)
        sorted_x = xs[order]
        g = _grouped_mm(sorted_x, routed_gate_w, tokens_per_expert)
        u = _grouped_mm(sorted_x, routed_up_w, tokens_per_expert)
        d = _grouped_mm(jax.nn.silu(g) * u, routed_down_w, tokens_per_expert)
        inv = jnp.argsort(order)
        routed_out = d[inv]
        return (shared_out + routed_out).reshape(b, s, h)

    def _L1_attn_ref(x, W_qkv, RF, W_out, b_out):
        import jax, jax.numpy as jnp
        import numpy as np
        import math
        B, N, DIM = (4, 512, 128)
        HEADS, DHEAD, NRF = (16, 64, 64)
        STAB = 1e-06

        def _phi(t, RF):
            return jax.nn.relu(jnp.einsum('bhnd,hdr->bhnr', t, RF))
        b, n, _ = x.shape
        qkv = x @ W_qkv
        q, k, v = jnp.split(qkv, 3, axis=-1)

        def to_heads(t):
            return t.reshape(b, n, HEADS, DHEAD).transpose(0, 2, 1, 3)
        q, k, v = (to_heads(q), to_heads(k), to_heads(v))
        phi_q = _phi(q, RF)
        phi_k = _phi(k, RF)
        kv = jnp.einsum('bhnr,bhnd->bhrd', phi_k, v)
        out = jnp.einsum('bhnr,bhrd->bhnd', phi_q, kv)
        k_sum = phi_k.sum(axis=2)
        normalizer = jnp.einsum('bhnr,bhr->bhn', phi_q, k_sum)[..., None] + STAB
        out = out / normalizer
        out = out.transpose(0, 2, 1, 3).reshape(b, n, HEADS * DHEAD)
        out = out @ W_out + b_out
        return out

    def _L1_ffn_ref(x, router_w, wg_r, wu_r, wd_r, wg_s, wu_s, wd_s):
        import jax, jax.numpy as jnp
        import numpy as np
        HIDDEN = 128
        N_ROUTED = 16
        N_SHARED = 2
        TOP_K = 2
        MID_R = HIDDEN // 4
        MID_S = HIDDEN // 2
        orig_shape = x.shape
        flat = x.reshape(-1, orig_shape[-1])
        gs = jnp.einsum('td,ndm->tnm', flat, wg_s)
        us = jnp.einsum('td,ndm->tnm', flat, wu_s)
        out = jnp.einsum('tnm,nmd->td', jax.nn.silu(gs) * us, wd_s)
        logits = (flat @ router_w).astype(jnp.float32)
        probs = jax.nn.softmax(logits, axis=-1)
        weights, indices = jax.lax.top_k(probs, TOP_K)
        weights = weights / (weights.sum(axis=-1, keepdims=True) + 1e-09)
        weights = weights.astype(x.dtype)
        comb = jnp.sum(jax.nn.one_hot(indices, N_ROUTED, dtype=x.dtype) * weights[..., None], axis=1)
        g = jnp.einsum('td,edm->tem', flat, wg_r)
        u = jnp.einsum('td,edm->tem', flat, wu_r)
        h = jax.nn.silu(g) * u
        h = h * comb[:, :, None]
        out = out + jnp.einsum('tem,emd->td', h, wd_r)
        return out.reshape(orig_shape)
    x = L0_attn_x
    x = x + _L0_attn_ref(_layernorm(x, axis=-1), L0_attn_w_qkv, L0_attn_b_qkv, L0_attn_w_out, L0_attn_b_out)
    x = x + _L0_ffn_ref(_layernorm(x, axis=-1), L0_ffn_gate_w, L0_ffn_shared_gate_w, L0_ffn_shared_up_w, L0_ffn_shared_down_w, L0_ffn_routed_gate_w, L0_ffn_routed_up_w, L0_ffn_routed_down_w)
    x = x + _L1_attn_ref(_layernorm(x, axis=-1), L1_attn_W_qkv, L1_attn_RF, L1_attn_W_out, L1_attn_b_out)
    x = x + _L1_ffn_ref(_layernorm(x, axis=-1), L1_ffn_router_w, L1_ffn_wg_r, L1_ffn_wu_r, L1_ffn_wd_r, L1_ffn_wg_s, L1_ffn_wu_s, L1_ffn_wd_s)
    return x

_drawn_inputs = setup_inputs


def setup_inputs(seed=0):
    import zlib

    import numpy as np

    out = dict(_drawn_inputs(seed))
    spreads = {'L1_attn_b_out': (0.0, 0.31)}
    factors = {'L0_attn_w_qkv': 8.0,
     'L0_attn_b_qkv': 8.0,
     'L0_attn_w_out': 5.779,
     'L0_ffn_gate_w': 8.0,
     'L0_ffn_shared_gate_w': 6.819,
     'L0_ffn_shared_up_w': 6.758,
     'L0_ffn_shared_down_w': 6.816,
     'L0_ffn_routed_gate_w': 8.0,
     'L0_ffn_routed_up_w': 8.0,
     'L0_ffn_routed_down_w': 8.0,
     'L1_ffn_router_w': 8.0,
     'L1_ffn_wg_r': 8.0,
     'L1_ffn_wu_r': 8.0,
     'L1_ffn_wd_r': 8.0,
     'L1_ffn_wg_s': 8.0,
     'L1_ffn_wu_s': 8.0,
     'L1_ffn_wd_s': 8.0,
     'L1_attn_RF': 5.164}
    for name, (base, spread) in spreads.items():
        noise = np.random.default_rng([zlib.crc32(name.encode()), seed]).standard_normal(out[name].shape)
        drawn = base * np.exp(spread * noise) if base else spread * noise
        out[name] = jnp.asarray(drawn.astype(out[name].dtype))
    for name, factor in factors.items():
        out[name] = (out[name] * factor).astype(out[name].dtype)
    return out
```

```python
from contextlib import ExitStack

import concourse.bass as bass
from concourse import mybir
from concourse.bass import ds

F32 = mybir.dt.float32
F32R = mybir.dt.float32r
BF16 = mybir.dt.bfloat16
I32 = mybir.dt.int32
ALU = mybir.AluOpType
ACT = mybir.ActivationFunctionType
AX = mybir.AxisListType

P = 128
D = 128
NB, SEQ = 16, 512
NT = SEQ // P
TILES = NB * NT
EPS = 1e-5

E0, MID0 = 32, 256
SLOTS = TILES + E0
ZERO_TILES = 24

H1, HD1 = 16, 64

H0, HD0 = 16, 8
GROUPS = 4
GH = H0 // GROUPS
SLOT = 32
MAXROW_HI, MAXROW_LO = 24, 25
ONES_COL = 8
BIG = 1e30
STEPS = NB * GROUPS
SCORE_TILES = [(s, h, n) for s, n in enumerate((1, 1, 2, 4)) for h in range(0, GH, n)]
UNITS = len(SCORE_TILES)
FIRST_UNIT = [next(u for u, t in enumerate(SCORE_TILES) if t[0] == s) for s in range(NT)] + [UNITS]
A_BANKS, B_BANKS = 3, 2
HALF_BEFORE = (0, 2)
FIN_AFTER = (1, 2)


def score_bank(banks, g, u):
    return (UNITS * g + u) % banks


def read_before(banks, g, u):
    at = UNITS * g + u - 1
    while score_bank(banks, 0, at % (UNITS * GROUPS)) != score_bank(banks, g, u):
        at -= 1
    return at + 1


def wait(eng, sem, batch, per_batch, n, total):
    if isinstance(batch, int):
        value = min(batch * per_batch + n, total)
        if value > 0:
            eng.wait_ge(sem, value)
    else:
        eng.wait_ge(sem, batch * per_batch + n)


def wait_first(eng, own, sem, batch, per_batch, n, total):
    wait(eng, sem, batch, per_batch, n, total)
    eng.sem_inc(own, 1)


def shifted(batch, group, by):
    at = group + by
    return batch + at // GROUPS, at % GROUPS


def exists(batch):
    return not isinstance(batch, int) or 0 <= batch < NB


def layer0_attention(nc, mem, dram, x_sorted):
    x_res, mean2, rstd2, logits = mem["x_res"], mem["mean2"], mem["rstd2"], mem["logits"]
    ident, ident_r = mem["ident"], mem["ident_r"]
    with ExitStack() as ctx:
        def sb(name, shape, dt=F32):
            return ctx.enter_context(nc.sbuf_tensor(name, shape, dt))

        def pb(name, shape, dt=F32):
            return ctx.enter_context(nc.psum_tensor(name, shape, dt))

        def sem(name):
            return ctx.enter_context(nc.semaphore(name))

        zeros = sb("zeros", [P, D])
        stage = sb("stage", [P, 512])
        w_q = sb("w_q", [P, 2, GROUPS, P], F32R)
        w_k = sb("w_k", [P, 2, GROUPS, P], F32R)
        w_v = sb("w_v", [P, 2, P], F32R)
        w_o = sb("w_o", [P, P])
        w_router = sb("w_router", [P, 32])
        b_qk = sb("b_qk", [P, 2, GROUPS])
        lo_rows = sb("lo_rows", [P, 2])
        b_qk_lo = sb("b_qk_lo", [P, 2, GROUPS])
        b_v = sb("b_v", [P, D])
        b_o = sb("b_o", [P, D])
        ident_b = sb("ident_b", [P, P], BF16)
        mask = sb("mask", [P, P])
        mask_b = sb("mask_b", [P, P], BF16)
        minus_half = sb("minus_half", [P, NT])

        stat1 = sb("stat1", [P, NT, 6])
        mv1 = sb("mv1", [P, NT, 2])
        veps1 = sb("veps1", [P, NT])
        rstd1 = sb("rstd1", [P, NT])
        xn = sb("xn", [P, NT, D])
        xt_hi = sb("xt_hi", [P, SEQ], F32R)
        xt_lo = sb("xt_lo", [P, SEQ], F32R)
        half = sb("half", [P, 2, SEQ], F32R)
        q_pk = sb("q_pk", [P, GROUPS, SEQ], F32R)
        k_pk = sb("k_pk", [P, 2, SEQ], F32R)
        k_z = sb("k_z", [P, GROUPS, GH, SEQ], F32R)
        v_pk = sb("v_pk", [P, NT, H0, SLOT])
        neg_max = sb("neg_max", [P, 2, NT, GH])
        max_pad = sb("max_pad", [P, 2, NT, P], F32R)
        probs = sb("probs", [P, 2, GH, SEQ])
        o_sb = sb("o_sb", [P, 2, SEQ])
        rsum = sb("rsum", [P, NT * GH])
        attn = sb("attn", [P, NT, D])
        attn_t = sb("attn_t", [P, SEQ])
        stat_tmp = sb("stat_tmp", [P, NT, 6])
        mv2 = sb("mv2", [P, NT, 2])
        veps2 = sb("veps2", [P, NT])
        xn2 = sb("xn2", [P, NT, D])
        xn2_t = sb("xn2_t", [P, SEQ])

        ps_a = [pb(f"ps_a{i}", [P, 512]) for i in range(A_BANKS)]
        ps_b = [pb(f"ps_b{i}", [P, 512]) for i in range(B_BANKS)]
        ps_o = pb("ps_o", [P, 512])
        ps_m = [pb(f"ps_m{i}", [P, 512]) for i in range(2)]

        s_w = sem("s_w")
        s_split = sem("s_split")
        s_stage = sem("s_stage")
        s_x0, s_xr = sem("s_x0"), sem("s_xr")
        s_tab = sem("s_tab")
        s_kz = [sem("s_kz0"), sem("s_kz1")]
        s_set = sem("s_set")
        s_bn, s_bn2 = sem("s_bn"), sem("s_bn2")
        s_veps1, s_rstd1, s_xn = sem("s_veps1"), sem("s_rstd1"), sem("s_xn")
        s_mx, s_xh, s_xl = sem("s_mx"), sem("s_xh"), sem("s_xl")
        s_proj, s_half, s_fin = sem("s_proj"), sem("s_half"), sem("s_fin")
        s_vps, s_v = sem("s_vps"), sem("s_v")
        s_a, s_max = sem("s_a"), sem("s_max")
        s_mhi, s_mlo, s_mps, s_qmax = sem("s_mhi"), sem("s_mlo"), sem("s_mps"), sem("s_qmax")
        s_b, s_exp, s_mask, s_pv, s_o = sem("s_b"), sem("s_exp"), sem("s_mask"), sem("s_pv"), sem("s_o")
        s_ot, s_rs, s_attn = sem("s_ot"), sem("s_rs"), sem("s_attn")
        s_atps, s_at, s_ops, s_x1 = sem("s_atps"), sem("s_at"), sem("s_ops"), sem("s_x1")
        s_bo = sem("s_bo")
        s_zero, s_zeroed = sem("s_zero"), sem("s_zeroed")
        s_own_d, s_own_p, s_own_s = sem("s_own_d"), sem("s_own_p"), sem("s_own_s")
        s_mean2 = sem("s_mean2")
        s_veps2, s_rstd2, s_xn2 = sem("s_veps2"), sem("s_rstd2"), sem("s_xn2")
        s_n2ps, s_n2t, s_lgps, s_lg = sem("s_n2ps"), sem("s_n2t"), sem("s_lgps"), sem("s_lg")

        STEP4 = GROUPS
        UNIT = GROUPS * UNITS
        SPREAD = 16 * GH * GROUPS // 2

        block = ctx.enter_context(nc.Block())

        @block.sync
        def _(sp):
            x_dram = dram["x"].rearrange("(b t p) d -> b p t d", p=P, t=NT)
            sp.dma_start(x_res[:, 0:NT, :], x_dram[0]).then_inc(s_x0, 16)
            for dst, name in ((w_o[:], "w_o0"), (w_router[:], "router0"), (b_qk[:], "b_qk"),
                              (lo_rows[:], "lo_rows"), (b_v[:], "b_v"), (b_o[:], "b_o0"),
                              (mask[:], "mask"), (ident[:], "ident")):
                sp.dma_start(dst, dram[name]).then_inc(s_w, 16)
            for n, (name, width) in enumerate((("w_q4", 512), ("w_k4", 512), ("w_v0", 128))):
                if n:
                    sp.wait_ge(s_split, 2 * n)
                sp.dma_start(stage[:, 0:width], dram[name]).then_inc(s_stage, 16)
            for b in range(1, NB):
                sp.dma_start(x_res[:, b * NT:(b + 1) * NT, :], x_dram[b]).then_inc(s_xr, 16)
            sp.wait_ge(s_zero, 1)
            for part in x_sorted.rearrange("(c q p) d -> c p q d", p=P, q=ZERO_TILES):
                sp.dma_start(part, zeros[:].unsqueeze(1).broadcast_to([P, ZERO_TILES, D])).then_inc(s_zeroed, 16)

            def body(b):
                for g in range(GROUPS):
                    bp, gp = shifted(b, g, 3)
                    if exists(bp):
                        wait_first(sp, s_own_s, s_fin, bp, 2 * STEP4, 2 * gp + 1, 2 * STEPS)
                        wait(sp, s_b, b, UNIT, UNITS * g, UNITS * STEPS)
                        for h in range(GH):
                            rows = slice(SLOT * h, SLOT * (h + 1))
                            sp.dma_start(k_z[rows, gp, h, :].bitcast(F32),
                                         k_pk[rows, gp % 2, :].bitcast(F32)).then_inc(s_kz[gp % 2], 16)

            sp.wait_ge(s_set, 5)
            body(-1)
            body(0)
            body(1)
            with sp.Fori(2, NB - 1) as b:
                body(b)
            body(NB - 1)
            sp.wait_ge(s_zeroed, 16 * SLOTS // ZERO_TILES)

        @block.tensor
        def _(pe):
            def score_tiles(b, g, s, do_a, do_b):
                ba, ga = shifted(b, g, 2)
                n = SEQ - s * P
                for u in range(FIRST_UNIT[s], FIRST_UNIT[s + 1]):
                    _, h0, heads = SCORE_TILES[u]
                    if do_a:
                        if u == 0:
                            wait(pe, s_fin, ba, 2 * STEP4, 2 * ga + 2, 2 * STEPS)
                            wait(pe, s_kz[ga % 2], ba, SPREAD, 16 * GH * (ga // 2 + 1), SPREAD * NB)
                        wait(pe, s_max, ba, UNIT, read_before(A_BANKS, ga, u), UNITS * STEPS)
                        bank = ps_a[score_bank(A_BANKS, ga, u)]
                        pe.matmul(bank[:, 0:heads * n], q_pk[:, ga, s * P:(s + 1) * P],
                                  k_z[:, ga, h0:h0 + heads, s * P:SEQ], start=True, stop=False,
                                  skip_group_check=True)
                        pe.matmul(bank[:, 0:heads * n].rearrange("p (h c) -> p h c", h=heads)[:, :, 0:P],
                                  ident_b[:], mask_b[:].unsqueeze(1).broadcast_to([P, heads, P]),
                                  start=False, stop=True, skip_group_check=True).then_inc(s_a, 1)
                    if do_b:
                        if u == 0:
                            wait(pe, s_qmax, b, STEP4, g + 1, STEPS)
                        wait(pe, s_exp, b, UNIT, read_before(B_BANKS, g, u), UNITS * STEPS)
                        kb = NT - 1 - s
                        for h in range(heads):
                            last = pe.matmul(ps_b[score_bank(B_BANKS, g, u)][:, h * n:(h + 1) * n],
                                             k_z[:, g, h0 + h, kb * P:(kb + 1) * P], q_pk[:, g, 0:n],
                                             start=(h == 0), stop=(h == heads - 1), skip_group_check=True)
                        last.then_inc(s_b, 1)

            def probs_times_v(b, g, s):
                n = SEQ - s * P
                if s == 0:
                    wait(pe, s_o, b, STEP4, g, STEPS)
                    if g == 0:
                        wait(pe, s_v, b, 1, 1, NB)
                wait(pe, s_mask, b, NT * STEP4, NT * g + s + 1, NT * STEPS)
                for j in range(GH):
                    last = pe.matmul(ps_o[SLOT * j:SLOT * (j + 1), 0:n], v_pk[:, NT - 1 - s, GH * g + j, :],
                                     probs[:, s % 2, j, 0:n], start=(s == 0), stop=(s == NT - 1),
                                     skip_group_check=True)
                last.then_inc(s_pv, 1)

            def three_passes(out, pairs):
                (a_hi, a_lo), (c_hi, c_lo) = pairs
                pe.matmul(out, a_hi, c_hi, start=True, stop=False)
                pe.matmul(out, a_lo, c_hi, start=False, stop=False)
                return pe.matmul(out, a_hi, c_lo, start=False, stop=True)

            def batch_jobs_read(b, g):
                if isinstance(b, int):
                    wait(pe, s_at, b, 1, 0 if g >= 1 else -1, NB)
                    wait(pe, s_n2t, b, 1, 0 if g >= 3 else -1, NB)
                    wait(pe, s_lg, b, 1, -1, NB)
                    wait(pe, s_xl, b, 1, 2 if g >= 1 else 1, NB)
                    wait(pe, s_x1, b, 1, 0 if g >= 2 else -1, NB)
                    wait(pe, s_v, b, 1, 1, NB)
                    wait(pe, s_qmax, b, STEP4, g + 1, STEPS)
                    wait(pe, s_attn, b, STEP4, g - 1, STEPS)

            def side_jobs(b, g, s):
                bp, gp = shifted(b, g, 3)
                if s == 0 and exists(bp):
                    wait(pe, s_xl, bp, 1, 1, NB)
                    batch_jobs_read(b, g)
                    if g == 0:
                        wait(pe, s_lg, b, 1, -1, NB)
                    elif g == 1:
                        wait(pe, s_at, b, 1, 0, NB)
                    elif g == 2:
                        wait(pe, s_qmax, b, STEP4, g + 1, STEPS)
                    else:
                        wait(pe, s_n2t, b, 1, 0, NB)
                    wk, wq = w_k[:, :, gp, :], w_q[:, :, gp, :]
                    x_pair = (xt_hi[:], xt_lo[:])
                    three_passes(ps_m[0][:], ((wk[:, 0], wk[:, 1]), x_pair)).then_inc(s_proj, 1)
                    if g == 0:
                        wait(pe, s_v, b, 1, 1, NB)
                    elif g == 2:
                        wait(pe, s_x1, b, 1, 0, NB)
                    elif g == 3:
                        wait(pe, s_attn, b, STEP4, g - 1, STEPS)
                    three_passes(ps_m[1][:], ((wq[:, 0], wq[:, 1]), x_pair)).then_inc(s_proj, 1)
                if s == 2:
                    batch_jobs_read(b, g)
                    bm, gm = shifted(b, g, 1)
                    if exists(bm):
                        wait(pe, s_fin, bp, 2 * STEP4, 2 * gp + 1, 2 * STEPS)
                        wait(pe, s_mlo, bm, STEP4, gm + 1, STEPS)
                        for t in range(NT):
                            last = pe.matmul(ps_m[0][:, t * P:(t + 1) * P], max_pad[:, gm % 2, t, :], ident_r[:],
                                             start=True, stop=True)
                        last.then_inc(s_mps, 1)
                    bo, go = shifted(b, g, -1)
                    if exists(bo):
                        wait(pe, s_fin, bp, 2 * STEP4, 2 * gp + 2, 2 * STEPS)
                        wait(pe, s_o, b, STEP4, g, STEPS)
                        for t in range(NT):
                            last = pe.transpose(ps_m[1][:, t * P:(t + 1) * P],
                                                o_sb[:, go % 2, t * P:(t + 1) * P], ident[:])
                        last.then_inc(s_ot, 1)
                if s != 3:
                    return
                m0_jobs = g in (0, 2, 3) and exists(b - 1)
                m1_jobs = (g == 1 and exists(b - 1)) or (g in (0, 3) and exists(b + 1))
                if m0_jobs or m1_jobs:
                    wait(pe, s_fin, bp, 2 * STEP4, 2 * gp + 2, 2 * STEPS)
                    batch_jobs_read(b, g)
                if m0_jobs:
                    wait(pe, s_qmax, b, STEP4, g + 2, STEPS)
                if m1_jobs:
                    wait(pe, s_attn, b, STEP4, g, STEPS)
                if g == 0:
                    if exists(b - 1):
                        wait(pe, s_attn, b, STEP4, 0, STEPS)
                        for t in range(NT):
                            last = pe.transpose(ps_m[0][:, t * P:(t + 1) * P], attn[:, t, :], ident[:])
                        last.then_inc(s_atps, 1)
                    if exists(b + 1):
                        wait(pe, s_xn, b, 1, 2, NB)
                        for t in range(NT):
                            last = pe.transpose(ps_m[1][:, t * P:(t + 1) * P], xn[:, t, :], ident[:])
                        last.then_inc(s_mx, 1)
                if g == 1 and exists(b - 1):
                    wait(pe, s_at, b, 1, 0, NB)
                    for t in range(NT):
                        last = pe.matmul(ps_m[1][:, t * P:(t + 1) * P], attn_t[:, t * P:(t + 1) * P], w_o[:],
                                         start=True, stop=True)
                    last.then_inc(s_ops, 1)
                if g == 2 and exists(b - 1):
                    wait(pe, s_xn2, b, 1, 0, NB)
                    for t in range(NT):
                        last = pe.transpose(ps_m[0][:, t * P:(t + 1) * P], xn2[:, t, :], ident[:])
                    last.then_inc(s_n2ps, 1)
                if g == 3 and exists(b - 1):
                    wait(pe, s_n2t, b, 1, 0, NB)
                    for t in range(NT):
                        last = pe.matmul(ps_m[0][:, 32 * t:32 * (t + 1)], xn2_t[:, t * P:(t + 1) * P], w_router[:],
                                         start=True, stop=True)
                    last.then_inc(s_lgps, 1)
                if g == 3 and exists(b + 1):
                    for t in range(NT):
                        x_pair = (xt_hi[:, t * P:(t + 1) * P], xt_lo[:, t * P:(t + 1) * P])
                        last = three_passes(ps_m[1][:, t * P:(t + 1) * P], (x_pair, (w_v[:, 0], w_v[:, 1])))
                    last.then_inc(s_vps, 1)

            def body(b):
                for g in range(GROUPS):
                    do_a = exists(shifted(b, g, 2)[0])
                    do_b = exists(b)
                    for s in range(NT):
                        score_tiles(b, g, s, do_a, do_b)
                        bv, gv = (b, g) if s else shifted(b, g, -1)
                        if exists(bv):
                            probs_times_v(bv, gv, (s - 1) % NT)
                        side_jobs(b, g, s)

            pe.wait_ge(s_split, 9)
            pe.wait_ge(s_w, 16 * 8)
            body(-1)
            body(0)
            body(1)
            with pe.Fori(2, NB - 1) as b:
                body(b)
            body(NB - 1)
            body(NB)

        @block.scalar
        def _(act):
            def high_half(b, g, i):
                bp, gp = shifted(b, g, 3)
                if exists(bp):
                    wait(act, s_proj, bp, 2 * STEP4, 2 * gp + i + 1, 2 * STEPS)
                    wait(act, s_fin, bp, 2 * STEP4, 2 * (gp - 1) + i + 1, 2 * STEPS)
                    act.activation(half[:, i, :], ps_m[i][:], ACT.Identity, bias=b_qk_lo[:, 1 - i, gp:gp + 1],
                                   scale=lo_rows[:, 1 - i:2 - i]).then_inc(s_half, 1)

            def body(b):
                for g in range(GROUPS):
                    for s in range(NT):
                        n = SEQ - s * P
                        if exists(b):
                            wait(act, s_pv, b, NT * STEP4, NT * g + s - 1, NT * STEPS)
                        for u in range(FIRST_UNIT[s], FIRST_UNIT[s + 1]):
                            if s == 1 and u - FIRST_UNIT[s] in HALF_BEFORE:
                                high_half(b, g, HALF_BEFORE.index(u - FIRST_UNIT[s]))
                            if exists(b):
                                _, h0, heads = SCORE_TILES[u]
                                wait(act, s_b, b, UNIT, UNITS * g + u + 1, UNITS * STEPS)
                                act.activation(probs[:, s % 2, h0:h0 + heads, 0:n],
                                               ps_b[score_bank(B_BANKS, g, u)][:, 0:heads * n].rearrange("p (h c) -> p h c", h=heads),
                                               ACT.Exp, scale=HD0 ** -0.5).then_inc(s_exp, 1)
                        bo, go = shifted(b, g, -1)
                        if s == 0 and exists(bo):
                            wait(act, s_pv, b, NT * STEP4, NT * g, NT * STEPS)
                            wait(act, s_ot, b, STEP4, g - 2, STEPS)
                            act.copy(o_sb[:, go % 2, :], ps_o[:]).then_inc(s_o, 1)
                        if (g, s) == (0, 3):
                            if exists(b - 1):
                                wait(act, s_atps, b, 1, 0, NB)
                                wait(act, s_ops, b, 1, -1, NB)
                                act.copy(attn_t[:], ps_m[0][:]).then_inc(s_at, 1)
                            if exists(b + 1):
                                wait(act, s_mx, b, 1, 2, NB)
                                act.copy(xt_hi[:], ps_m[1][:]).then_inc(s_xh, 1)
                        if (g, s) == (2, 3) and exists(b - 1):
                            wait(act, s_n2ps, b, 1, 0, NB)
                            wait(act, s_lgps, b, 1, -1, NB)
                            act.copy(xn2_t[:], ps_m[0][:]).then_inc(s_n2t, 1)

            act.wait_ge(s_split, 10)
            act.wait_ge(s_w, 16 * 8)
            act.activation(rsum[:, 0:1], minus_half[:, 0:1], ACT.Exp).then_inc(s_tab, 1)
            body(-1)
            body(0)
            body(1)
            with act.Fori(2, NB - 1) as b:
                body(b)
            body(NB - 1)
            body(NB)

        @block.vector
        def _(dve):
            def finish_projection(b, g, i):
                bp, gp = shifted(b, g, 3)
                if not exists(bp):
                    return
                if i == 0:
                    wait(dve, s_kz[gp % 2], bp, SPREAD, 16 * GH * (gp // 2), SPREAD * NB)
                wait(dve, s_half, bp, 2 * STEP4, 2 * gp + i + 1, 2 * STEPS)
                dve.scalar_tensor_tensor((k_pk[:, gp % 2, :], q_pk[:, gp, :])[i], ps_m[i][:],
                                         b_qk[:, 1 - i, gp:gp + 1], half[:, i, :].bitcast(F32), ALU.add,
                                         ALU.subtract).then_inc(s_fin, 1)

            def body(b):
                for g in range(GROUPS):
                    for s in range(NT):
                        n = SEQ - s * P
                        ba, ga = shifted(b, g, 2)
                        for u in range(FIRST_UNIT[s], FIRST_UNIT[s + 1]):
                            if exists(ba):
                                _, h0, heads = SCORE_TILES[u]
                                wait(dve, s_a, ba, UNIT, UNITS * ga + u + 1, UNITS * STEPS)
                                dve.tensor_reduce(neg_max[:, ga % 2, s, h0:h0 + heads],
                                                  ps_a[score_bank(A_BANKS, ga, u)][:, 0:heads * n].rearrange("p (h c) -> p h c", h=heads),
                                                  AX.X, ALU.max, negate=True).then_inc(s_max, 1)
                            if s == 1 and u - FIRST_UNIT[s] in FIN_AFTER:
                                finish_projection(b, g, FIN_AFTER.index(u - FIRST_UNIT[s]))
                        if (g, s) == (0, 0) and exists(b):
                            wait(dve, s_vps, b, 1, 1, NB)
                            wait(dve, s_pv, b, NT * STEP4, 0, NT * STEPS)
                            dve.tensor_tensor(v_pk[:, :, :, 0:HD0].rearrange("p t h d -> p t h d"),
                                              ps_m[1][:].rearrange("p (t h d) -> p t h d", t=NT, d=HD0),
                                              b_v[:].rearrange("p (h d) -> p h d", d=HD0).unsqueeze(1)
                                              .broadcast_to([P, NT, H0, HD0]), ALU.add).then_inc(s_v, 1)
                        if (g, s) == (0, 0) and exists(b + 1):
                            if isinstance(b, int):
                                dve.wait_ge(s_x0 if b < 0 else s_xr, 16 if b < 0 else 16 * (NB - 1))
                            for t in range(NT):
                                dve.bn_stats(stat1[:, t, :], x_res[:, (b + 1) * NT + t, :]).then_inc(s_bn, 1)
                            wait_first(dve, s_own_d, s_bn, b, 2 * NT, 3 * NT, 1 << 20)
                            for t in range(NT):
                                dve.bn_aggr(mv1[:, t, :], stat1[:, t, :]).then_inc(s_bn, 1)
                            wait(dve, s_bn, b, 2 * NT, 4 * NT, 1 << 20)
                            dve.tensor_scalar(veps1[:], mv1[:, :, 1], EPS, None, ALU.add).then_inc(s_veps1, 1)
                        bm, gm = shifted(b, g, 1)
                        if s == 2 and exists(bm):
                            wait(dve, s_mps, bm, STEP4, gm + 1, STEPS)
                            dve.tensor_tensor(q_pk[:, gm, :], ps_m[0][:], q_pk[:, gm, :].bitcast(F32),
                                              ALU.add).then_inc(s_qmax, 1)
                        bo, go = shifted(b, g, -1)
                        if s == 2 and exists(bo):
                            wait(dve, s_ot, b, STEP4, g, STEPS)
                            heads = ps_m[1][:].rearrange("p (n c) -> p n c", c=SLOT)
                            dve.reciprocal(rsum[:], heads[:, :, ONES_COL]).then_inc(s_rs, 1)
                            wait(dve, s_rs, b, STEP4, g, STEPS)
                            if g == 1:
                                wait(dve, s_atps, b, 1, 0, NB)
                            dve.tensor_tensor(
                                attn[:, :, GH * HD0 * go:GH * HD0 * (go + 1)].rearrange("p t (h d) -> p t h d", d=HD0),
                                ps_m[1][:].rearrange("p (t h c) -> p t h c", t=NT, c=SLOT)[:, :, :, 0:HD0],
                                rsum[:].rearrange("p (t h) -> p t h", t=NT).unsqueeze(3)
                                .broadcast_to([P, NT, GH, HD0]), ALU.mult).then_inc(s_attn, 1)
                        bp, gp = shifted(b, g, 3)
                        if (g, s) == (0, 2) and exists(b + 1):
                            wait(dve, s_rstd1, b, 1, 2, NB)
                            wait(dve, s_mx, b, 1, 1, NB)
                            for t in range(NT):
                                last = dve.tensor_scalar(xn[:, t, :], x_res[:, (b + 1) * NT + t, :], mv1[:, t, 0:1],
                                                         rstd1[:, t:t + 1], ALU.subtract, ALU.mult)
                            last.then_inc(s_xn, 1)
                        if (g, s) == (0, 3) and exists(b + 1):
                            wait(dve, s_xh, b, 1, 2, NB)
                            dve.tensor_tensor(xt_lo[:], ps_m[1][:], xt_hi[:].bitcast(F32),
                                              ALU.subtract).then_inc(s_xl, 1)
                        if (g, s) == (1, 3) and exists(b - 1):
                            wait(dve, s_ops, b, 1, 0, NB)
                            wait(dve, s_bo, b, 1, 0, NB)
                            x_b = x_res[:, ds((b - 1) * NT, NT), :]
                            dve.tensor_tensor(x_b, ps_m[1][:].rearrange("p (t d) -> p t d", t=NT), x_b,
                                              ALU.add).then_inc(s_x1, 1)
                        if (g, s) == (2, 0) and exists(b - 1):
                            wait_first(dve, s_own_d, s_x1, b, 1, 0, NB)
                            for t in range(NT):
                                dve.bn_stats(stat_tmp[:, t, :], x_res[:, (b - 1) * NT + t, :]).then_inc(s_bn2, 1)
                            wait_first(dve, s_own_d, s_bn2, b, 2 * NT, -NT, 1 << 20)
                            for t in range(NT):
                                dve.bn_aggr(mv2[:, t, :], stat_tmp[:, t, :]).then_inc(s_bn2, 1)
                            wait(dve, s_bn2, b, 2 * NT, 0, 1 << 20)
                            dve.tensor_scalar(veps2[:], mv2[:, :, 1], EPS, None, ALU.add).then_inc(s_veps2, 1)
                            dve.tensor_copy(mean2[:, ds((b - 1) * NT, NT)], mv2[:, :, 0]).then_inc(s_mean2, 1)
                        if (g, s) == (2, 1) and exists(b - 1):
                            wait(dve, s_rstd2, b, 1, 0, NB)
                            wait(dve, s_n2ps, b, 1, -1, NB)
                            for t in range(NT):
                                last = dve.tensor_scalar(xn2[:, t, :], x_res[:, (b - 1) * NT + t, :],
                                                         mv2[:, t, 0:1],
                                                         rstd2[:, ds((b - 1) * NT + t, 1)], ALU.subtract, ALU.mult)
                            last.then_inc(s_xn2, 1)
                        if (g, s) == (3, 3) and exists(b - 1):
                            wait(dve, s_lgps, b, 1, 0, NB)
                            dve.tensor_copy(logits[:, ds((b - 1) * NT, NT), :],
                                            ps_m[0][:, 0:32 * NT].rearrange("p (t e) -> p t e", e=32)).then_inc(s_lg, 1)
                        if s == 3 and exists(ba):
                            wait(dve, s_max, ba, UNIT, UNITS * (ga + 1), UNITS * STEPS)
                            wait(dve, s_mps, ba, STEP4, ga - 1, STEPS)
                            pad = max_pad[:, ga % 2].rearrange("p t (h c) -> p t h c", c=SLOT)
                            dve.tensor_copy(pad[:, :, :, MAXROW_HI], neg_max[:, ga % 2]).then_inc(s_mhi, 1)
                            wait(dve, s_mhi, ba, STEP4, ga + 1, STEPS)
                            dve.tensor_tensor(pad[:, :, :, MAXROW_LO], neg_max[:, ga % 2],
                                              pad[:, :, :, MAXROW_HI].bitcast(F32), ALU.subtract).then_inc(s_mlo, 1)

            dve.memset(zeros[:], 0.0).then_inc(s_zero, 1)
            dve.memset(k_z[:].bitcast(F32), 0.0).then_inc(s_set, 1)
            dve.memset(v_pk[:], 0.0).then_inc(s_set, 1)
            dve.memset(max_pad[:].bitcast(F32), 0.0).then_inc(s_set, 1)
            dve.memset(minus_half[:], -0.5).then_inc(s_set, 1)
            dve.wait_ge(s_set, 4)
            dve.memset(v_pk[:, :, :, ONES_COL:ONES_COL + 1], 1.0).then_inc(s_set, 1)
            for n, (dst, width) in enumerate(((w_q, 512), (w_k, 512), (w_v, 128))):
                flat = [dst[:, i].rearrange("p g c -> p (g c)") if width == 512 else dst[:, i] for i in range(2)]
                dve.wait_ge(s_stage, 16 * (n + 1))
                dve.tensor_copy(flat[0], stage[:, 0:width]).then_inc(s_split, 1)
                dve.wait_ge(s_split, 2 * n + 1)
                dve.tensor_tensor(flat[1], stage[:, 0:width], flat[0].bitcast(F32), ALU.subtract).then_inc(s_split, 1)
            dve.wait_ge(s_w, 16 * 8)
            dve.tensor_copy(ident_r[:], ident[:]).then_inc(s_split, 1)
            dve.tensor_copy(ident_b[:], ident[:]).then_inc(s_split, 1)
            dve.tensor_copy(mask_b[:], mask[:]).then_inc(s_split, 1)
            dve.tensor_tensor(b_qk_lo[:], b_qk[:], lo_rows[:].unsqueeze(2).broadcast_to([P, 2, GROUPS]),
                              ALU.mult).then_inc(s_split, 1)
            dve.wait_ge(s_set, 5)
            body(-1)
            body(0)
            body(1)
            with dve.Fori(2, NB - 1) as b:
                body(b)
            body(NB - 1)
            body(NB)

        @block.gpsimd
        def _(pool):
            def body(b):
                for g in range(GROUPS):
                    for s in range(NT):
                        if exists(b):
                            kb = NT - 1 - s
                            wait_first(pool, s_own_p, s_exp, b, UNIT, UNITS * g + FIRST_UNIT[s + 1], UNITS * STEPS)
                            diag = probs[:, s % 2, :, kb * P:(kb + 1) * P]
                            pool.affine_select(out=diag, in_=diag, compare_op=ALU.is_ge, fill=0.0, base=0,
                                               pattern=[[0, GH], [-1, P]], channel_multiplier=1).then_inc(s_mask, 1)
                        if (g, s) == (0, 0) and exists(b + 1):
                            wait(pool, s_veps1, b, 1, 2, NB)
                            pool.tensor_tensor(rstd1[:], veps1[:], minus_half[:], ALU.pow).then_inc(s_rstd1, 1)
                        if (g, s) == (0, 3) and exists(b + 1):
                            wait(pool, s_xn, b, 1, 2, NB)
                            x_b = x_res[:, ds((b + 1) * NT, NT), :]
                            pool.tensor_tensor(x_b, x_b, b_o[:].unsqueeze(1).broadcast_to([P, NT, D]),
                                               ALU.add).then_inc(s_bo, 1)
                        if (g, s) == (2, 0) and exists(b - 1):
                            wait(pool, s_veps2, b, 1, 0, NB)
                            pool.tensor_tensor(rstd2[:, ds((b - 1) * NT, NT)], veps2[:], minus_half[:],
                                               ALU.pow).then_inc(s_rstd2, 1)

            pool.wait_ge(s_set, 4)
            pool.wait_ge(s_w, 16 * 8)
            body(-1)
            body(0)
            body(1)
            with pool.Fori(2, NB - 1) as b:
                body(b)
            body(NB - 1)
            body(NB)




def routing(nc, mem, dram):
    logits, pos, score, slot_expert = mem["logits"], mem["pos"], mem["score"], mem["slot_expert"]
    w_qf, w_kf, w_vo = mem["w_qf"], mem["w_kf"], mem["w_vo"]
    with ExitStack() as ctx:
        def sb(name, shape, dt=F32):
            return ctx.enter_context(nc.sbuf_tensor(name, shape, dt))

        def sem(name):
            return ctx.enter_context(nc.semaphore(name))

        w_t = sb("w_t", [P, 24, D])
        rf = sb("rf", [P, 8, P])
        w_out1 = sb("w_out1", [P, 8, 2 * D])
        iota_e = sb("iota_e", [P, E0])
        iota_q = sb("iota_q", [P, SLOTS])
        before = sb("before", [P, P])
        before_b = sb("before_b", [P, P], BF16)
        ones_b = sb("ones_b", [P, P], BF16)
        top = sb("top", [P, TILES])
        first = sb("first", [P, TILES])
        wide = [sb(f"wide{i}", [P, TILES * E0]) for i in range(3)]
        chosen = sb("chosen", [P, TILES, E0], BF16)
        slots_f = sb("slots_f", [P, E0])
        slots_i = sb("slots_i", [P, E0], I32)
        slots_end = sb("slots_end", [P, E0])
        base = sb("base", [P, E0])
        ones_e = sb("ones_e", [P, E0])
        pos_f = sb("pos_f", [P, TILES])
        passed = sb("passed", [P, SLOTS])
        ps = ctx.enter_context(nc.psum_tensor("ps_r", [P, 8, 512], F32))

        s_wt, s_const = sem("s_wt"), sem("s_const")
        s_d = sem("s_d")
        s_f = sem("s_f")
        s_fa, s_fd = sem("s_fa"), sem("s_fd")
        s_chosen, s_rank, s_tot = sem("s_chosen"), sem("s_rank"), sem("s_tot")
        s_top, s_score = sem("s_top"), sem("s_score")
        block = ctx.enter_context(nc.Block())

        @block.sync
        def _(sp):
            for dst, name in ((iota_e[:], "iota_e"), (iota_q[:], "iota_q"), (before[:], "before")):
                sp.dma_start(dst, dram[name]).then_inc(s_const, 16)
            for dst, name in ((w_t[:], "w_qkv1_t"), (rf[:], "rf1"), (w_out1[:], "w_out1")):
                sp.dma_start(dst, dram[name]).then_inc(s_wt, 16)

        @block.tensor
        def _(pe):
            pe.wait_ge(s_wt, 48)
            for bank in range(8):
                for c in range(4 if bank < 4 else 2):
                    if bank < 4:
                        pair = (bank % 2) * 4 + c
                        last = pe.matmul(ps[:, bank, P * c:P * (c + 1)], w_t[:, (bank // 2) * 8 + pair, :],
                                         rf[:, pair, :], start=True, stop=True)
                    else:
                        pair = (bank - 4) * 2 + c
                        last = pe.matmul(ps[:, bank, 2 * P * c:2 * P * (c + 1)], w_t[:, 16 + pair, :],
                                         w_out1[:, pair, :], start=True, stop=True)
                last.then_inc(s_f, 1)
            pe.wait_ge(s_fa, 8)
            pe.wait_ge(s_fd, 4)
            pe.wait_ge(s_chosen, 1)
            flat = chosen[:].rearrange("p t e -> p (t e)")
            for i in range(4):
                last = pe.matmul(ps[:, 4 + i, :], ones_b[:], flat[:, 512 * i:512 * (i + 1)], start=True, stop=True)
            last.then_inc(s_rank, 1)
            for i in range(4):
                last = pe.matmul(ps[:, i, :], before_b[:], flat[:, 512 * i:512 * (i + 1)], start=True, stop=True)
            last.then_inc(s_rank, 1)

        @block.scalar
        def _(act):
            act.wait_ge(s_top, 1)
            act.activation(score[:], top[:], ACT.Sigmoid).then_inc(s_score, 1)
            for bank in range(8):
                act.wait_ge(s_f, bank + 1)
                if bank < 4:
                    dst = (w_qf, w_kf)[bank // 2][:, 0, (bank % 2) * 512:(bank % 2) * 512 + 512]
                else:
                    dst = w_vo[:, 4 * (bank - 4):4 * (bank - 3), :].rearrange("p h d -> p (h d)")
                act.copy(dst, ps[:, bank, :]).then_inc(s_fa, 1)
            act.wait_ge(s_rank, 1)
            act.copy(wide[0][:].rearrange("p (e t) -> p t e", e=E0),
                     ps[:, 4:8, :].rearrange("p b (t e) -> p (b t) e", e=E0)).then_inc(s_tot, 1)

        @block.vector
        def _(dve):
            done = [0]

            def then(ins):
                done[0] += 1
                ins.then_inc(s_d, 1)
                dve.wait_ge(s_d, done[0])

            tile_e = [P, TILES, E0]
            by_tile = wide[0][:].rearrange("p (t e) -> p t e", e=E0)
            dve.wait_ge(s_const, 48)
            dve.tensor_reduce(top[:], logits[:], AX.X, ALU.max).then_inc(s_top, 1)
            dve.wait_ge(s_top, 1)
            then(dve.tensor_tensor(by_tile, logits[:], top[:].unsqueeze(2).broadcast_to(tile_e), ALU.is_equal))
            then(dve.scalar_tensor_tensor(by_tile, by_tile, -64.0, iota_e[:].unsqueeze(1).broadcast_to(tile_e),
                                          ALU.mult, ALU.add))
            then(dve.tensor_reduce(first[:], by_tile, AX.X, ALU.min))
            then(dve.tensor_scalar(first[:], first[:], 64.0, None, ALU.add))
            then(dve.memset(ones_b[:], 1.0))
            then(dve.tensor_copy(before_b[:], before[:]))
            dve.tensor_tensor(chosen[:], iota_e[:].unsqueeze(1).broadcast_to(tile_e),
                              first[:].unsqueeze(2).broadcast_to(tile_e), ALU.is_equal).then_inc(s_chosen, 1)
            for bank in range(4):
                dst = (w_qf, w_kf)[bank // 2][:, :, (bank % 2) * 512:(bank % 2) * 512 + 512]
                dve.wait_ge(s_fa, bank + 1)
                dve.tensor_tensor(dst[:, 1], ps[:, bank, :], dst[:, 0].bitcast(F32), ALU.subtract).then_inc(s_fd, 1)
            keep = wide[1][:].rearrange("p (e t) -> p e t", e=E0)
            then(dve.memset(ones_e[:], 1.0))
            then(dve.memset(keep, 1.0))
            then(dve.memset(keep[:, :, 0:1], 0.0))
            dve.wait_ge(s_tot, 1)
            then(dve.tensor_tensor_scan(wide[2][:], wide[1][:], wide[0][:], 0.0, ALU.mult, ALU.add))
            upto = wide[2][:].rearrange("p (e t) -> p e t", e=E0)
            then(dve.tensor_scalar(slots_f[:], upto[:, :, TILES - 1], float(P - 1), None, ALU.add))
            then(dve.tensor_copy(slots_i[:], slots_f[:]))
            then(dve.tensor_scalar(slots_i[:], slots_i[:], 7, None, ALU.arith_shift_right))
            then(dve.tensor_copy(slots_f[:], slots_i[:]))
            then(dve.tensor_tensor_scan(slots_end[:], ones_e[:], slots_f[:], 0.0, ALU.mult, ALU.add))
            then(dve.tensor_tensor(base[:], slots_end[:], slots_f[:], ALU.subtract))
            then(dve.tensor_scalar(base[:], base[:], float(P), None, ALU.mult))
            then(dve.tensor_tensor(wide[2][:], wide[2][:], wide[0][:], ALU.subtract))
            then(dve.tensor_tensor(upto, upto, base[:].unsqueeze(2).broadcast_to([P, E0, TILES]), ALU.add))
            dve.wait_ge(s_rank, 2)
            then(dve.tensor_tensor(by_tile, ps[:, 0:4, :].rearrange("p b (t e) -> p (b t) e", e=E0),
                                   wide[2][:].rearrange("p (e t) -> p t e", e=E0), ALU.add))
            then(dve.tensor_tensor(by_tile, by_tile, chosen[:], ALU.mult))
            then(dve.tensor_reduce(pos_f[:], by_tile, AX.X, ALU.add))
            then(dve.tensor_copy(pos[:], pos_f[:]))
            passes = wide[1][:].rearrange("p (a e) -> p a e", e=E0)[:, 0:SLOTS // 2, :]
            for half in range(2):
                q = slice(half * SLOTS // 2, (half + 1) * SLOTS // 2)
                then(dve.tensor_tensor(passes, slots_end[:].unsqueeze(1).broadcast_to([P, SLOTS // 2, E0]),
                                       iota_q[:, q].unsqueeze(2).broadcast_to([P, SLOTS // 2, E0]), ALU.is_le))
                then(dve.tensor_reduce(passed[:, q], passes, AX.X, ALU.add))
            then(dve.tensor_scalar(passed[:], passed[:], float(E0 - 1), None, ALU.min))
            then(dve.tensor_copy(slot_expert[:], passed[:]))


def layer0_experts(nc, mem, dram, x_sorted, y_sorted):
    x_res, mean2, rstd2, pos, score = mem["x_res"], mem["mean2"], mem["rstd2"], mem["pos"], mem["score"]
    ident, slot_expert = mem["ident"], mem["slot_expert"]
    with ExitStack() as ctx:
        def sb(name, shape, dt=F32):
            return ctx.enter_context(nc.sbuf_tensor(name, shape, dt))

        def pb(name, shape, dt=F32):
            return ctx.enter_context(nc.psum_tensor(name, shape, dt))

        def sem(name):
            return ctx.enter_context(nc.semaphore(name))

        w_gu = sb("w_gu", [P, E0, 2 * MID0])
        w_dn = sb("w_dn", [P, E0, 2, D])
        stage = sb("stage_s", [P, 512])
        w_sh = sb("w_sh", [P, 2, 2 * MID0], F32R)
        w_sd = sb("w_sd", [P, 2, D])

        xn2 = sb("xn2_s", [P, NT, D])
        x_go = sb("x_go", [P, 2, NT, D])
        pos_go = sb("pos_go", [P, 2, NT], I32)
        xt_hi = sb("xt_hi_s", [P, SEQ], F32R)
        xt_lo = sb("xt_lo_s", [P, SEQ], F32R)
        sg_s = sb("sg_s", [P, 2, SEQ])
        h_s = sb("h_s", [P, 2, 2, SEQ])

        x_in = sb("x_in", [P, 2, 4, D])
        y_go = sb("y_go", [P, 2, 4, D])
        x_t = sb("x_t", [P, 2, P])
        sg = sb("sg", [P, 2, MID0])
        h = sb("h", [P, 2, MID0])
        h_t = sb("h_t", [P, 2, MID0])

        s_w = sem("s_w2")
        s_split = sem("s_split2")
        s_wgu, s_wdn = sem("s_wgu"), sem("s_wdn")
        s_xn, s_xgo, s_pgo = sem("s_xn_s"), sem("s_xgo"), sem("s_pgo")
        s_tab = sem("s_tab_s")
        s_sent = [sem("s_sent0"), sem("s_sent1")]
        s_t, s_xh, s_xl = sem("s_t_s"), sem("s_xh_s"), sem("s_xl_s")
        s_gu, s_silu, s_h, s_dn, s_res = sem("s_gu_s"), sem("s_silu_s"), sem("s_h_s"), sem("s_dn_s"), sem("s_res")
        e_in = [sem("e_in0"), sem("e_in1")]
        e_out = [sem("e_out0"), sem("e_out1")]
        e_t, e_xt, e_gu, e_silu, e_h = sem("e_t"), sem("e_xt"), sem("e_gu"), sem("e_silu"), sem("e_h")
        e_hps, e_ht, e_dn, e_y = sem("e_hps"), sem("e_ht"), sem("e_dn"), sem("e_y")
        e_own, e_own_p = sem("e_own"), sem("e_own_p")
        N8 = SLOTS // 8

        ps = [pb(f"ps_e{i}", [P, 512]) for i in range(8)]
        block = ctx.enter_context(nc.Block())

        def live(b, total=NB):
            return not isinstance(b, int) or 0 <= b < total

        def over_batches(eng, body):
            body(-1, 1)
            body(0, 0)
            body(0, 1)
            with eng.Fori(1, NB // 2 - 1) as i:
                body(i, 0)
                body(i, 1)
            body(NB // 2 - 1, 0)
            body(NB // 2 - 1, 1)
            body(NB // 2, 0)

        def over_slots(eng, body):
            for c in (6, 7):
                body(-1, c)
            for c in range(8):
                body(0, c)
            with eng.Fori(1, N8 - 1) as i:
                for c in range(8):
                    body(i, c)
            for c in range(8):
                body(N8 - 1, c)
            for c in (0, 1):
                body(N8, c)

        def slot_live(i, c):
            return not isinstance(i, int) or 0 <= 8 * i + c < SLOTS

        @block.sync
        def _(sp):
            sp.dma_start(stage[:], dram["w_shared0"]).then_inc(s_w, 16)
            sp.dma_start(w_sd[:], dram["w_shared_dn0"]).then_inc(s_w, 16)
            for i in range(4):
                e = slice(8 * i, 8 * i + 8)
                sp.dma_start(w_gu[:, e, 0:MID0], dram["w_gate0"][:, e, :]).then_inc(s_wgu, 16)
                sp.dma_start(w_gu[:, e, MID0:2 * MID0], dram["w_up0"][:, e, :]).then_inc(s_wgu, 16)
                sp.dma_start(w_dn[:, e], dram["w_down0"][:, e]).then_inc(s_wdn, 16)

            x_dram = x_sorted.rearrange("(q t p) d -> q p t d", p=P, t=4)
            y_dram = y_sorted.rearrange("(q t p) d -> q p t d", p=P, t=4)
            for par in range(2):
                sp.wait_ge(s_sent[par], 16 * NT * NB // 2)

            def load(i, c):
                q, half = (2 * i + c // 4), c // 4
                wait(sp, e_t, i, 8, 4 * half - 4, SLOTS)
                sp.dma_start(x_in[:, half], x_dram[q]).then_inc(e_in[half], 16)

            def store(i, half):
                wait(sp, e_y, i, 8, 4 * half + 4, SLOTS)
                sp.dma_start(y_dram[2 * i + half], y_go[:, half]).then_inc(e_out[half], 16)

            load(0, 0)
            load(0, 4)
            load(1, 0)
            store(0, 0)
            load(1, 4)
            store(0, 1)
            with sp.Fori(1, N8 - 1) as i:
                load(i + 1, 0)
                store(i, 0)
                load(i + 1, 4)
                store(i, 1)
            store(N8 - 1, 0)
            store(N8 - 1, 1)
            for half in range(2):
                sp.wait_ge(e_out[half], 16 * N8)

        @block.tensor
        def _(pe):
            def shared(i, par):
                b = 2 * i + par
                if live(b):
                    wait(pe, s_xl, b, 1, 1, NB)
                    for m in range(4):
                        if m < 2:
                            wait(pe, s_silu, b, 2, m - 1, 2 * NB)
                        else:
                            wait(pe, s_h, b, 2, m - 3, 2 * NB)
                        for n, (a, c) in enumerate(((0, xt_hi), (1, xt_hi), (0, xt_lo))):
                            last = pe.matmul(ps[m][:], w_sh[:, a, P * m:P * (m + 1)], c[:], start=(n == 0), stop=(n == 2))
                        last.then_inc(s_gu, 1)
                if live(b + 1):
                    wait(pe, s_xn, b, 1, 2, NB)
                    wait(pe, s_xl, b, 1, 1, NB)
                    for t in range(NT):
                        last = pe.transpose(ps[4][:, P * t:P * (t + 1)], xn2[:, t, :], ident[:])
                    last.then_inc(s_t, 1)
                if live(b - 1):
                    wait(pe, s_h, b, 2, 0, 2 * NB)
                    wait(pe, s_res, b, 1, -1, NB)
                    for t in range(NT):
                        for k in range(2):
                            last = pe.matmul(ps[5][:, P * t:P * (t + 1)], h_s[:, 1 - par, k, P * t:P * (t + 1)],
                                             w_sd[:, k, :], start=(k == 0), stop=(k == 1))
                    last.then_inc(s_dn, 1)

            pe.wait_ge(s_split, 2)
            pe.wait_ge(s_w, 32)
            over_batches(pe, shared)

            expert = {}

            def routed(i, c):
                if c == 0:
                    expert.clear()
                for tile in (c - 2, c + 1):
                    if slot_live(i, tile) and tile not in expert:
                        expert[tile] = pe.value_load(slot_expert[0:1, ds(8 * i + tile, 1)], min_val=0,
                                                        max_val=E0 - 1)
                if slot_live(i, c + 2):
                    half, t = (c + 2) // 4 % 2, (c + 2) % 4
                    wait(pe, e_in[half], i, 16, 16 * ((c + 2) // 8 + 1), 16 * N8)
                    wait(pe, e_xt, i, 8, c + 1, SLOTS)
                    pe.transpose(ps[c % 2][:, 0:P], x_in[:, half, t, :], ident[:]).then_inc(e_t, 1)
                if slot_live(i, c - 2):
                    wait(pe, e_ht, i, 8, c - 1, SLOTS)
                    wait(pe, e_y, i, 8, c - 3, SLOTS)
                    for k in range(2):
                        last = pe.matmul(ps[6 + c % 2][:, 0:P], h_t[:, c % 2, P * k:P * (k + 1)],
                                         w_dn[:, ds(expert[c - 2], 1), k, :], start=(k == 0), stop=(k == 1))
                    last.then_inc(e_dn, 1)
                if slot_live(i, c - 1):
                    wait(pe, e_h, i, 8, c, SLOTS)
                    wait(pe, e_ht, i, 8, c - 2, SLOTS)
                    for k in range(2):
                        last = pe.transpose(ps[4 + (c - 1) % 2][:, P * k:P * (k + 1)],
                                            h[:, (c - 1) % 2, P * k:P * (k + 1)], ident[:])
                    last.then_inc(e_hps, 1)
                if slot_live(i, c + 1):
                    wait(pe, e_h, i, 8, c, SLOTS)
                    wait(pe, e_xt, i, 8, c + 2, SLOTS)
                    pe.matmul(ps[2 + (c + 1) % 2][:], x_t[:, (c + 1) % 2, :], w_gu[:, ds(expert[c + 1], 1), :],
                              start=True, stop=True).then_inc(e_gu, 1)

            pe.wait_ge(s_wgu, 16 * 8)
            pe.wait_ge(s_wdn, 16 * 4)
            pe.wait_ge(s_res, NB)
            pe.wait_ge(s_silu, 2 * NB)
            pe.wait_ge(s_h, 2 * NB)
            over_slots(pe, routed)

        @block.scalar
        def _(act):
            def shared(i, par):
                b = 2 * i + par
                if live(b):
                    for m in range(2):
                        wait(act, s_gu, b, 4, m + 1, 4 * NB)
                        wait(act, s_h, b, 2, m - 1, 2 * NB)
                        act.activation(sg_s[:, m, :], ps[m][:], ACT.Silu).then_inc(s_silu, 1)
                if live(b + 1):
                    wait(act, s_t, b, 1, 2, NB)
                    act.copy(xt_hi[:], ps[4][:]).then_inc(s_xh, 1)

            def routed(i, c):
                if slot_live(i, c - 1):
                    wait(act, e_hps, i, 8, c, SLOTS)
                    wait(act, e_dn, i, 8, c - 2, SLOTS)
                    act.copy(h_t[:, (c - 1) % 2, :], ps[4 + (c - 1) % 2][:, 0:MID0]).then_inc(e_ht, 1)
                if slot_live(i, c + 1):
                    wait(act, e_gu, i, 8, c + 2, SLOTS)
                    wait(act, e_h, i, 8, c, SLOTS)
                    act.activation(sg[:, (c + 1) % 2, :], ps[2 + (c + 1) % 2][:, 0:MID0],
                                   ACT.Silu).then_inc(e_silu, 1)

            act.wait_ge(s_w, 32)
            act.activation(sg[:, 0, 0:1], stage[:, 0:1], ACT.Silu).then_inc(s_tab, 1)
            act.wait_ge(s_tab, 1)
            over_batches(act, shared)
            over_slots(act, routed)

        @block.vector
        def _(dve):
            def prepare(i, par):
                b = 2 * i + par
                if isinstance(b, int) and b >= NB:
                    return
                wait(dve, s_t, b, 1, 0, NB)
                wait(dve, s_xgo, b, 1, 0, NB)
                for t in range(NT):
                    last = dve.tensor_scalar(xn2[:, t, :], x_res[:, b * NT + t, :], mean2[:, ds(b * NT + t, 1)],
                                             rstd2[:, ds(b * NT + t, 1)], ALU.subtract, ALU.mult)
                last.then_inc(s_xn, 1)
                wait(dve, s_xn, b, 1, 1, NB)
                wait(dve, s_sent[par], i, 16 * NT, 0, 16 * NT * NB // 2)
                dve.tensor_copy(pos_go[:, par, :], pos[:, ds(b * NT, NT)]).then_inc(s_pgo, 1)
                for t in range(NT):
                    last = dve.tensor_scalar(x_go[:, par, t, :], xn2[:, t, :], score[:, ds(b * NT + t, 1)], None,
                                             ALU.mult)
                last.then_inc(s_xgo, 1)

            def shared(i, par):
                b = 2 * i + par
                if live(b):
                    for m in range(2):
                        wait(dve, s_silu, b, 2, m + 1, 2 * NB)
                        wait(dve, s_gu, b, 4, m + 3, 4 * NB)
                        dve.tensor_tensor(h_s[:, par, m, :], ps[2 + m][:], sg_s[:, m, :], ALU.mult).then_inc(s_h, 1)
                if live(b + 1):
                    wait(dve, s_xh, b, 1, 2, NB)
                    dve.tensor_tensor(xt_lo[:], ps[4][:], xt_hi[:].bitcast(F32), ALU.subtract).then_inc(s_xl, 1)
                if live(b - 1):
                    wait(dve, s_dn, b, 1, 0, NB)
                    x_b = x_res[:, ds((b - 1) * NT, NT), :]
                    dve.tensor_tensor(x_b, ps[5][:].rearrange("p (t d) -> p t d", t=NT), x_b,
                                      ALU.add).then_inc(s_res, 1)
                if live(b + 2):
                    prepare(i + 1, par)

            def routed(i, c):
                if slot_live(i, c + 2):
                    wait(dve, e_t, i, 8, c + 3, SLOTS)
                    wait(dve, e_gu, i, 8, c + 1, SLOTS)
                    dve.tensor_copy(x_t[:, c % 2, :], ps[c % 2][:, 0:P]).then_inc(e_xt, 1)
                if slot_live(i, c - 2):
                    wait(dve, e_dn, i, 8, c - 1, SLOTS)
                    half = (c - 2) // 4 % 2
                    if (c - 2) % 4 == 0:
                        wait(dve, e_out[half], i, 16, 16 * ((c - 2) // 8), 16 * N8)
                    dve.tensor_copy(y_go[:, half, (c - 2) % 4, :], ps[6 + c % 2][:, 0:P]).then_inc(e_y, 1)
                if slot_live(i, c + 1):
                    wait(dve, e_silu, i, 8, c + 2, SLOTS)
                    wait(dve, e_hps, i, 8, c, SLOTS)
                    dve.tensor_tensor(h[:, (c + 1) % 2, :], ps[2 + (c + 1) % 2][:, MID0:2 * MID0],
                                      sg[:, (c + 1) % 2, :], ALU.mult).then_inc(e_h, 1)

            dve.wait_ge(s_w, 32)
            dve.tensor_copy(w_sh[:, 0, :], stage[:]).then_inc(s_split, 1)
            dve.wait_ge(s_split, 1)
            dve.tensor_tensor(w_sh[:, 1, :], stage[:], w_sh[:, 0, :].bitcast(F32), ALU.subtract).then_inc(s_split, 1)
            prepare(0, 0)
            over_batches(dve, shared)
            over_slots(dve, routed)

        @block.gpsimd
        def _(pool):
            def send(i, par):
                b = 2 * i + par
                if not live(b):
                    return
                wait_first(pool, e_own_p, s_xgo, b, 1, 1, NB)
                for t in range(NT):
                    pool.indirect_dma_start(x_sorted[:, :],
                                            bass.IndirectOffsetOnAxis(ap=pos_go[:, par, t:t + 1], axis=0),
                                            x_go[:, par, t, :], None).then_inc(s_sent[par], 16)

            over_batches(pool, send)


MID1, E1, FFN_TILES = 32, 16, 5
PAIRS = H1 // 2
LOG_ROWS = 32
COMB_STEPS = 20
RING = ([("phi_k", n) for n in range(8)] + [("phi_q", n) for n in range(4)] + [("x4t", 0)]
        + [("phi_q", n) for n in range(4, 8)]
        + [("gate", 0), ("up", 0)]
        + [(kind, i) for i in (1, 2) for kind in ("gate", "up", "comb")]
        + [("kvw", n) for n in range(4)]
        + [(kind, i) for i in (3, 4) for kind in ("gate", "up", "comb")]
        + [("inv", n) for n in range(8)] + [("x3t", 0)])
RING_BANKS = 4


def layer1(nc, mem, dram, y_sorted, out):
    x_res, pos, ident, ident_r = mem["x_res"], mem["pos"], mem["ident"], mem["ident_r"]
    w_qf, w_kf, w_vo = mem["w_qf"], mem["w_kf"], mem["w_vo"]
    with ExitStack() as ctx:
        def sb(name, shape, dt=F32):
            return ctx.enter_context(nc.sbuf_tensor(name, shape, dt))

        def sem(name):
            return ctx.enter_context(nc.semaphore(name))

        stage = sb("stage1", [P, 2, FFN_TILES * P])
        spread_stage = sb("spread_stage", [P, PAIRS + FFN_TILES - 1, P])
        w_gate = sb("w_gate1", [P, 2, FFN_TILES * P], F32R)
        w_up = sb("w_up1", [P, 2, FFN_TILES * P], F32R)
        w_down = sb("w_down1", [P, FFN_TILES, D])
        w_rt_stage = sb("w_rt_stage", [P, E1])
        w_rt = sb("w_rt", [P, 2, E1], F32R)
        b_o = sb("b_o1s", [P, D])
        spread = sb("spread", [P, PAIRS, P], F32R)
        spread_e = sb("spread_e", [P, FFN_TILES - 1, P], F32R)
        low = sb("low", [P, 1])
        own_head = sb("own_head", [P, PAIRS, 8])
        iota = sb("iota1", [P, NT, E1])
        iota64 = sb("iota64", [P, NT, E1])
        minus_half = sb("minus_half1", [P, NT])

        pos_y = sb("pos_y", [P, NT], I32)
        y = sb("y", [P, NT, D])
        stat3, stat4 = sb("stat3", [P, NT, 6]), sb("stat4", [P, NT, 6])
        mv3, mv4 = sb("mv3", [P, NT, 2]), sb("mv4", [P, NT, 2])
        veps3, veps4 = sb("veps3", [P, NT]), sb("veps4", [P, NT])
        rstd3, rstd4 = sb("rstd3", [P, NT]), sb("rstd4", [P, NT])
        xn3 = sb("xn3", [P, NT, D + 2])
        x3_hi, x3_lo = sb("x3_hi", [P, SEQ], F32R), sb("x3_lo", [P, SEQ], F32R)
        phi_k = sb("phi_k", [P, NT, H1 * HD1])
        phi_q = sb("phi_q", [P, PAIRS, SEQ])
        g_sb = sb("g_sb", [P, PAIRS, D + 2])
        gt_sb = sb("gt_sb", [P, PAIRS, P])
        kvw = sb("kvw", [P, PAIRS, D])
        ksum = sb("ksum", [P, PAIRS, LOG_ROWS])
        norm = sb("norm", [P, SEQ])
        inv = sb("inv", [P, SEQ])
        inv_half = sb("inv_half", [P, SEQ], F32R)
        inv_pk = sb("inv_pk", [P, SEQ], F32R)
        xn4 = sb("xn4", [P, NT, D])
        x4_hi, x4_lo = sb("x4_hi", [P, SEQ], F32R), sb("x4_lo", [P, SEQ], F32R)
        t_e = [P, NT, E1]
        top = [sb(f"top{i}", [P, NT]) for i in range(2)]
        first = [sb(f"first{i}", [P, NT]) for i in range(2)]
        hot = [sb(f"hot{i}", t_e) for i in range(2)]
        cand, dif, dif2, expo, w12 = (sb(n, t_e) for n in ("cand", "dif", "dif2", "expo", "w12"))
        s12, z, den = sb("s12", [P, NT]), sb("z", [P, NT]), sb("den", [P, NT])
        comb = sb("comb", [P, NT, P], F32R)
        comb_t = sb("comb_t", [P, SEQ], F32R)
        silu = sb("silu", [P, 2, SEQ])
        h = sb("h1", [P, FFN_TILES, SEQ])

        ps = ctx.enter_context(nc.psum_tensor("ps1", [P, 8, 512], F32))
        G_BANKS, PER_BANK = 3, 3
        OUT, DOWN, NORM, ROUTE = 4, 5, 6, 7

        s_w, s_split, s_set = sem("c_w"), sem("c_split"), sem("c_set")
        s_own_d, s_own_p = sem("c_own_d"), sem("c_own_p")
        s_posy, s_y, s_x3, s_bn3, s_ve3, s_rstd3, s_xn3, s_bo = map(
            sem, ("c_posy", "c_y", "c_x3", "c_bn3", "c_ve3", "c_rstd3", "c_xn3", "c_bo"))
        s_x3t, s_x3h, s_x3l = sem("c_x3t"), sem("c_x3h"), sem("c_x3l")
        s_kps, s_k, s_qps, s_q = sem("c_kps"), sem("c_k"), sem("c_qps"), sem("c_q")
        s_g, s_gsb, s_gt, s_gtsb = sem("c_g"), sem("c_gsb"), sem("c_gt"), sem("c_gtsb")
        s_kv, s_kva = sem("c_kv"), sem("c_kva")
        s_ksum, s_n, s_norm, s_inv, s_ihalf, s_ipk = map(
            sem, ("c_ksum", "c_n", "c_norm", "c_inv", "c_ihalf", "c_ipk"))
        s_bc, s_qn, s_ao, s_x4 = sem("c_bc"), sem("c_qn"), sem("c_ao"), sem("c_x4")
        s_bn4, s_ve4, s_rstd4, s_xn4 = sem("c_bn4"), sem("c_ve4"), sem("c_rstd4"), sem("c_xn4")
        s_x4t, s_x4h, s_x4l = sem("c_x4t"), sem("c_x4h"), sem("c_x4l")
        s_lg, s_dif, s_expo, s_comb, s_cps, s_ct = map(
            sem, ("c_lg", "c_dif", "c_expo", "c_comb", "c_cps", "c_ct"))
        s_gate, s_up, s_cb = sem("c_gate"), sem("c_up"), sem("c_cb")
        s_silu, s_h, s_hc = sem("c_silu"), sem("c_h"), sem("c_hc")
        s_dn, s_xo, s_out = sem("c_dn"), sem("c_xo"), sem("c_out")

        READERS = {"phi_k": ((s_k,), 8, 0, 0), "phi_q": ((s_q,), 8, 0, 0), "kvw": ((s_kva,), 8, 0, 0),
                   "inv": ((s_qn,), 8, 0, 0), "x3t": ((s_x3l,), 1, 0, -1), "x4t": ((s_x4l,), 1, 0, 1),
                   "gate": ((s_silu,), FFN_TILES, 0, 1), "up": ((s_h,), FFN_TILES, 0, 1),
                   "comb": ((s_hc,), FFN_TILES - 1, 1, 1)}
        W_ALL = 16 * 11

        def ring_bank(kind, n):
            return RING.index((kind, n)) % RING_BANKS

        def take_bank(pe, b, kind, n):
            at = RING.index((kind, n)) - RING_BANKS
            while True:
                turn, (kind0, n0) = b + at // len(RING), RING[at % len(RING)]
                sems, per, low_n, lag = READERS[kind0]
                if isinstance(b, int) and turn < -1:
                    break
                if exists(turn - lag):
                    for s in sems:
                        reads = 2 if kind0 == "kvw" else 1
                        wait(pe, s, turn - lag, per, reads * (n0 - low_n + 1), per * NB)
                    break
                at -= RING_BANKS
            return ps[:, ring_bank(kind, n), :]

        def turns(eng, body):
            body(-1)
            body(0)
            body(1)
            with eng.Fori(2, NB - 1) as b:
                body(b)
            body(NB - 1)
            body(NB)

        block = ctx.enter_context(nc.Block())

        @block.sync
        def _(sp):
            for dst, name in ((stage[:, 0], "w_gate1"), (stage[:, 1], "w_up1"), (w_rt_stage[:], "router1"),
                              (w_down[:], "w_down1"), (b_o[:], "b_o1"), (spread_stage[:, 0:PAIRS], "spread"),
                              (spread_stage[:, PAIRS:], "spread_e"), (low[:], "low"), (iota[:], "iota1"),
                              (own_head[:], "own_head"),
                              (iota64[:], "iota64")):
                sp.dma_start(dst, dram[name]).then_inc(s_w, 16)
            out_dram = out.rearrange("(b t p) d -> b p t d", p=P, t=NT)

            def body(b):
                f = b - 1
                if exists(f):
                    wait(sp, s_xo, f, 1, 1, NB)
                    sp.dma_start(out_dram[f], x_res[:, ds(f * NT, NT), :]).then_inc(s_out, 16)

            turns(sp, body)
            sp.wait_ge(s_out, 16 * NB)

        @block.tensor
        def _(pe):
            def three_passes(to, a, c):
                pe.matmul(to, a[0], c[0], start=True, stop=False)
                pe.matmul(to, a[1], c[0], start=False, stop=False)
                return pe.matmul(to, a[0], c[1], start=False, stop=True)

            def tile(t):
                return slice(t * P, (t + 1) * P)

            def expert_tile(b, i):
                f = b - 1
                if not exists(f):
                    return
                cols = slice(i * P, (i + 1) * P)
                for kind, w, done in (("gate", w_gate, s_gate), ("up", w_up, s_up)):
                    bank = take_bank(pe, b, kind, i)
                    three_passes(bank, (w[:, 0, cols], w[:, 1, cols]), (x4_hi[:], x4_lo[:])).then_inc(done, 1)
                if i:
                    bank = take_bank(pe, b, "comb", i)
                    wait(pe, s_ct, f, 1, 1, NB)
                    pe.matmul(bank, spread_e[:, i - 1, :], comb_t[:], start=True, stop=True).then_inc(s_cb, 1)

            def phi_q_tile(b, j):
                bank = take_bank(pe, b, "phi_q", j)
                cols = slice(j * P, (j + 1) * P)
                three_passes(bank, (w_qf[:, 0, cols], w_qf[:, 1, cols]), (x3_hi[:], x3_lo[:])).then_inc(s_qps, 1)

            def body(b):
                f = b - 1
                if exists(b):
                    wait(pe, s_x3l, b, 1, 1, NB)
                    for n in range(8):
                        bank = take_bank(pe, b, "phi_k", n)
                        t, cols = n // 2, slice(n % 2 * 512, (n % 2 + 1) * 512)
                        three_passes(bank, (x3_hi[:, tile(t)], x3_lo[:, tile(t)]),
                                     (w_kf[:, 0, cols], w_kf[:, 1, cols])).then_inc(s_kps, 1)
                if exists(b):
                    for j in range(4):
                        phi_q_tile(b, j)
                if exists(f):
                    bank = take_bank(pe, b, "x4t", 0)
                    wait(pe, s_xn4, f, 1, 1, NB)
                    for t in range(NT):
                        last = pe.transpose(bank[:, tile(t)], xn4[:, t, :], ident[:])
                    last.then_inc(s_x4t, 1)
                if exists(b):
                    for j in range(4, 8):
                        phi_q_tile(b, j)
                if exists(f):
                    wait(pe, s_x4l, f, 1, 1, NB)
                    wait(pe, s_ct, f, 1, 0, NB)
                    for t in range(NT):
                        last = three_passes(ps[:, ROUTE, E1 * t:E1 * (t + 1)], (x4_hi[:, tile(t)], x4_lo[:, tile(t)]),
                                            (w_rt[:, 0], w_rt[:, 1]))
                    last.then_inc(s_lg, 1)
                if exists(b):
                    wait(pe, s_k, b, 8, 8, 8 * NB)
                    for i in range(G_BANKS):
                        if i == 0:
                            wait(pe, s_x4, b, 1, 0, NB)
                        elif i == 1:
                            wait(pe, s_xo, b, 1, -1, NB)
                        else:
                            wait(pe, s_norm, b, 1, 0, NB)
                        for j in range(i * PER_BANK, min((i + 1) * PER_BANK, PAIRS)):
                            c = (j - i * PER_BANK) * (D + 2)
                            for t in range(NT):
                                last = pe.matmul(ps[:, OUT + i, c:c + D + 2], phi_k[:, t, tile(j)], xn3[:, t, :],
                                                 start=(t == 0), stop=(t == NT - 1))
                        last.then_inc(s_g, 1)
                if exists(f):
                    wait(pe, s_comb, f, COMB_STEPS, COMB_STEPS, COMB_STEPS * NB)
                    for t in range(NT):
                        last = pe.matmul(ps[:, ROUTE, tile(t)], comb[:, t, :], ident_r[:], start=True, stop=True)
                    last.then_inc(s_cps, 1)
                expert_tile(b, 0)
                if exists(b):
                    wait(pe, s_gsb, b, G_BANKS, G_BANKS, G_BANKS * NB)
                    for i in range(2):
                        for j in range(4):
                            last = pe.transpose(ps[:, OUT + i, tile(j)], g_sb[:, 4 * i + j, 0:D], ident[:])
                        last.then_inc(s_gt, 1)
                expert_tile(b, 1)
                expert_tile(b, 2)
                if exists(b):
                    wait(pe, s_ksum, b, 1, 1, NB)
                    wait(pe, s_q, b, 8, 8, 8 * NB)
                    for j in range(PAIRS):
                        rows = slice(LOG_ROWS * (j % 4), LOG_ROWS * (j % 4 + 1))
                        last = pe.matmul(ps[rows, NORM, :], ksum[:, j, :], phi_q[:, j, :], start=(j < 4),
                                         stop=(j >= 4), skip_group_check=True)
                    last.then_inc(s_n, 1)
                    wait(pe, s_gtsb, b, 2, 2, 2 * NB)
                    for n in range(4):
                        bank = take_bank(pe, b, "kvw", n)
                        for c in range(2):
                            j = 2 * n + c
                            last = pe.matmul(bank[:, 2 * D * c:2 * D * (c + 1)], gt_sb[:, j, :],
                                             w_vo[:, 2 * j:2 * j + 2, :], start=True, stop=True)
                        last.then_inc(s_kv, 1)
                expert_tile(b, 3)
                expert_tile(b, 4)
                for part in range(2):
                    if exists(b):
                        if part == 0:
                            wait(pe, s_ipk, b, 1, 1, NB)
                        for j in range(4 * part, 4 * part + 4):
                            bank = take_bank(pe, b, "inv", j)
                            pe.matmul(bank, spread[:, j, :], inv_pk[:], start=True, stop=True).then_inc(s_bc, 1)
                    if exists(f):
                        if part == 0:
                            wait(pe, s_h, f, FFN_TILES, FFN_TILES, FFN_TILES * NB)
                            wait(pe, s_hc, f, FFN_TILES - 1, FFN_TILES - 1, (FFN_TILES - 1) * NB)
                        for t in (2 * part, 2 * part + 1):
                            for i in range(FFN_TILES):
                                last = pe.matmul(ps[:, DOWN, tile(t)], h[:, i, tile(t)], w_down[:, i, :],
                                                 start=(i == 0), stop=(i == FFN_TILES - 1))
                        if part == 1:
                            last.then_inc(s_dn, 1)
                if exists(b + 1):
                    bank = take_bank(pe, b, "x3t", 0)
                    wait(pe, s_xn3, b, 1, 2, NB)
                    for t in range(NT):
                        last = pe.transpose(bank[:, tile(t)], xn3[:, t, 0:D], ident[:])
                    last.then_inc(s_x3t, 1)
                if exists(b):
                    wait(pe, s_kva, b, 8, 8, 8 * NB)
                    for j in range(PAIRS):
                        wait(pe, s_qn, b, 8, j + 1, 8 * NB)
                        for t in range(NT):
                            last = pe.matmul(ps[:, OUT, tile(t)], phi_q[:, j, tile(t)], kvw[:, j, :],
                                             start=(j == 0 and t == 0), stop=(j == PAIRS - 1), skip_group_check=True)
                    last.then_inc(s_ao, 1)

            pe.wait_ge(s_w, W_ALL)
            pe.wait_ge(s_split, 8)
            turns(pe, body)

        @block.scalar
        def _(act):
            def expert_tile(b, i):
                f = b - 1
                if exists(f):
                    wait(act, s_gate, f, FFN_TILES, i + 1, FFN_TILES * NB)
                    wait(act, s_h, f, FFN_TILES, i - 1, FFN_TILES * NB)
                    act.activation(silu[:, i % 2, :], ps[:, ring_bank("gate", i), :], ACT.Silu).then_inc(s_silu, 1)

            def phi_q_tile(b, j):
                wait(act, s_qps, b, 8, j + 1, 8 * NB)
                wait(act, s_ao, b, 1, 0, NB)
                act.activation(phi_q[:, j, :], ps[:, ring_bank("phi_q", j), :], ACT.Relu).then_inc(s_q, 1)

            def body(b):
                f = b - 1
                if exists(b):
                    for n in range(8):
                        wait(act, s_kps, b, 8, n + 1, 8 * NB)
                        wait(act, s_g, b, G_BANKS, 0, G_BANKS * NB)
                        act.activation(phi_k[:, n // 2, n % 2 * 512:(n % 2 + 1) * 512],
                                       ps[:, ring_bank("phi_k", n), :], ACT.Relu).then_inc(s_k, 1)
                if exists(b):
                    for j in range(4):
                        phi_q_tile(b, j)
                if exists(f):
                    wait(act, s_x4t, f, 1, 1, NB)
                    wait(act, s_up, f, FFN_TILES, 0, FFN_TILES * NB)
                    act.copy(x4_hi[:], ps[:, ring_bank("x4t", 0), :]).then_inc(s_x4h, 1)
                if exists(b):
                    for j in range(4, 8):
                        phi_q_tile(b, j)
                if exists(f):
                    wait(act, s_dif, f, 1, 1, NB)
                    wait(act, s_comb, f, COMB_STEPS, 0, COMB_STEPS * NB)
                    act.activation(expo[:], dif[:], ACT.Exp).then_inc(s_expo, 1)
                if exists(b):
                    for i in range(G_BANKS):
                        pairs = min((i + 1) * PER_BANK, PAIRS) - i * PER_BANK
                        wait(act, s_g, b, G_BANKS, i + 1, G_BANKS * NB)
                        wait(act, s_gt, b, 2, 0, 2 * NB)
                        wait(act, s_ksum, b, 1, 0, NB)
                        act.copy(g_sb[:, i * PER_BANK:i * PER_BANK + pairs, :],
                                 ps[:, OUT + i, 0:pairs * (D + 2)].rearrange("p (j c) -> p j c", j=pairs)
                                 ).then_inc(s_gsb, 1)
                if exists(f):
                    wait(act, s_cps, f, 1, 1, NB)
                    wait(act, s_cb, f, FFN_TILES - 1, 0, (FFN_TILES - 1) * NB)
                    act.copy(comb_t[:], ps[:, ROUTE, :]).then_inc(s_ct, 1)
                expert_tile(b, 0)
                if exists(b):
                    for i in range(2):
                        wait(act, s_gt, b, 2, i + 1, 2 * NB)
                        wait(act, s_kv, b, 4, 0, 4 * NB)
                        act.copy(gt_sb[:, 4 * i:4 * i + 4, :],
                                 ps[:, OUT + i, :].rearrange("p (j c) -> p j c", j=4)).then_inc(s_gtsb, 1)
                expert_tile(b, 1)
                expert_tile(b, 2)
                if exists(b):
                    for n in range(4):
                        wait(act, s_kv, b, 4, n + 1, 4 * NB)
                        wait(act, s_ao, b, 1, 0, NB)
                        act.copy(kvw[0:HD1, 2 * n:2 * n + 2, :],
                                 ps[0:HD1, ring_bank("kvw", n), :].rearrange("p (j i d) -> p j i d", j=2, i=2)
                                 [:, :, 0, :]).then_inc(s_kva, 1)
                        act.copy(kvw[HD1:P, 2 * n:2 * n + 2, :],
                                 ps[HD1:P, ring_bank("kvw", n), :].rearrange("p (j i d) -> p j i d", j=2, i=2)
                                 [:, :, 1, :]).then_inc(s_kva, 1)
                    wait(act, s_inv, b, 1, 1, NB)
                    wait(act, s_ipk, b, 1, 0, NB)
                    act.activation(inv_half[:], inv[:], ACT.Identity, scale=low[:, 0:1]).then_inc(s_ihalf, 1)
                expert_tile(b, 3)
                expert_tile(b, 4)
                if exists(b + 1):
                    wait(act, s_x3t, b, 1, 2, NB)
                    if exists(b):
                        wait(act, s_qps, b, 8, 8, 8 * NB)
                    act.copy(x3_hi[:], ps[:, ring_bank("x3t", 0), :]).then_inc(s_x3h, 1)

            act.wait_ge(s_w, W_ALL)
            act.wait_ge(s_set, 4)
            act.activation(norm[:, 0:1], low[:, 0:1], ACT.Silu).then_inc(s_own_d, 1)
            turns(act, body)

        @block.vector
        def _(dve):
            def experts_tile(b, i):
                f = b - 1
                if not exists(f):
                    return
                wait(dve, s_silu, f, FFN_TILES, i + 1, FFN_TILES * NB)
                wait(dve, s_up, f, FFN_TILES, i + 1, FFN_TILES * NB)
                wait(dve, s_dn, f, 1, 0, NB)
                dve.tensor_tensor(h[:, i, :], ps[:, ring_bank("up", i), :], silu[:, i % 2, :],
                                  ALU.mult).then_inc(s_h, 1)
                if i:
                    wait(dve, s_cb, f, FFN_TILES - 1, i, (FFN_TILES - 1) * NB)
                    wait(dve, s_h, f, FFN_TILES, i + 1, FFN_TILES * NB)
                    dve.tensor_tensor(h[:, i, :], ps[:, ring_bank("comb", i), :], h[:, i, :],
                                      ALU.mult).then_inc(s_hc, 1)

            def comb_weights(f):
                done = [0]

                def then(ins):
                    done[0] += 1
                    ins.then_inc(s_comb, 1)
                    wait(dve, s_comb, f, COMB_STEPS, done[0], COMB_STEPS * NB)

                def wide(v):
                    return v[:].unsqueeze(2).broadcast_to(t_e)

                logits = ps[:, ROUTE, 0:NT * E1].rearrange("p (t e) -> p t e", e=E1)
                wait(dve, s_lg, f, 1, 1, NB)
                then(dve.tensor_reduce(top[0][:], logits, AX.X, ALU.max))
                wait(dve, s_expo, f, 1, 0, NB)
                dve.tensor_tensor(dif[:], logits, wide(top[0]), ALU.subtract).then_inc(s_dif, 1)
                then(dve.tensor_tensor(cand[:], logits, wide(top[0]), ALU.is_equal))
                then(dve.scalar_tensor_tensor(cand[:], cand[:], -64.0, iota[:], ALU.mult, ALU.add))
                then(dve.tensor_reduce(first[0][:], cand[:], AX.X, ALU.min))
                then(dve.tensor_tensor(hot[0][:], iota64[:], wide(first[0]), ALU.is_equal))
                wait(dve, s_dif, f, 1, 1, NB)
                then(dve.scalar_tensor_tensor(dif2[:], hot[0][:], -BIG, dif[:], ALU.mult, ALU.add))
                then(dve.tensor_reduce(top[1][:], dif2[:], AX.X, ALU.max))
                then(dve.tensor_tensor(cand[:], dif2[:], wide(top[1]), ALU.is_equal))
                then(dve.scalar_tensor_tensor(cand[:], cand[:], -64.0, iota[:], ALU.mult, ALU.add))
                then(dve.tensor_reduce(first[1][:], cand[:], AX.X, ALU.min))
                then(dve.tensor_tensor(hot[1][:], iota64[:], wide(first[1]), ALU.is_equal))
                then(dve.tensor_tensor(hot[1][:], hot[0][:], hot[1][:], ALU.add))
                wait(dve, s_expo, f, 1, 1, NB)
                then(dve.tensor_tensor(w12[:], hot[1][:], expo[:], ALU.mult))
                then(dve.tensor_reduce(s12[:], w12[:], AX.X, ALU.add))
                then(dve.tensor_reduce(z[:], expo[:], AX.X, ALU.add))
                then(dve.scalar_tensor_tensor(den[:], z[:], 1e-9, s12[:], ALU.mult, ALU.add))
                then(dve.reciprocal(den[:], den[:]))
                then(dve.tensor_tensor(w12[:], w12[:], wide(den), ALU.mult))
                wait(dve, s_cps, f, 1, 0, NB)
                then(dve.tensor_copy(comb[:, :, 0:E1], w12[:]))
                then(dve.tensor_tensor(comb[:, :, E1:2 * E1], w12[:], comb[:, :, 0:E1].bitcast(F32), ALU.subtract))
                assert done[0] == COMB_STEPS

            def layernorm_stats(batch, stat, mv, veps, s_x, s_bn, s_ve):
                wait_first(dve, s_own_d, s_x, batch, 1, 1, NB)
                for t in range(NT):
                    dve.bn_stats(stat[:, t, :], x_res[:, batch * NT + t, :]).then_inc(s_bn, 1)
                wait_first(dve, s_own_d, s_bn, batch, 2 * NT, NT, 2 * NT * NB)
                for t in range(NT):
                    dve.bn_aggr(mv[:, t, :], stat[:, t, :]).then_inc(s_bn, 1)
                wait(dve, s_bn, batch, 2 * NT, 2 * NT, 2 * NT * NB)
                dve.tensor_scalar(veps[:], mv[:, :, 1], EPS, None, ALU.add).then_inc(s_ve, 1)

            def body(b):
                f, nxt = b - 1, b + 1
                if exists(f):
                    wait(dve, s_ao, f, 1, 1, NB)
                    wait(dve, s_bo, f, 1, 1, NB)
                    x_f = x_res[:, ds(f * NT, NT), :]
                    dve.tensor_tensor(x_f, ps[:, OUT, :].rearrange("p (t d) -> p t d", t=NT), x_f,
                                      ALU.add).then_inc(s_x4, 1)
                    layernorm_stats(f, stat4, mv4, veps4, s_x4, s_bn4, s_ve4)
                    wait(dve, s_rstd4, f, 1, 1, NB)
                    wait(dve, s_x4t, f, 1, 0, NB)
                    for t in range(NT):
                        last = dve.tensor_scalar(xn4[:, t, :], x_res[:, f * NT + t, :], mv4[:, t, 0:1],
                                                 rstd4[:, t:t + 1], ALU.subtract, ALU.mult)
                    last.then_inc(s_xn4, 1)
                    wait(dve, s_x4h, f, 1, 1, NB)
                    dve.tensor_tensor(x4_lo[:], ps[:, ring_bank("x4t", 0), :], x4_hi[:].bitcast(F32),
                                      ALU.subtract).then_inc(s_x4l, 1)
                if exists(nxt):
                    wait(dve, s_y, nxt, 16 * NT, 16 * NT, 16 * NT * NB)
                    x_n = x_res[:, ds(nxt * NT, NT), :]
                    dve.tensor_tensor(x_n, y[:], x_n, ALU.add).then_inc(s_x3, 1)
                    layernorm_stats(nxt, stat3, mv3, veps3, s_x3, s_bn3, s_ve3)
                if exists(f):
                    comb_weights(f)
                experts_tile(b, 0)
                if exists(nxt):
                    wait(dve, s_rstd3, nxt, 1, 1, NB)
                    if exists(b):
                        wait(dve, s_g, b, G_BANKS, G_BANKS, G_BANKS * NB)
                    for t in range(NT):
                        last = dve.tensor_scalar(xn3[:, t, 0:D], x_res[:, nxt * NT + t, :], mv3[:, t, 0:1],
                                                 rstd3[:, t:t + 1], ALU.subtract, ALU.mult)
                    last.then_inc(s_xn3, 1)
                experts_tile(b, 1)
                experts_tile(b, 2)
                if exists(b):
                    wait(dve, s_n, b, 1, 1, NB)
                    wait(dve, s_inv, b, 1, 0, NB)
                    dve.tensor_scalar(norm[:], ps[:, NORM, :], 1e-6, None, ALU.add).then_inc(s_norm, 1)
                    wait(dve, s_norm, b, 1, 1, NB)
                    wait(dve, s_ipk, b, 1, 0, NB)
                    dve.reciprocal(inv[:], norm[:]).then_inc(s_inv, 1)
                    wait(dve, s_ihalf, b, 1, 1, NB)
                    wait(dve, s_bc, b, 8, 0, 8 * NB)
                    dve.tensor_tensor(inv_pk[:], inv[:], inv_half[:].bitcast(F32), ALU.subtract).then_inc(s_ipk, 1)
                experts_tile(b, 3)
                experts_tile(b, 4)
                if exists(b):
                    for j in range(PAIRS):
                        wait(dve, s_bc, b, 8, j + 1, 8 * NB)
                        wait(dve, s_n, b, 1, 1, NB)
                        dve.tensor_tensor(phi_q[:, j, :], ps[:, ring_bank("inv", j), :], phi_q[:, j, :],
                                          ALU.mult).then_inc(s_qn, 1)
                if exists(f):
                    wait(dve, s_dn, f, 1, 1, NB)
                    x_f = x_res[:, ds(f * NT, NT), :]
                    dve.tensor_tensor(x_f, ps[:, DOWN, :].rearrange("p (t d) -> p t d", t=NT), x_f,
                                      ALU.add).then_inc(s_xo, 1)
                if exists(nxt):
                    wait(dve, s_x3h, nxt, 1, 1, NB)
                    dve.tensor_tensor(x3_lo[:], ps[:, ring_bank("x3t", 0), :], x3_hi[:].bitcast(F32),
                                      ALU.subtract).then_inc(s_x3l, 1)

            dve.memset(xn3[:, :, D:D + 2], 1.0).then_inc(s_set, 1)
            dve.memset(ksum[:], 0.0).then_inc(s_set, 1)
            dve.memset(comb[:].bitcast(F32), 0.0).then_inc(s_set, 1)
            dve.memset(minus_half[:], -0.5).then_inc(s_set, 1)
            dve.wait_ge(s_w, W_ALL)
            for n, (dst, src) in enumerate(((w_gate, stage[:, 0]), (w_up, stage[:, 1]), (w_rt, w_rt_stage[:]))):
                dve.tensor_copy(dst[:, 0], src).then_inc(s_split, 1)
                dve.wait_ge(s_split, 2 * n + 1)
                dve.tensor_tensor(dst[:, 1], src, dst[:, 0].bitcast(F32), ALU.subtract).then_inc(s_split, 1)
            dve.tensor_copy(spread[:], spread_stage[:, 0:PAIRS]).then_inc(s_split, 1)
            dve.tensor_copy(spread_e[:], spread_stage[:, PAIRS:]).then_inc(s_split, 1)
            dve.wait_ge(s_set, 4)
            turns(dve, body)

        @block.gpsimd
        def _(pool):
            def gather(batch):
                wait_first(pool, s_own_p, s_y, batch, 16 * NT, 0, 16 * NT * NB)
                pool.tensor_copy(pos_y[:], pos[:, ds(batch * NT, NT)]).then_inc(s_posy, 1)
                wait(pool, s_x3, batch, 1, 0, NB)
                wait_first(pool, s_own_p, s_posy, batch, 1, 1, NB)
                for t in range(NT):
                    pool.indirect_dma_start(y[:, t, :], None, y_sorted[:, :],
                                            bass.IndirectOffsetOnAxis(ap=pos_y[:, t:t + 1], axis=0)).then_inc(s_y, 16)

            def body(b):
                f, nxt = b - 1, b + 1
                if exists(nxt):
                    gather(nxt)
                if exists(f):
                    wait(pool, s_ve4, f, 1, 1, NB)
                    wait(pool, s_xn4, f, 1, 0, NB)
                    pool.tensor_tensor(rstd4[:], veps4[:], minus_half[:], ALU.pow).then_inc(s_rstd4, 1)
                if exists(nxt):
                    wait(pool, s_ve3, nxt, 1, 1, NB)
                    wait(pool, s_xn3, nxt, 1, 0, NB)
                    pool.tensor_tensor(rstd3[:], veps3[:], minus_half[:], ALU.pow).then_inc(s_rstd3, 1)
                if exists(b):
                    wait(pool, s_gsb, b, G_BANKS, G_BANKS, G_BANKS * NB)
                    wait(pool, s_n, b, 1, 0, NB)
                    pool.tensor_tensor(ksum[:, :, 0:8], g_sb[:, :, D:D + 1].broadcast_to([P, PAIRS, 8]), own_head[:],
                                       ALU.mult).then_inc(s_ksum, 1)
                if exists(nxt):
                    wait(pool, s_xn3, nxt, 1, 1, NB)
                    x_n = x_res[:, ds(nxt * NT, NT), :]
                    pool.tensor_tensor(x_n, x_n, b_o[:].unsqueeze(1).broadcast_to([P, NT, D]),
                                       ALU.add).then_inc(s_bo, 1)

            pool.wait_ge(s_set, 4)
            pool.wait_ge(s_w, W_ALL)
            turns(pool, body)


def pairs_diagonal(w):
    import numpy as np

    heads, rows, cols = w.shape
    out = np.zeros((2 * rows, heads // 2, 2 * cols), np.float32)
    for i in range(2):
        out[i * rows:(i + 1) * rows, :, i * cols:(i + 1) * cols] = w[i::2].transpose(1, 0, 2)
    return out


def host_layouts(a):
    import numpy as np

    f = np.float32
    w_qkv, b_qkv = a["L0_attn_w_qkv"], a["L0_attn_b_qkv"]
    w4 = {n: np.zeros((D, H0, SLOT), f) for n in "qk"}
    b4 = {n: np.zeros((H0, SLOT), f) for n in "qk"}
    for i, n in enumerate("qk"):
        w = w_qkv[:, i * D:(i + 1) * D].reshape(D, H0, HD0)
        b = b_qkv[i * D:(i + 1) * D].reshape(H0, HD0)
        for c in range(3):
            w4[n][:, :, c * HD0:(c + 1) * HD0] = w
            b4[n][:, c * HD0:(c + 1) * HD0] = b
    b4["k"][:, MAXROW_HI] = 1.0
    b4["k"][:, MAXROW_LO] = 1.0
    b_qk = np.stack([b4["q"].reshape(GROUPS, P).T, b4["k"].reshape(GROUPS, P).T], axis=1)
    lo = np.zeros((P, 2), f)
    row = np.arange(P) % SLOT
    lo[:, 0] = (row >= 2 * HD0) & (row < 3 * HD0)
    lo[:, 1] = (row >= HD0) & (row < 2 * HD0)
    rep = lambda v: np.broadcast_to(v, (P, v.shape[0]))
    i = np.arange(P)
    by_middle = lambda w: w.transpose(1, 0, 2).reshape(D, -1)
    spread, own_head = np.zeros((P, PAIRS, P), f), np.zeros((P, PAIRS, 8), f)
    for j in range(PAIRS):
        for c in range(2):
            for half in range(2):
                spread[LOG_ROWS * (j % 4) + 2 * (j // 4) + c + 4 * half, j, HD1 * c:HD1 * (c + 1)] = 1.0
                own_head[HD1 * c:HD1 * (c + 1), j, 2 * (j // 4) + c + 4 * half] = 1.0
    low = np.zeros((P, 1), f)
    low[np.arange(P) % LOG_ROWS // 4 == 1] = 1.0
    spread_e = np.zeros((P, FFN_TILES - 1, P), f)
    for e in range(E1):
        for half in range(2):
            spread_e[e + E1 * half, e // 4, MID1 * (e % 4):MID1 * (e % 4 + 1)] = 1.0
    return {
        "x": a["L0_attn_x"].reshape(NB * SEQ, D),
        "w_q4": w4["q"].reshape(D, -1), "w_k4": w4["k"].reshape(D, -1), "w_v0": w_qkv[:, 2 * D:],
        "b_qk": b_qk, "lo_rows": lo, "b_v": rep(b_qkv[2 * D:]), "b_o0": rep(a["L0_attn_b_out"]),
        "w_o0": a["L0_attn_w_out"], "router0": a["L0_ffn_gate_w"],
        "iota_e": rep(np.arange(E0, dtype=f)), "iota_q": rep(np.arange(SLOTS, dtype=f)),
        "before": (i[:, None] < i[None, :]).astype(f),
        "w_qkv1_t": a["L1_attn_W_qkv"].reshape(D, 24, P).transpose(2, 1, 0),
        "rf1": pairs_diagonal(a["L1_attn_RF"]), "w_out1": pairs_diagonal(a["L1_attn_W_out"].reshape(H1, HD1, D)),
        "w_shared0": np.concatenate([a["L0_ffn_shared_gate_w"], a["L0_ffn_shared_up_w"]], axis=1),
        "w_shared_dn0": a["L0_ffn_shared_down_w"].reshape(2, P, D).transpose(1, 0, 2),
        "w_gate0": a["L0_ffn_routed_gate_w"].transpose(1, 0, 2), "w_up0": a["L0_ffn_routed_up_w"].transpose(1, 0, 2),
        "w_down0": a["L0_ffn_routed_down_w"].reshape(E0, 2, P, D).transpose(2, 0, 1, 3),
        "w_gate1": np.concatenate([by_middle(a["L1_ffn_wg_s"]), by_middle(a["L1_ffn_wg_r"])], axis=1),
        "w_up1": np.concatenate([by_middle(a["L1_ffn_wu_s"]), by_middle(a["L1_ffn_wu_r"])], axis=1),
        "w_down1": np.concatenate([a["L1_ffn_wd_s"].reshape(-1, D), a["L1_ffn_wd_r"].reshape(-1, D)])
                     .reshape(FFN_TILES, P, D).transpose(1, 0, 2),
        "router1": a["L1_ffn_router_w"], "b_o1": rep(a["L1_attn_b_out"]),
        "spread": spread, "spread_e": spread_e, "low": low, "own_head": own_head,
        "iota1": np.broadcast_to(np.arange(E1, dtype=f), (P, NT, E1)),
        "iota64": np.broadcast_to(np.arange(E1, dtype=f) - f(64), (P, NT, E1)),
        "mask": np.where(i[None, :] < i[:, None], f(-BIG), f(0)), "ident": np.eye(P, dtype=f),
    }


def two_layers(nc, dram, out):
    x_sorted = nc.dram_tensor("x_sorted", (SLOTS * P, D), F32, kind="Internal").ap()
    y_sorted = nc.dram_tensor("y_sorted", (SLOTS * P, D), F32, kind="Internal").ap()
    with ExitStack() as ctx:
        def sb(name, shape, dt=F32):
            return ctx.enter_context(nc.sbuf_tensor(name, shape, dt))

        mem = {"x_res": sb("x_res", [P, TILES, D]), "ident": sb("ident", [P, P]), "ident_r": sb("ident_r", [P, P], F32R),
               "mean2": sb("mean2", [P, TILES]), "rstd2": sb("rstd2", [P, TILES]),
               "pos": sb("pos", [P, TILES], I32), "score": sb("score", [P, TILES]),
               "slot_expert": sb("slot_expert", [P, SLOTS], I32),
               "w_qf": sb("w_qf", [P, 2, H1 * HD1], F32R), "w_kf": sb("w_kf", [P, 2, H1 * HD1], F32R),
               "w_vo": sb("w_vo", [P, H1, D])}
        with nc.sbuf_tensor("logits", [P, TILES, E0], F32) as logits:
            mem["logits"] = logits
            layer0_attention(nc, mem, dram, x_sorted)
            routing(nc, mem, dram)
        layer0_experts(nc, mem, dram, x_sorted, y_sorted)
        layer1(nc, mem, dram, y_sorted, out)


def kernel(**inputs):
    import numpy as np
    import concourse.bacc as bacc
    from concourse.bass_utils import run_bass_kernel_spmd

    nc = bacc.Bacc("TRN2", target_bir_lowering=False, num_devices=1)
    arrays, dram = {}, {}
    for name, value in host_layouts({n: np.asarray(v) for n, v in inputs.items()}).items():
        value = np.ascontiguousarray(value)
        arrays["in_" + name] = value
        dram[name] = nc.dram_tensor("in_" + name, value.shape, mybir.dt.from_np(value.dtype), kind="ExternalInput").ap()
    out = nc.dram_tensor("out", (NB * SEQ, D), F32, kind="ExternalOutput").ap()
    two_layers(nc, dram, out)
    r = run_bass_kernel_spmd(nc, [arrays], core_ids=[0])
    return r.results[0]["out"].reshape(NB, SEQ, D)
```

```python
from contextlib import ExitStack

import concourse.bass as bass
from concourse import mybir
from concourse.bass import ds

F32 = mybir.dt.float32
F32R = mybir.dt.float32r
BF16 = mybir.dt.bfloat16
I32 = mybir.dt.int32
ALU = mybir.AluOpType
ACT = mybir.ActivationFunctionType
AX = mybir.AxisListType

P = 128
D = 128
NB, SEQ = 16, 512
NT = SEQ // P
TILES = NB * NT
EPS = 1e-5

E0, MID0 = 32, 256
SLOTS = TILES + E0
ZERO_TILES = 8

H1, HD1 = 16, 64

H0, HD0 = 16, 8
GROUPS = 4
GH = H0 // GROUPS
SLOT = 32
MAXROW_HI, MAXROW_LO = 24, 25
ONES_COL = 8
BIG = 1e30
STEPS = NB * GROUPS
SCORE_TILES = [(s, h, n) for s, n in enumerate((1, 1, 2, 4)) for h in range(0, GH, n)]
UNITS = len(SCORE_TILES)
FIRST_UNIT = [next(u for u, t in enumerate(SCORE_TILES) if t[0] == s) for s in range(NT)] + [UNITS]
PV_AFTER = (1, 3, 1, 0)
SPLIT_WEIGHTS = (("w_q4", 512), ("w_k4", 512), ("w_v0", 128))
A_BANKS, B_BANKS = 3, 2
FIN_AFTER = (1, 2)
HALF_BEFORE = (0, 2)


def score_bank(banks, g, u):
    return (UNITS * g + u) % banks


def read_before(banks, g, u):
    at = UNITS * g + u - 1
    while score_bank(banks, 0, at % (UNITS * GROUPS)) != score_bank(banks, g, u):
        at -= 1
    return at + 1


def wait(eng, sem, batch, per_batch, n, total):
    if isinstance(batch, int):
        value = min(batch * per_batch + n, total)
        if value > 0:
            eng.wait_ge(sem, value)
    else:
        eng.wait_ge(sem, batch * per_batch + n)


def wait_first(eng, own, sem, batch, per_batch, n, total):
    wait(eng, sem, batch, per_batch, n, total)
    eng.sem_inc(own, 1)


def shifted(batch, group, by):
    at = group + by
    return batch + at // GROUPS, at % GROUPS


def exists(batch):
    return not isinstance(batch, int) or 0 <= batch < NB


def layer0_attention(nc, mem, dram, x_sorted):
    x_res, mean2, rstd2, logits = mem["x_res"], mem["mean2"], mem["rstd2"], mem["logits"]
    ident, ident_r = mem["ident"], mem["ident_r"]
    with ExitStack() as ctx:
        def sb(name, shape, dt=F32):
            return ctx.enter_context(nc.sbuf_tensor(name, shape, dt))

        def pb(name, shape, dt=F32):
            return ctx.enter_context(nc.psum_tensor(name, shape, dt))

        def sem(name):
            return ctx.enter_context(nc.semaphore(name))

        zeros = sb("zeros", [P, D])
        w_q = sb("w_q", [P, 2, GROUPS, P], F32R)
        w_k = sb("w_k", [P, 2, GROUPS, P], F32R)
        w_v = sb("w_v", [P, 2, P], F32R)
        w_o = sb("w_o", [P, P])
        w_router = sb("w_router", [P, 32])
        b_qk = sb("b_qk", [P, 2, GROUPS])
        lo_rows = sb("lo_rows", [P, 2])
        b_qk_lo = sb("b_qk_lo", [P, 2, GROUPS])
        b_v = sb("b_v", [P, D])
        b_o = sb("b_o", [P, D])
        ident_b = sb("ident_b", [P, P], BF16)
        mask = sb("mask", [P, P])
        mask_b = sb("mask_b", [P, P], BF16)
        minus_half = sb("minus_half", [P, NT])

        stat1 = sb("stat1", [P, NT, 6])
        mv1 = sb("mv1", [P, NT, 2])
        veps1 = sb("veps1", [P, NT])
        rstd1 = sb("rstd1", [P, NT])
        xn = sb("xn", [P, NT, D])
        xt_hi = sb("xt_hi", [P, SEQ], F32R)
        xt_lo = sb("xt_lo", [P, SEQ], F32R)
        half = sb("half", [P, 2, SEQ], F32R)
        q_pk = sb("q_pk", [P, GROUPS, SEQ], F32R)
        k_pk = sb("k_pk", [P, 2, SEQ], F32R)
        k_z = sb("k_z", [P, GROUPS, GH, SEQ], F32R)
        v_pk = sb("v_pk", [P, NT, H0, SLOT])
        neg_max = sb("neg_max", [P, 2, NT, GH])
        max_pad = sb("max_pad", [P, 2, NT, P], F32R)
        probs = sb("probs", [P, 2, GH, SEQ])
        o_sb = sb("o_sb", [P, 2, SEQ])
        rsum = sb("rsum", [P, NT * GH])
        attn = sb("attn", [P, NT, D])
        attn_t = sb("attn_t", [P, SEQ])
        stat_tmp = sb("stat_tmp", [P, NT, 6])
        mv2 = sb("mv2", [P, NT, 2])
        veps2 = sb("veps2", [P, NT])
        xn2 = sb("xn2", [P, NT, D])
        xn2_t = sb("xn2_t", [P, SEQ])

        ps_a = [pb(f"ps_a{i}", [P, 512]) for i in range(A_BANKS)]
        ps_b = [pb(f"ps_b{i}", [P, 512]) for i in range(B_BANKS)]
        ps_o = pb("ps_o", [P, 512])
        ps_m = [pb(f"ps_m{i}", [P, 512]) for i in range(2)]

        s_w = sem("s_w")
        s_split = sem("s_split")
        s_stage = sem("s_stage")
        s_x0, s_x12, s_xr = sem("s_x0"), sem("s_x12"), sem("s_xr")
        s_tab = mem["own_act"]
        s_kz = [sem("s_kz0"), sem("s_kz1")]
        s_set = sem("s_set")
        s_kz_zero = sem("s_kz_zero")
        s_bn, s_bn2 = sem("s_bn"), sem("s_bn2")
        s_veps1, s_rstd1, s_xn = sem("s_veps1"), sem("s_rstd1"), sem("s_xn")
        s_mx, s_xh, s_xl = sem("s_mx"), sem("s_xh"), sem("s_xl")
        s_proj, s_half, s_fin = sem("s_proj"), sem("s_half"), sem("s_fin")
        s_vps, s_v = sem("s_vps"), sem("s_v")
        s_a, s_max = sem("s_a"), sem("s_max")
        s_mcut, s_mps, s_qmax = sem("s_mcut"), sem("s_mps"), sem("s_qmax")
        s_b, s_exp, s_mask, s_pv, s_o = sem("s_b"), sem("s_exp"), sem("s_mask"), sem("s_pv"), sem("s_o")
        s_ot, s_rs, s_attn = sem("s_ot"), sem("s_rs"), sem("s_attn")
        s_atps, s_at, s_ops, s_x1 = sem("s_atps"), sem("s_at"), sem("s_ops"), sem("s_x1")
        s_bo = sem("s_bo")
        s_next = sem("s_next")
        s_mean2 = sem("s_mean2")
        s_veps2, s_rstd2, s_xn2 = sem("s_veps2"), sem("s_rstd2"), sem("s_xn2")
        s_n2ps, s_n2t, s_lgps, s_lg = sem("s_n2ps"), sem("s_n2t"), sem("s_lgps"), sem("s_lg")

        STEP4 = GROUPS
        UNIT = GROUPS * UNITS
        SPREAD = 16 * GH * GROUPS // 2

        block = ctx.enter_context(nc.Block())

        @block.sync
        def _(sp):
            x_dram = dram["x"].rearrange("(b t p) d -> b p t d", p=P, t=NT)
            sp.dma_start(x_res[:, 0:NT, :], x_dram[0]).then_inc(s_x0, 16)
            for n, (name, width) in enumerate(SPLIT_WEIGHTS):
                sp.dma_start(probs[:, 0, n, 0:width], dram[name]).then_inc(s_stage, 16)
            for dst, name in ((w_o[:], "w_o0"), (w_router[:], "router0"), (b_qk[:], "b_qk"),
                              (lo_rows[:], "lo_rows"), (b_v[:], "b_v"), (b_o[:], "b_o0"),
                              (mask[:], "mask"), (ident[:], "ident")):
                sp.dma_start(dst, dram[name]).then_inc(s_w, 16)
            sp.dma_start(x_res[:, NT:3 * NT, :], dram["x"][SEQ:3 * SEQ].rearrange("(t p) d -> p t d", p=P)
                         ).then_inc(s_x12, 16)
            x_zero = x_sorted.rearrange("(c q p) d -> c p q d", p=P, q=ZERO_TILES)

            def bulk(b, g):
                if b == 0:
                    for n in range(3 + g, NB, GROUPS):
                        sp.dma_start(x_res[:, n * NT:(n + 1) * NT, :], x_dram[n]).then_inc(s_xr, 16)
                if b == 1:
                    if g == 0:
                        sp.wait_ge(s_set, 5)
                    for n in range(g, SLOTS // ZERO_TILES, GROUPS):
                        sp.dma_start(x_zero[n], zeros[:].unsqueeze(1).broadcast_to([P, ZERO_TILES, D])
                                     ).then_inc(s_next, 16)
                if b == NB - 1:
                    for dst, name in mem["preload"][g::GROUPS]:
                        sp.dma_start(dst, dram[name]).then_inc(s_next, 16)

            def body(b):
                for g in range(GROUPS):
                    if isinstance(b, int):
                        bulk(b, g)
                    bp, gp = shifted(b, g, 3)
                    if exists(bp):
                        wait_first(sp, mem["own_sp"], s_fin, bp, 2 * STEP4, 2 * gp + 1, 2 * STEPS)
                        wait(sp, s_b, b, UNIT, UNITS * g, UNITS * STEPS)
                        for h in range(GH):
                            rows = slice(SLOT * h, SLOT * (h + 1))
                            sp.dma_start(k_z[rows, gp, h, :].bitcast(F32),
                                         k_pk[rows, gp % 2, :].bitcast(F32)).then_inc(s_kz[gp % 2], 16)

            sp.wait_ge(s_kz_zero, 1)
            body(-1)
            body(0)
            body(1)
            with sp.Fori(2, NB - 1) as b:
                body(b)
            body(NB - 1)
            sp.wait_ge(s_next, 16 * (SLOTS // ZERO_TILES + len(mem["preload"])))

        @block.tensor
        def _(pe):
            def score_tiles(b, g, s, do_a, do_b, after):
                ba, ga = shifted(b, g, 2)
                n = SEQ - s * P
                for u in range(FIRST_UNIT[s], FIRST_UNIT[s + 1]):
                    _, h0, heads = SCORE_TILES[u]
                    if do_a:
                        if u == 0:
                            wait(pe, s_fin, ba, 2 * STEP4, 2 * ga + 2, 2 * STEPS)
                            wait(pe, s_kz[ga % 2], ba, SPREAD, 16 * GH * (ga // 2 + 1), SPREAD * NB)
                        wait(pe, s_max, ba, UNIT, read_before(A_BANKS, ga, u), UNITS * STEPS)
                        bank = ps_a[score_bank(A_BANKS, ga, u)]
                        pe.matmul(bank[:, 0:heads * n], q_pk[:, ga, s * P:(s + 1) * P],
                                  k_z[:, ga, h0:h0 + heads, s * P:SEQ], start=True, stop=False,
                                  skip_group_check=True)
                        pe.matmul(bank[:, 0:heads * n].rearrange("p (h c) -> p h c", h=heads)[:, :, 0:P],
                                  ident_b[:], mask_b[:].unsqueeze(1).broadcast_to([P, heads, P]),
                                  start=False, stop=True, skip_group_check=True).then_inc(s_a, 1)
                    if do_b:
                        if u == 0:
                            wait(pe, s_qmax, b, STEP4, g + 1, STEPS)
                        wait(pe, s_exp, b, UNIT, read_before(B_BANKS, g, u), UNITS * STEPS)
                        kb = NT - 1 - s
                        for h in range(heads):
                            last = pe.matmul(ps_b[score_bank(B_BANKS, g, u)][:, h * n:(h + 1) * n],
                                             k_z[:, g, h0 + h, kb * P:(kb + 1) * P], q_pk[:, g, 0:n],
                                             start=(h == 0), stop=(h == heads - 1), skip_group_check=True)
                        last.then_inc(s_b, 1)
                    if u in after:
                        after[u]()

            def probs_times_v(b, g, s):
                n = SEQ - s * P
                if s == 0:
                    wait(pe, s_o, b, STEP4, g, STEPS)
                    if g == 0:
                        wait(pe, s_v, b, 1, 1, NB)
                wait(pe, s_mask, b, NT * STEP4, NT * g + s + 1, NT * STEPS)
                for j in range(GH):
                    last = pe.matmul(ps_o[SLOT * j:SLOT * (j + 1), 0:n], v_pk[:, NT - 1 - s, GH * g + j, :],
                                     probs[:, s % 2, j, 0:n], start=(s == 0), stop=(s == NT - 1),
                                     skip_group_check=True)
                last.then_inc(s_pv, 1)

            def three_passes(out, pairs):
                (a_hi, a_lo), (c_hi, c_lo) = pairs
                pe.matmul(out, a_hi, c_hi, start=True, stop=False)
                pe.matmul(out, a_lo, c_hi, start=False, stop=False)
                return pe.matmul(out, a_hi, c_lo, start=False, stop=True)

            def batch_jobs_read(b, g):
                if isinstance(b, int):
                    wait(pe, s_at, b, 1, 0 if g >= 1 else -1, NB)
                    wait(pe, s_n2t, b, 1, 0 if g >= 3 else -1, NB)
                    wait(pe, s_lg, b, 1, -1, NB)
                    wait(pe, s_xl, b, 1, 2 if g >= 1 else 1, NB)
                    wait(pe, s_x1, b, 1, 0 if g >= 2 else -1, NB)
                    wait(pe, s_v, b, 1, 1, NB)
                    wait(pe, s_qmax, b, STEP4, g + 1, STEPS)
                    wait(pe, s_attn, b, STEP4, g - 1, STEPS)

            def project(b, g, i):
                bp, gp = shifted(b, g, 3)
                if not exists(bp):
                    return
                if i == 0:
                    wait(pe, s_xl, bp, 1, 1, NB)
                    if g == 0:
                        wait(pe, s_lg, b, 1, -1, NB)
                    elif g == 1:
                        wait(pe, s_at, b, 1, 0, NB)
                    elif g == 2:
                        wait(pe, s_qmax, b, STEP4, g + 1, STEPS)
                    else:
                        wait(pe, s_n2t, b, 1, 0, NB)
                    if isinstance(b, int):
                        wait(pe, s_qmax, b, STEP4, g + 1, STEPS)
                else:
                    batch_jobs_read(b, g)
                    if g == 0:
                        wait(pe, s_v, b, 1, 1, NB)
                    elif g == 2:
                        wait(pe, s_x1, b, 1, 0, NB)
                    elif g == 3:
                        wait(pe, s_attn, b, STEP4, g - 1, STEPS)
                w = (w_k, w_q)[i][:, :, gp, :]
                three_passes(ps_m[i][:], ((w[:, 0], w[:, 1]), (xt_hi[:], xt_lo[:]))).then_inc(s_proj, 1)

            def side_jobs(b, g, s):
                bp, gp = shifted(b, g, 3)
                if s == 0:
                    project(b, g, 0)
                    project(b, g, 1)
                if s == 2:
                    batch_jobs_read(b, g)
                    bm, gm = shifted(b, g, 1)
                    if exists(bm):
                        wait(pe, s_fin, bp, 2 * STEP4, 2 * gp + 1, 2 * STEPS)
                        wait(pe, s_mcut, bm, 2 * STEP4, 2 * gm + 2, 2 * STEPS)
                        for t in range(NT):
                            last = pe.matmul(ps_m[0][:, t * P:(t + 1) * P], max_pad[:, gm % 2, t, :], ident_r[:],
                                             start=True, stop=True)
                        last.then_inc(s_mps, 1)
                    bo, go = shifted(b, g, -1)
                    if exists(bo):
                        wait(pe, s_fin, bp, 2 * STEP4, 2 * gp + 2, 2 * STEPS)
                        wait(pe, s_o, b, STEP4, g, STEPS)
                        for t in range(NT):
                            last = pe.transpose(ps_m[1][:, t * P:(t + 1) * P],
                                                o_sb[:, go % 2, t * P:(t + 1) * P], ident[:])
                        last.then_inc(s_ot, 1)
                if s != 3:
                    return
                m0_jobs = g in (0, 2, 3) and exists(b - 1)
                m1_jobs = (g == 1 and exists(b - 1)) or (g in (0, 3) and exists(b + 1))
                if m0_jobs or m1_jobs:
                    wait(pe, s_fin, bp, 2 * STEP4, 2 * gp + 2, 2 * STEPS)
                    batch_jobs_read(b, g)
                if m0_jobs:
                    wait(pe, s_qmax, b, STEP4, g + 2, STEPS)
                if m1_jobs:
                    wait(pe, s_attn, b, STEP4, g, STEPS)
                if g == 0:
                    if exists(b - 1):
                        wait(pe, s_attn, b, STEP4, 0, STEPS)
                        for t in range(NT):
                            last = pe.transpose(ps_m[0][:, t * P:(t + 1) * P], attn[:, t, :], ident[:])
                        last.then_inc(s_atps, 1)
                    if exists(b + 1):
                        wait(pe, s_xn, b, 1, 2, NB)
                        for t in range(NT):
                            last = pe.transpose(ps_m[1][:, t * P:(t + 1) * P], xn[:, t, :], ident[:])
                        last.then_inc(s_mx, 1)
                if g == 1 and exists(b - 1):
                    wait(pe, s_at, b, 1, 0, NB)
                    for t in range(NT):
                        last = pe.matmul(ps_m[1][:, t * P:(t + 1) * P], attn_t[:, t * P:(t + 1) * P], w_o[:],
                                         start=True, stop=True)
                    last.then_inc(s_ops, 1)
                if g == 2 and exists(b - 1):
                    wait(pe, s_xn2, b, 1, 0, NB)
                    for t in range(NT):
                        last = pe.transpose(ps_m[0][:, t * P:(t + 1) * P], xn2[:, t, :], ident[:])
                    last.then_inc(s_n2ps, 1)
                if g == 3 and exists(b - 1):
                    wait(pe, s_n2t, b, 1, 0, NB)
                    for t in range(NT):
                        last = pe.matmul(ps_m[0][:, 32 * t:32 * (t + 1)], xn2_t[:, t * P:(t + 1) * P], w_router[:],
                                         start=True, stop=True)
                    last.then_inc(s_lgps, 1)
                if g == 3 and exists(b + 1):
                    for t in range(NT):
                        x_pair = (xt_hi[:, t * P:(t + 1) * P], xt_lo[:, t * P:(t + 1) * P])
                        last = three_passes(ps_m[1][:, t * P:(t + 1) * P], (x_pair, (w_v[:, 0], w_v[:, 1])))
                    last.then_inc(s_vps, 1)

            def body(b):
                for g in range(GROUPS):
                    do_a = exists(shifted(b, g, 2)[0])
                    do_b = exists(b)
                    for s in range(NT):
                        bv, gv = (b, g) if s else shifted(b, g, -1)
                        pv = (lambda: probs_times_v(bv, gv, (s - 1) % NT)) if exists(bv) else (lambda: None)
                        score_tiles(b, g, s, do_a, do_b, {FIRST_UNIT[s] + PV_AFTER[s]: pv})
                        side_jobs(b, g, s)

            pe.wait_ge(s_split, 9)
            pe.wait_ge(s_w, 16 * 8)
            body(-1)
            body(0)
            body(1)
            with pe.Fori(2, NB - 1) as b:
                body(b)
            body(NB - 1)
            body(NB)

        @block.scalar
        def _(act):
            def high_half(b, g, i):
                bp, gp = shifted(b, g, 3)
                if exists(bp):
                    wait(act, s_proj, bp, 2 * STEP4, 2 * gp + i + 1, 2 * STEPS)
                    wait(act, s_fin, bp, 2 * STEP4, 2 * (gp - 1) + i + 1, 2 * STEPS)
                    act.activation(half[:, i, :], ps_m[i][:], ACT.Identity, bias=b_qk_lo[:, 1 - i, gp:gp + 1],
                                   scale=lo_rows[:, 1 - i:2 - i]).then_inc(s_half, 1)

            def body(b):
                for g in range(GROUPS):
                    for s in range(NT):
                        n = SEQ - s * P
                        if exists(b):
                            wait(act, s_pv, b, NT * STEP4, NT * g + s - 1, NT * STEPS)
                        for u in range(FIRST_UNIT[s], FIRST_UNIT[s + 1]):
                            if s == 1 and u - FIRST_UNIT[s] in HALF_BEFORE:
                                high_half(b, g, HALF_BEFORE.index(u - FIRST_UNIT[s]))
                            if exists(b):
                                _, h0, heads = SCORE_TILES[u]
                                wait(act, s_b, b, UNIT, UNITS * g + u + 1, UNITS * STEPS)
                                act.activation(probs[:, s % 2, h0:h0 + heads, 0:n],
                                               ps_b[score_bank(B_BANKS, g, u)][:, 0:heads * n].rearrange("p (h c) -> p h c", h=heads),
                                               ACT.Exp, scale=HD0 ** -0.5).then_inc(s_exp, 1)
                        bo, go = shifted(b, g, -1)
                        if s == 0 and exists(bo):
                            wait(act, s_pv, b, NT * STEP4, NT * g, NT * STEPS)
                            wait(act, s_ot, b, STEP4, g - 2, STEPS)
                            act.copy(o_sb[:, go % 2, :], ps_o[:]).then_inc(s_o, 1)
                        if (g, s) == (0, 3):
                            if exists(b - 1):
                                wait(act, s_atps, b, 1, 0, NB)
                                wait(act, s_ops, b, 1, -1, NB)
                                act.copy(attn_t[:], ps_m[0][:]).then_inc(s_at, 1)
                            if exists(b + 1):
                                wait(act, s_mx, b, 1, 2, NB)
                                act.copy(xt_hi[:], ps_m[1][:]).then_inc(s_xh, 1)
                        if (g, s) == (2, 3) and exists(b - 1):
                            wait(act, s_n2ps, b, 1, 0, NB)
                            wait(act, s_lgps, b, 1, -1, NB)
                            act.copy(xn2_t[:], ps_m[0][:]).then_inc(s_n2t, 1)

            act.wait_ge(s_split, 10)
            act.wait_ge(s_w, 16 * 8)
            act.activation(rsum[:, 0:1], minus_half[:, 0:1], ACT.Exp).then_inc(s_tab, 1)
            body(-1)
            body(0)
            body(1)
            with act.Fori(2, NB - 1) as b:
                body(b)
            body(NB - 1)
            body(NB)

        @block.vector
        def _(dve):
            def finish_projection(b, g, i):
                bp, gp = shifted(b, g, 3)
                if not exists(bp):
                    return
                if i == 0:
                    wait(dve, s_kz[gp % 2], bp, SPREAD, 16 * GH * (gp // 2), SPREAD * NB)
                wait(dve, s_half, bp, 2 * STEP4, 2 * gp + i + 1, 2 * STEPS)
                dve.scalar_tensor_tensor((k_pk[:, gp % 2, :], q_pk[:, gp, :])[i], ps_m[i][:],
                                         b_qk[:, 1 - i, gp:gp + 1], half[:, i, :].bitcast(F32), ALU.add,
                                         ALU.subtract).then_inc(s_fin, 1)

            def body(b):
                for g in range(GROUPS):
                    for s in range(NT):
                        n = SEQ - s * P
                        ba, ga = shifted(b, g, 2)
                        for u in range(FIRST_UNIT[s], FIRST_UNIT[s + 1]):
                            if exists(ba):
                                _, h0, heads = SCORE_TILES[u]
                                wait(dve, s_a, ba, UNIT, UNITS * ga + u + 1, UNITS * STEPS)
                                dve.tensor_reduce(neg_max[:, ga % 2, s, h0:h0 + heads],
                                                  ps_a[score_bank(A_BANKS, ga, u)][:, 0:heads * n].rearrange("p (h c) -> p h c", h=heads),
                                                  AX.X, ALU.max, negate=True).then_inc(s_max, 1)
                            if s == 1 and u - FIRST_UNIT[s] in FIN_AFTER:
                                finish_projection(b, g, FIN_AFTER.index(u - FIRST_UNIT[s]))
                        if (g, s) == (0, 0) and exists(b):
                            wait(dve, s_vps, b, 1, 1, NB)
                            wait(dve, s_pv, b, NT * STEP4, 0, NT * STEPS)
                            dve.tensor_tensor(v_pk[:, :, :, 0:HD0].rearrange("p t h d -> p t h d"),
                                              ps_m[1][:].rearrange("p (t h d) -> p t h d", t=NT, d=HD0),
                                              b_v[:].rearrange("p (h d) -> p h d", d=HD0).unsqueeze(1)
                                              .broadcast_to([P, NT, H0, HD0]), ALU.add).then_inc(s_v, 1)
                        if (g, s) == (0, 0) and exists(b + 1):
                            if isinstance(b, int) and b <= 0:
                                dve.wait_ge((s_x0, s_x12)[b + 1], 16)
                            for t in range(NT):
                                dve.bn_stats(stat1[:, t, :], x_res[:, (b + 1) * NT + t, :]).then_inc(s_bn, 1)
                            wait_first(dve, mem["own_dve"], s_bn, b, 2 * NT, 3 * NT, 1 << 20)
                            for t in range(NT):
                                dve.bn_aggr(mv1[:, t, :], stat1[:, t, :]).then_inc(s_bn, 1)
                            wait(dve, s_bn, b, 2 * NT, 4 * NT, 1 << 20)
                            dve.tensor_scalar(veps1[:], mv1[:, :, 1], EPS, None, ALU.add).then_inc(s_veps1, 1)
                        bm, gm = shifted(b, g, 1)
                        if s == 2 and exists(bm):
                            wait(dve, s_mps, bm, STEP4, gm + 1, STEPS)
                            dve.tensor_tensor(q_pk[:, gm, :], ps_m[0][:], q_pk[:, gm, :].bitcast(F32),
                                              ALU.add).then_inc(s_qmax, 1)
                        bo, go = shifted(b, g, -1)
                        if s == 2 and exists(bo):
                            wait(dve, s_ot, b, STEP4, g, STEPS)
                            heads = ps_m[1][:].rearrange("p (n c) -> p n c", c=SLOT)
                            dve.reciprocal(rsum[:], heads[:, :, ONES_COL]).then_inc(s_rs, 1)
                            wait(dve, s_rs, b, STEP4, g, STEPS)
                            if g == 1:
                                wait(dve, s_atps, b, 1, 0, NB)
                            dve.tensor_tensor(
                                attn[:, :, GH * HD0 * go:GH * HD0 * (go + 1)].rearrange("p t (h d) -> p t h d", d=HD0),
                                ps_m[1][:].rearrange("p (t h c) -> p t h c", t=NT, c=SLOT)[:, :, :, 0:HD0],
                                rsum[:].rearrange("p (t h) -> p t h", t=NT).unsqueeze(3)
                                .broadcast_to([P, NT, GH, HD0]), ALU.mult).then_inc(s_attn, 1)
                        bp, gp = shifted(b, g, 3)
                        if (g, s) == (0, 2) and exists(b + 1):
                            wait(dve, s_rstd1, b, 1, 2, NB)
                            wait(dve, s_mx, b, 1, 1, NB)
                            for t in range(NT):
                                last = dve.tensor_scalar(xn[:, t, :], x_res[:, (b + 1) * NT + t, :], mv1[:, t, 0:1],
                                                         rstd1[:, t:t + 1], ALU.subtract, ALU.mult)
                            last.then_inc(s_xn, 1)
                        if (g, s) == (0, 3) and exists(b + 1):
                            wait(dve, s_xh, b, 1, 2, NB)
                            dve.tensor_tensor(xt_lo[:], ps_m[1][:], xt_hi[:].bitcast(F32),
                                              ALU.subtract).then_inc(s_xl, 1)
                        if (g, s) == (1, 3) and exists(b - 1):
                            wait(dve, s_ops, b, 1, 0, NB)
                            wait(dve, s_bo, b, 1, 0, NB)
                            x_b = x_res[:, ds((b - 1) * NT, NT), :]
                            dve.tensor_tensor(x_b, ps_m[1][:].rearrange("p (t d) -> p t d", t=NT), x_b,
                                              ALU.add).then_inc(s_x1, 1)
                        if (g, s) == (2, 0) and exists(b - 1):
                            wait_first(dve, mem["own_dve"], s_x1, b, 1, 0, NB)
                            for t in range(NT):
                                dve.bn_stats(stat_tmp[:, t, :], x_res[:, (b - 1) * NT + t, :]).then_inc(s_bn2, 1)
                            wait_first(dve, mem["own_dve"], s_bn2, b, 2 * NT, -NT, 1 << 20)
                            for t in range(NT):
                                dve.bn_aggr(mv2[:, t, :], stat_tmp[:, t, :]).then_inc(s_bn2, 1)
                            wait(dve, s_bn2, b, 2 * NT, 0, 1 << 20)
                            dve.tensor_scalar(veps2[:], mv2[:, :, 1], EPS, None, ALU.add).then_inc(s_veps2, 1)
                            dve.tensor_copy(mean2[:, ds((b - 1) * NT, NT)], mv2[:, :, 0]).then_inc(s_mean2, 1)
                        if (g, s) == (2, 1) and exists(b - 1):
                            wait(dve, s_rstd2, b, 1, 0, NB)
                            wait(dve, s_n2ps, b, 1, -1, NB)
                            for t in range(NT):
                                last = dve.tensor_scalar(xn2[:, t, :], x_res[:, (b - 1) * NT + t, :],
                                                         mv2[:, t, 0:1],
                                                         rstd2[:, ds((b - 1) * NT + t, 1)], ALU.subtract, ALU.mult)
                            last.then_inc(s_xn2, 1)
                        if (g, s) == (3, 3) and exists(b - 1):
                            wait(dve, s_lgps, b, 1, 0, NB)
                            dve.tensor_copy(logits[:, ds((b - 1) * NT, NT), :],
                                            ps_m[0][:, 0:32 * NT].rearrange("p (t e) -> p t e", e=32)).then_inc(s_lg, 1)
                        if s == 3 and exists(ba):
                            wait(dve, s_max, ba, UNIT, UNITS * (ga + 1), UNITS * STEPS)
                            wait(dve, s_mps, ba, STEP4, ga - 1, STEPS)
                            pad = max_pad[:, ga % 2].rearrange("p t (h c) -> p t h c", c=SLOT)
                            dve.tensor_copy(pad[:, :, :, MAXROW_HI], neg_max[:, ga % 2]).then_inc(s_mcut, 1)
                            wait(dve, s_mcut, ba, 2 * STEP4, 2 * ga + 1, 2 * STEPS)
                            dve.tensor_tensor(pad[:, :, :, MAXROW_LO], neg_max[:, ga % 2],
                                              pad[:, :, :, MAXROW_HI].bitcast(F32), ALU.subtract).then_inc(s_mcut, 1)

            dve.memset(v_pk[:], 0.0).then_inc(s_set, 1)
            dve.memset(max_pad[:].bitcast(F32), 0.0).then_inc(s_set, 1)
            dve.memset(minus_half[:], -0.5).then_inc(s_set, 1)
            dve.wait_ge(s_set, 3)
            dve.memset(v_pk[:, :, :, ONES_COL:ONES_COL + 1], 1.0).then_inc(s_set, 1)
            dve.memset(zeros[:], 0.0).then_inc(s_set, 1)
            dve.wait_ge(s_stage, 16 * len(SPLIT_WEIGHTS))
            for n, (dst, (_, width)) in enumerate(zip((w_q, w_k, w_v), SPLIT_WEIGHTS)):
                staged = probs[:, 0, n, 0:width]
                flat = [dst[:, i].rearrange("p g c -> p (g c)") if width == 512 else dst[:, i] for i in range(2)]
                dve.tensor_copy(flat[0], staged).then_inc(s_split, 1)
                dve.wait_ge(s_split, 2 * n + 1)
                dve.tensor_tensor(flat[1], staged, flat[0].bitcast(F32), ALU.subtract).then_inc(s_split, 1)
            dve.wait_ge(s_w, 16 * 8)
            dve.tensor_copy(ident_r[:], ident[:]).then_inc(s_split, 1)
            dve.tensor_copy(ident_b[:], ident[:]).then_inc(s_split, 1)
            dve.tensor_copy(mask_b[:], mask[:]).then_inc(s_split, 1)
            dve.tensor_tensor(b_qk_lo[:], b_qk[:], lo_rows[:].unsqueeze(2).broadcast_to([P, 2, GROUPS]),
                              ALU.mult).then_inc(s_split, 1)
            dve.wait_ge(s_set, 4)
            body(-1)
            body(0)
            body(1)
            dve.wait_ge(s_xr, 16 * (NB - 3))
            with dve.Fori(2, NB - 1) as b:
                body(b)
            body(NB - 1)
            body(NB)

        @block.gpsimd
        def _(pool):
            def body(b):
                for g in range(GROUPS):
                    for s in range(NT):
                        if exists(b):
                            kb = NT - 1 - s
                            wait_first(pool, mem["own_pool"], s_exp, b, UNIT, UNITS * g + FIRST_UNIT[s + 1], UNITS * STEPS)
                            diag = probs[:, s % 2, :, kb * P:(kb + 1) * P]
                            pool.affine_select(out=diag, in_=diag, compare_op=ALU.is_ge, fill=0.0, base=0,
                                               pattern=[[0, GH], [-1, P]], channel_multiplier=1).then_inc(s_mask, 1)
                        if (g, s) == (0, 0) and exists(b + 1):
                            wait(pool, s_veps1, b, 1, 2, NB)
                            pool.tensor_tensor(rstd1[:], veps1[:], minus_half[:], ALU.pow).then_inc(s_rstd1, 1)
                        if (g, s) == (0, 3) and exists(b + 1):
                            wait(pool, s_xn, b, 1, 2, NB)
                            x_b = x_res[:, ds((b + 1) * NT, NT), :]
                            pool.tensor_tensor(x_b, x_b, b_o[:].unsqueeze(1).broadcast_to([P, NT, D]),
                                               ALU.add).then_inc(s_bo, 1)
                        if (g, s) == (2, 0) and exists(b - 1):
                            wait(pool, s_veps2, b, 1, 0, NB)
                            pool.tensor_tensor(rstd2[:, ds((b - 1) * NT, NT)], veps2[:], minus_half[:],
                                               ALU.pow).then_inc(s_rstd2, 1)

            pool.memset(k_z[:].bitcast(F32), 0.0).then_inc(s_kz_zero, 1)
            pool.wait_ge(s_set, 4)
            pool.wait_ge(s_w, 16 * 8)
            body(-1)
            body(0)
            body(1)
            with pool.Fori(2, NB - 1) as b:
                body(b)
            body(NB - 1)
            body(NB)




def routing(nc, mem, dram):
    logits, pos, score = mem["logits"], mem["pos"], mem["score"]
    w_qf, w_kf, w_vo = mem["w_qf"], mem["w_kf"], mem["w_vo"]
    with ExitStack() as ctx:
        def sb(name, shape, dt=F32):
            return ctx.enter_context(nc.sbuf_tensor(name, shape, dt))

        def sem(name):
            return ctx.enter_context(nc.semaphore(name))

        w_t, rf, w_out1 = mem["w_t"], mem["rf"], mem["w_out1"]
        iota_e, before = mem["iota_e"], mem["before"]
        before_b = sb("before_b", [P, P], BF16)
        ones_b = sb("ones_b", [P, P], BF16)
        top = sb("top", [P, TILES])
        first = sb("first", [P, TILES])
        wide = [sb(f"wide{i}", [P, TILES * E0]) for i in range(3)]
        chosen = sb("chosen", [P, TILES, E0], BF16)
        slots_f = sb("slots_f", [P, E0])
        slots_i = sb("slots_i", [P, E0], I32)
        slots_end = mem["slots_end"]
        base = sb("base", [P, E0])
        ones_e = sb("ones_e", [P, E0])
        pos_f = sb("pos_f", [P, TILES])
        ps = ctx.enter_context(nc.psum_tensor("ps_r", [P, 8, 512], F32))

        s_d = sem("s_d")
        s_f = sem("s_f")
        s_fa, s_fd = sem("s_fa"), sem("s_fd")
        s_chosen, s_rank, s_tot = sem("s_chosen"), sem("s_rank"), sem("s_tot")
        s_top, s_score = sem("s_top"), sem("s_score")
        block = ctx.enter_context(nc.Block())

        @block.tensor
        def _(pe):
            for bank in range(8):
                for c in range(4 if bank < 4 else 2):
                    if bank < 4:
                        pair = (bank % 2) * 4 + c
                        last = pe.matmul(ps[:, bank, P * c:P * (c + 1)], w_t[:, (bank // 2) * 8 + pair, :],
                                         rf[:, pair, :], start=True, stop=True)
                    else:
                        pair = (bank - 4) * 2 + c
                        last = pe.matmul(ps[:, bank, 2 * P * c:2 * P * (c + 1)], w_t[:, 16 + pair, :],
                                         w_out1[:, pair, :], start=True, stop=True)
                last.then_inc(s_f, 1)
            pe.wait_ge(s_fa, 8)
            pe.wait_ge(s_fd, 4)
            pe.wait_ge(s_chosen, 1)
            flat = chosen[:].rearrange("p t e -> p (t e)")
            for i in range(4):
                last = pe.matmul(ps[:, 4 + i, :], ones_b[:], flat[:, 512 * i:512 * (i + 1)], start=True, stop=True)
            last.then_inc(s_rank, 1)
            for i in range(4):
                last = pe.matmul(ps[:, i, :], before_b[:], flat[:, 512 * i:512 * (i + 1)], start=True, stop=True)
            last.then_inc(s_rank, 1)

        @block.scalar
        def _(act):
            act.wait_ge(s_top, 1)
            act.activation(score[:], top[:], ACT.Sigmoid).then_inc(s_score, 1)
            for bank in range(8):
                act.wait_ge(s_f, bank + 1)
                if bank < 4:
                    dst = (w_qf, w_kf)[bank // 2][:, 0, (bank % 2) * 512:(bank % 2) * 512 + 512]
                else:
                    dst = w_vo[:, 4 * (bank - 4):4 * (bank - 3), :].rearrange("p h d -> p (h d)")
                act.copy(dst, ps[:, bank, :]).then_inc(s_fa, 1)
            act.wait_ge(s_rank, 1)
            act.copy(wide[0][:].rearrange("p (e t) -> p t e", e=E0),
                     ps[:, 4:8, :].rearrange("p b (t e) -> p (b t) e", e=E0)).then_inc(s_tot, 1)

        @block.vector
        def _(dve):
            done = [0]

            def then(ins):
                done[0] += 1
                ins.then_inc(s_d, 1)
                dve.wait_ge(s_d, done[0])

            tile_e = [P, TILES, E0]
            by_tile = wide[0][:].rearrange("p (t e) -> p t e", e=E0)
            dve.tensor_reduce(top[:], logits[:], AX.X, ALU.max).then_inc(s_top, 1)
            dve.wait_ge(s_top, 1)
            then(dve.tensor_tensor(by_tile, logits[:], top[:].unsqueeze(2).broadcast_to(tile_e), ALU.is_equal))
            then(dve.scalar_tensor_tensor(by_tile, by_tile, -64.0, iota_e[:].unsqueeze(1).broadcast_to(tile_e),
                                          ALU.mult, ALU.add))
            then(dve.tensor_reduce(first[:], by_tile, AX.X, ALU.min))
            then(dve.tensor_scalar(first[:], first[:], 64.0, None, ALU.add))
            then(dve.memset(ones_b[:], 1.0))
            then(dve.tensor_copy(before_b[:], before[:]))
            dve.tensor_tensor(chosen[:], iota_e[:].unsqueeze(1).broadcast_to(tile_e),
                              first[:].unsqueeze(2).broadcast_to(tile_e), ALU.is_equal).then_inc(s_chosen, 1)
            for bank in range(4):
                dst = (w_qf, w_kf)[bank // 2][:, :, (bank % 2) * 512:(bank % 2) * 512 + 512]
                dve.wait_ge(s_fa, bank + 1)
                dve.tensor_tensor(dst[:, 1], ps[:, bank, :], dst[:, 0].bitcast(F32), ALU.subtract).then_inc(s_fd, 1)
            keep = wide[1][:].rearrange("p (e t) -> p e t", e=E0)
            then(dve.memset(ones_e[:], 1.0))
            then(dve.memset(keep, 1.0))
            then(dve.memset(keep[:, :, 0:1], 0.0))
            dve.wait_ge(s_tot, 1)
            then(dve.tensor_tensor_scan(wide[2][:], wide[1][:], wide[0][:], 0.0, ALU.mult, ALU.add))
            upto = wide[2][:].rearrange("p (e t) -> p e t", e=E0)
            then(dve.tensor_scalar(slots_f[:], upto[:, :, TILES - 1], float(P - 1), None, ALU.add))
            then(dve.tensor_copy(slots_i[:], slots_f[:]))
            then(dve.tensor_scalar(slots_i[:], slots_i[:], 7, None, ALU.arith_shift_right))
            then(dve.tensor_copy(slots_f[:], slots_i[:]))
            then(dve.tensor_tensor_scan(slots_end[:], ones_e[:], slots_f[:], 0.0, ALU.mult, ALU.add))
            then(dve.tensor_tensor(base[:], slots_end[:], slots_f[:], ALU.subtract))
            then(dve.tensor_scalar(base[:], base[:], float(P), None, ALU.mult))
            then(dve.tensor_tensor(wide[2][:], wide[2][:], wide[0][:], ALU.subtract))
            then(dve.tensor_tensor(upto, upto, base[:].unsqueeze(2).broadcast_to([P, E0, TILES]), ALU.add))
            dve.wait_ge(s_rank, 2)
            then(dve.tensor_tensor(by_tile, ps[:, 0:4, :].rearrange("p b (t e) -> p (b t) e", e=E0),
                                   wide[2][:].rearrange("p (e t) -> p t e", e=E0), ALU.add))
            then(dve.tensor_tensor(by_tile, by_tile, chosen[:], ALU.mult))
            then(dve.tensor_reduce(pos_f[:], by_tile, AX.X, ALU.add))
            then(dve.tensor_copy(pos[:], pos_f[:]))


def layer0_experts(nc, mem, dram, x_sorted, y_sorted):
    x_res, mean2, rstd2, pos, score = mem["x_res"], mem["mean2"], mem["rstd2"], mem["pos"], mem["score"]
    ident, slot_expert = mem["ident"], mem["slot_expert"]
    slots_end, iota_q = mem["slots_end"], mem["iota_q"]
    with ExitStack() as ctx:
        def sb(name, shape, dt=F32):
            return ctx.enter_context(nc.sbuf_tensor(name, shape, dt))

        def pb(name, shape, dt=F32):
            return ctx.enter_context(nc.psum_tensor(name, shape, dt))

        def sem(name):
            return ctx.enter_context(nc.semaphore(name))

        w_gu = sb("w_gu", [P, E0, 2 * MID0])
        w_dn = sb("w_dn", [P, E0, 2, D])
        stage, w_sd = mem["w_sh_stage"], mem["w_sd"]
        w_sh = sb("w_sh", [P, 2, 2 * MID0], F32R)

        xn2 = sb("xn2_s", [P, NT, D])
        x_go = sb("x_go", [P, 2, NT, D])
        pos_go = sb("pos_go", [P, 2, NT], I32)
        xt_hi = sb("xt_hi_s", [P, SEQ], F32R)
        xt_lo = sb("xt_lo_s", [P, SEQ], F32R)
        sg_s = sb("sg_s", [P, 2, SEQ])
        h_s = sb("h_s", [P, 2, 2, SEQ])

        passes = sb("passes", [P, SLOTS // 2, E0])
        passed = sb("passed", [P, SLOTS])
        x_in = sb("x_in", [P, 2, 4, D])
        y_go = sb("y_go", [P, 2, 4, D])
        x_t = sb("x_t", [P, 2, P])
        sg = sb("sg", [P, 2, MID0])
        h = sb("h", [P, 2, MID0])
        h_t = sb("h_t", [P, 2, MID0])

        s_split = sem("s_split2")
        s_slot = sem("s_slot")
        s_wgu, s_wdn = sem("s_wgu"), sem("s_wdn")
        s_xn, s_xgo, s_pgo = sem("s_xn_s"), sem("s_xgo"), sem("s_pgo")
        s_tab = mem["own_act"]
        s_sent = [sem("s_sent0"), sem("s_sent1")]
        s_t, s_xh, s_xl = sem("s_t_s"), sem("s_xh_s"), sem("s_xl_s")
        s_gu, s_silu, s_h, s_dn, s_res = sem("s_gu_s"), sem("s_silu_s"), sem("s_h_s"), sem("s_dn_s"), sem("s_res")
        e_in = [sem("e_in0"), sem("e_in1")]
        e_out = [sem("e_out0"), sem("e_out1")]
        e_t, e_xt, e_gu, e_silu, e_h = sem("e_t"), sem("e_xt"), sem("e_gu"), sem("e_silu"), sem("e_h")
        e_hps, e_ht, e_dn, e_y = sem("e_hps"), sem("e_ht"), sem("e_dn"), sem("e_y")
        N8 = SLOTS // 8

        ps = [pb(f"ps_e{i}", [P, 512]) for i in range(8)]
        block = ctx.enter_context(nc.Block())

        def live(b, total=NB):
            return not isinstance(b, int) or 0 <= b < total

        def over_batches(eng, body):
            body(-1, 1)
            body(0, 0)
            body(0, 1)
            with eng.Fori(1, NB // 2 - 1) as i:
                body(i, 0)
                body(i, 1)
            body(NB // 2 - 1, 0)
            body(NB // 2 - 1, 1)
            body(NB // 2, 0)

        def over_slots(eng, body):
            for c in (6, 7):
                body(-1, c)
            for c in range(8):
                body(0, c)
            with eng.Fori(1, N8 - 1) as i:
                for c in range(8):
                    body(i, c)
            for c in range(8):
                body(N8 - 1, c)
            for c in (0, 1):
                body(N8, c)

        def slot_live(i, c):
            return not isinstance(i, int) or 0 <= 8 * i + c < SLOTS

        @block.sync
        def _(sp):
            def weights(i, par):
                b = 2 * i + par
                if live(b):
                    wait(sp, s_gu, b, 4, 1, 4 * NB)
                    e = ds(b * (E0 // NB), E0 // NB)
                    sp.dma_start(w_gu[:, e, 0:MID0], dram["w_gate0"][:, e, :]).then_inc(s_wgu, 16)
                    sp.dma_start(w_gu[:, e, MID0:2 * MID0], dram["w_up0"][:, e, :]).then_inc(s_wgu, 16)
                    sp.dma_start(w_dn[:, e], dram["w_down0"][:, e]).then_inc(s_wdn, 16)

            over_batches(sp, weights)
            x_dram = x_sorted.rearrange("(q t p) d -> q p t d", p=P, t=4)
            y_dram = y_sorted.rearrange("(q t p) d -> q p t d", p=P, t=4)
            for par in range(2):
                sp.wait_ge(s_sent[par], 16 * NT * NB // 2)

            def load(i, c):
                q, half = (2 * i + c // 4), c // 4
                wait(sp, e_t, i, 8, 4 * half - 4, SLOTS)
                sp.dma_start(x_in[:, half], x_dram[q]).then_inc(e_in[half], 16)

            def store(i, half):
                wait(sp, e_y, i, 8, 4 * half + 4, SLOTS)
                sp.dma_start(y_dram[2 * i + half], y_go[:, half]).then_inc(e_out[half], 16)

            load(0, 0)
            load(0, 4)
            load(1, 0)
            store(0, 0)
            load(1, 4)
            store(0, 1)
            with sp.Fori(1, N8 - 1) as i:
                load(i + 1, 0)
                store(i, 0)
                load(i + 1, 4)
                store(i, 1)
            store(N8 - 1, 0)
            store(N8 - 1, 1)
            for half in range(2):
                sp.wait_ge(e_out[half], 16 * N8)

        @block.tensor
        def _(pe):
            def shared(i, par):
                b = 2 * i + par
                if live(b):
                    wait(pe, s_xl, b, 1, 1, NB)
                    for m in range(4):
                        if m < 2:
                            wait(pe, s_silu, b, 2, m - 1, 2 * NB)
                        else:
                            wait(pe, s_h, b, 2, m - 3, 2 * NB)
                        for n, (a, c) in enumerate(((0, xt_hi), (1, xt_hi), (0, xt_lo))):
                            last = pe.matmul(ps[m][:], w_sh[:, a, P * m:P * (m + 1)], c[:], start=(n == 0), stop=(n == 2))
                        last.then_inc(s_gu, 1)
                if live(b + 1):
                    wait(pe, s_xn, b, 1, 2, NB)
                    wait(pe, s_xl, b, 1, 1, NB)
                    for t in range(NT):
                        last = pe.transpose(ps[4][:, P * t:P * (t + 1)], xn2[:, t, :], ident[:])
                    last.then_inc(s_t, 1)
                if live(b - 1):
                    wait(pe, s_h, b, 2, 0, 2 * NB)
                    wait(pe, s_res, b, 1, -1, NB)
                    for t in range(NT):
                        for k in range(2):
                            last = pe.matmul(ps[5][:, P * t:P * (t + 1)], h_s[:, 1 - par, k, P * t:P * (t + 1)],
                                             w_sd[:, k, :], start=(k == 0), stop=(k == 1))
                    last.then_inc(s_dn, 1)

            pe.wait_ge(s_split, 2)
            over_batches(pe, shared)

            pe.wait_ge(s_slot, 8)
            expert = {}

            def routed(i, c):
                if c == 0:
                    expert.clear()
                for tile in (c - 2, c + 1):
                    if slot_live(i, tile) and tile not in expert:
                        expert[tile] = pe.value_load(slot_expert[0:1, ds(8 * i + tile, 1)], min_val=0,
                                                        max_val=E0 - 1)
                if slot_live(i, c + 2):
                    half, t = (c + 2) // 4 % 2, (c + 2) % 4
                    wait(pe, e_in[half], i, 16, 16 * ((c + 2) // 8 + 1), 16 * N8)
                    wait(pe, e_xt, i, 8, c + 1, SLOTS)
                    pe.transpose(ps[c % 2][:, 0:P], x_in[:, half, t, :], ident[:]).then_inc(e_t, 1)
                if slot_live(i, c - 2):
                    wait(pe, e_ht, i, 8, c - 1, SLOTS)
                    wait(pe, e_y, i, 8, c - 3, SLOTS)
                    for k in range(2):
                        last = pe.matmul(ps[6 + c % 2][:, 0:P], h_t[:, c % 2, P * k:P * (k + 1)],
                                         w_dn[:, ds(expert[c - 2], 1), k, :], start=(k == 0), stop=(k == 1))
                    last.then_inc(e_dn, 1)
                if slot_live(i, c - 1):
                    wait(pe, e_h, i, 8, c, SLOTS)
                    wait(pe, e_ht, i, 8, c - 2, SLOTS)
                    for k in range(2):
                        last = pe.transpose(ps[4 + (c - 1) % 2][:, P * k:P * (k + 1)],
                                            h[:, (c - 1) % 2, P * k:P * (k + 1)], ident[:])
                    last.then_inc(e_hps, 1)
                if slot_live(i, c + 1):
                    wait(pe, e_h, i, 8, c, SLOTS)
                    wait(pe, e_xt, i, 8, c + 2, SLOTS)
                    pe.matmul(ps[2 + (c + 1) % 2][:], x_t[:, (c + 1) % 2, :], w_gu[:, ds(expert[c + 1], 1), :],
                              start=True, stop=True).then_inc(e_gu, 1)

            pe.wait_ge(s_wgu, 16 * 2 * NB)
            pe.wait_ge(s_wdn, 16 * NB)
            pe.wait_ge(s_res, NB)
            pe.wait_ge(s_silu, 2 * NB)
            pe.wait_ge(s_h, 2 * NB)
            over_slots(pe, routed)

        @block.scalar
        def _(act):
            def shared(i, par):
                b = 2 * i + par
                if live(b):
                    for m in range(2):
                        wait(act, s_gu, b, 4, m + 1, 4 * NB)
                        wait(act, s_h, b, 2, m - 1, 2 * NB)
                        act.activation(sg_s[:, m, :], ps[m][:], ACT.Silu).then_inc(s_silu, 1)
                if live(b + 1):
                    wait(act, s_t, b, 1, 2, NB)
                    act.copy(xt_hi[:], ps[4][:]).then_inc(s_xh, 1)

            def routed(i, c):
                if slot_live(i, c - 1):
                    wait(act, e_hps, i, 8, c, SLOTS)
                    wait(act, e_dn, i, 8, c - 2, SLOTS)
                    act.copy(h_t[:, (c - 1) % 2, :], ps[4 + (c - 1) % 2][:, 0:MID0]).then_inc(e_ht, 1)
                if slot_live(i, c + 1):
                    wait(act, e_gu, i, 8, c + 2, SLOTS)
                    wait(act, e_h, i, 8, c, SLOTS)
                    act.activation(sg[:, (c + 1) % 2, :], ps[2 + (c + 1) % 2][:, 0:MID0],
                                   ACT.Silu).then_inc(e_silu, 1)

            act.activation(sg[:, 0, 0:1], stage[:, 0:1], ACT.Silu).then_inc(s_tab, 1)
            over_batches(act, shared)
            over_slots(act, routed)

        @block.vector
        def _(dve):
            def tile_experts(half):
                q = slice(half * SLOTS // 2, (half + 1) * SLOTS // 2)
                wide = [P, SLOTS // 2, E0]
                if half:
                    dve.wait_ge(s_slot, 4)
                dve.tensor_tensor(passes[:], slots_end[:].unsqueeze(1).broadcast_to(wide),
                                  iota_q[:, q].unsqueeze(2).broadcast_to(wide), ALU.is_le).then_inc(s_slot, 1)
                dve.wait_ge(s_slot, 4 * half + 1)
                dve.tensor_reduce(passed[:, q], passes[:], AX.X, ALU.add).then_inc(s_slot, 1)
                dve.wait_ge(s_slot, 4 * half + 2)
                dve.tensor_scalar(passed[:, q], passed[:, q], float(E0 - 1), None, ALU.min).then_inc(s_slot, 1)
                dve.wait_ge(s_slot, 4 * half + 3)
                dve.tensor_copy(slot_expert[:, q], passed[:, q]).then_inc(s_slot, 1)

            def prepare(i, par):
                b = 2 * i + par
                if isinstance(b, int) and b >= NB:
                    return
                wait(dve, s_t, b, 1, 0, NB)
                wait(dve, s_xgo, b, 1, 0, NB)
                for t in range(NT):
                    last = dve.tensor_scalar(xn2[:, t, :], x_res[:, b * NT + t, :], mean2[:, ds(b * NT + t, 1)],
                                             rstd2[:, ds(b * NT + t, 1)], ALU.subtract, ALU.mult)
                last.then_inc(s_xn, 1)
                wait(dve, s_xn, b, 1, 1, NB)
                wait(dve, s_sent[par], i, 16 * NT, 0, 16 * NT * NB // 2)
                dve.tensor_copy(pos_go[:, par, :], pos[:, ds(b * NT, NT)]).then_inc(s_pgo, 1)
                for t in range(NT):
                    last = dve.tensor_scalar(x_go[:, par, t, :], xn2[:, t, :], score[:, ds(b * NT + t, 1)], None,
                                             ALU.mult)
                last.then_inc(s_xgo, 1)

            def low_half(b):
                if live(b):
                    wait(dve, s_xh, b, 1, 1, NB)
                    dve.tensor_tensor(xt_lo[:], ps[4][:], xt_hi[:].bitcast(F32), ALU.subtract).then_inc(s_xl, 1)

            def shared(i, par):
                b = 2 * i + par
                if live(b):
                    for m in range(2):
                        wait(dve, s_silu, b, 2, m + 1, 2 * NB)
                        wait(dve, s_gu, b, 4, m + 3, 4 * NB)
                        dve.tensor_tensor(h_s[:, par, m, :], ps[2 + m][:], sg_s[:, m, :], ALU.mult).then_inc(s_h, 1)
                        if m == 0:
                            low_half(b + 1)
                else:
                    low_half(b + 1)
                if live(b - 1):
                    wait(dve, s_dn, b, 1, 0, NB)
                    x_b = x_res[:, ds((b - 1) * NT, NT), :]
                    dve.tensor_tensor(x_b, ps[5][:].rearrange("p (t d) -> p t d", t=NT), x_b,
                                      ALU.add).then_inc(s_res, 1)
                if live(b + 2):
                    prepare(i + 1, par)
                if isinstance(b, int) and 0 <= b < 2:
                    tile_experts(b)

            def routed(i, c):
                if slot_live(i, c + 2):
                    wait(dve, e_t, i, 8, c + 3, SLOTS)
                    wait(dve, e_gu, i, 8, c + 1, SLOTS)
                    dve.tensor_copy(x_t[:, c % 2, :], ps[c % 2][:, 0:P]).then_inc(e_xt, 1)
                if slot_live(i, c - 2):
                    wait(dve, e_dn, i, 8, c - 1, SLOTS)
                    half = (c - 2) // 4 % 2
                    if (c - 2) % 4 == 0:
                        wait(dve, e_out[half], i, 16, 16 * ((c - 2) // 8), 16 * N8)
                    dve.tensor_copy(y_go[:, half, (c - 2) % 4, :], ps[6 + c % 2][:, 0:P]).then_inc(e_y, 1)
                if slot_live(i, c + 1):
                    wait(dve, e_silu, i, 8, c + 2, SLOTS)
                    wait(dve, e_hps, i, 8, c, SLOTS)
                    dve.tensor_tensor(h[:, (c + 1) % 2, :], ps[2 + (c + 1) % 2][:, MID0:2 * MID0],
                                      sg[:, (c + 1) % 2, :], ALU.mult).then_inc(e_h, 1)

            dve.tensor_copy(w_sh[:, 0, :], stage[:]).then_inc(s_split, 1)
            dve.wait_ge(s_split, 1)
            dve.tensor_tensor(w_sh[:, 1, :], stage[:], w_sh[:, 0, :].bitcast(F32), ALU.subtract).then_inc(s_split, 1)
            prepare(0, 0)
            over_batches(dve, shared)
            over_slots(dve, routed)

        @block.gpsimd
        def _(pool):
            def send(i, par):
                b = 2 * i + par
                if not live(b):
                    return
                wait_first(pool, mem["own_pool"], s_xgo, b, 1, 1, NB)
                for t in range(NT):
                    pool.indirect_dma_start(x_sorted[:, :],
                                            bass.IndirectOffsetOnAxis(ap=pos_go[:, par, t:t + 1], axis=0),
                                            x_go[:, par, t, :], None).then_inc(s_sent[par], 16)

            over_batches(pool, send)


MID1, E1, FFN_TILES = 32, 16, 5
PAIRS = H1 // 2
LOG_ROWS = 32
COMB_STEPS = 20
RING = ([("phi_k", n) for n in range(8)] + [("phi_q", n) for n in range(4)] + [("x4t", 0)]
        + [("phi_q", n) for n in range(4, 8)]
        + [("gate", 0), ("up", 0)]
        + [("gate", 1), ("gate", 2), ("comb", 1), ("up", 1), ("comb", 2), ("up", 2)]
        + [("kvw", n) for n in range(4)]
        + [("gate", 3), ("gate", 4), ("comb", 3), ("up", 3), ("comb", 4), ("up", 4)]
        + [("inv", n) for n in range(8)] + [("x3t", 0)])
RING_BANKS = 4
QN_SLOTS = 4
LOW_BEFORE = {4: 1, 6: 3}


def layer1(nc, mem, dram, y_sorted, out):
    x_res, pos, ident, ident_r = mem["x_res"], mem["pos"], mem["ident"], mem["ident_r"]
    w_qf, w_kf, w_vo = mem["w_qf"], mem["w_kf"], mem["w_vo"]
    with ExitStack() as ctx:
        def sb(name, shape, dt=F32):
            return ctx.enter_context(nc.sbuf_tensor(name, shape, dt))

        def sem(name):
            return ctx.enter_context(nc.semaphore(name))

        stage = sb("stage1", [P, 2, FFN_TILES * P])
        spread_stage = sb("spread_stage", [P, PAIRS + FFN_TILES - 1, P])
        w_gate = sb("w_gate1", [P, 2, FFN_TILES * P], F32R)
        w_up = sb("w_up1", [P, 2, FFN_TILES * P], F32R)
        w_down = sb("w_down1", [P, FFN_TILES, D])
        w_rt_stage = sb("w_rt_stage", [P, E1])
        w_rt = sb("w_rt", [P, 2, E1], F32R)
        b_o = sb("b_o1s", [P, D])
        spread = sb("spread", [P, PAIRS, P], F32R)
        spread_e = sb("spread_e", [P, FFN_TILES - 1, P], F32R)
        low = sb("low", [P, 1])
        own_head = sb("own_head", [P, PAIRS, 8])
        iota = sb("iota1", [P, NT, E1])
        iota64 = sb("iota64", [P, NT, E1])
        minus_half = sb("minus_half1", [P, NT])

        pos_y = sb("pos_y", [P, NT], I32)
        y = sb("y", [P, NT, D])
        stat3, stat4 = sb("stat3", [P, NT, 6]), sb("stat4", [P, NT, 6])
        mv3, mv4 = sb("mv3", [P, NT, 2]), sb("mv4", [P, NT, 2])
        veps3, veps4 = sb("veps3", [P, NT]), sb("veps4", [P, NT])
        rstd3, rstd4 = sb("rstd3", [P, NT]), sb("rstd4", [P, NT])
        xn3 = sb("xn3", [P, NT, D + 2])
        x3_hi, x3_lo = sb("x3_hi", [P, SEQ], F32R), sb("x3_lo", [P, SEQ], F32R)
        phi_k = sb("phi_k", [P, NT, H1 * HD1])
        phi_q = sb("phi_q", [P, PAIRS, SEQ])
        g_sb = sb("g_sb", [P, PAIRS, D + 2])
        gt_sb = sb("gt_sb", [P, PAIRS, P])
        kvw = sb("kvw", [P, PAIRS, D])
        kvw_hi, kvw_lo = sb("kvw_hi", [P, PAIRS, D], F32R), sb("kvw_lo", [P, PAIRS, D], F32R)
        qn_hi = sb("qn_hi", [P, QN_SLOTS, SEQ], F32R)
        qn_lo = sb("qn_lo", [P, QN_SLOTS, SEQ], F32R)
        attn_t = sb("attn_t1", [P, SEQ])
        ksum = sb("ksum", [P, PAIRS, LOG_ROWS])
        norm = sb("norm", [P, SEQ])
        inv = sb("inv", [P, SEQ])
        inv_half = sb("inv_half", [P, SEQ], F32R)
        inv_pk = sb("inv_pk", [P, SEQ], F32R)
        xn4 = sb("xn4", [P, NT, D])
        x4_hi, x4_lo = sb("x4_hi", [P, SEQ], F32R), sb("x4_lo", [P, SEQ], F32R)
        t_e = [P, NT, E1]
        top = [sb(f"top{i}", [P, NT]) for i in range(2)]
        first = [sb(f"first{i}", [P, NT]) for i in range(2)]
        hot = [sb(f"hot{i}", t_e) for i in range(2)]
        cand, dif, dif2, expo, w12 = (sb(n, t_e) for n in ("cand", "dif", "dif2", "expo", "w12"))
        s12, z, den = sb("s12", [P, NT]), sb("z", [P, NT]), sb("den", [P, NT])
        comb = sb("comb", [P, NT, P], F32R)
        comb_t = sb("comb_t", [P, SEQ], F32R)
        silu = sb("silu", [P, 2, SEQ])
        h = sb("h1", [P, FFN_TILES, SEQ])

        ps = ctx.enter_context(nc.psum_tensor("ps1", [P, 8, 512], F32))
        G_BANKS, PER_BANK = 3, 3
        OUT, DOWN, NORM, ROUTE = 4, 5, 6, 7

        s_tab = mem["own_act"]
        s_w, s_wb, s_split, s_set = sem("c_w"), sem("c_wb"), sem("c_split"), sem("c_set")
        s_posy, s_y, s_x3, s_bn3, s_ve3, s_rstd3, s_xn3, s_bo = map(
            sem, ("c_posy", "c_y", "c_x3", "c_bn3", "c_ve3", "c_rstd3", "c_xn3", "c_bo"))
        s_x3t, s_x3h, s_x3l = sem("c_x3t"), sem("c_x3h"), sem("c_x3l")
        s_kps, s_k, s_qps, s_q = sem("c_kps"), sem("c_k"), sem("c_qps"), sem("c_q")
        s_g, s_gsb, s_gt, s_gtsb = sem("c_g"), sem("c_gsb"), sem("c_gt"), sem("c_gtsb")
        s_kv, s_kva = sem("c_kv"), sem("c_kva")
        s_ksum, s_n, s_norm, s_inv, s_ihalf, s_ipk = map(
            sem, ("c_ksum", "c_n", "c_norm", "c_inv", "c_ihalf", "c_ipk"))
        s_bc, s_qn, s_ao, s_x4 = sem("c_bc"), sem("c_qn"), sem("c_ao"), sem("c_x4")
        s_kvh, s_kvl, s_qh = sem("c_kvh"), sem("c_kvl"), sem("c_qh")
        s_ql = [sem("c_ql0"), sem("c_ql1")]
        s_at, s_att = sem("c_at"), sem("c_att")
        s_bn4, s_ve4, s_rstd4, s_xn4 = sem("c_bn4"), sem("c_ve4"), sem("c_rstd4"), sem("c_xn4")
        s_x4t, s_x4h, s_x4l = sem("c_x4t"), sem("c_x4h"), sem("c_x4l")
        s_lg, s_dif, s_expo, s_comb, s_cps, s_ct = map(
            sem, ("c_lg", "c_dif", "c_expo", "c_comb", "c_cps", "c_ct"))
        s_gate, s_up, s_cb = sem("c_gate"), sem("c_up"), sem("c_cb")
        s_silu, s_h, s_hc = sem("c_silu"), sem("c_h"), sem("c_hc")
        s_dn, s_xo, s_out = sem("c_dn"), sem("c_xo"), sem("c_out")

        READERS = {"phi_k": ((s_k,), 8, 0, 0), "phi_q": ((s_q,), 8, 0, 0), "kvw": ((s_kva,), 8, 0, 0),
                   "inv": ((s_qn,), 8, 0, 0), "x3t": ((s_x3l,), 1, 0, -1), "x4t": ((s_x4l,), 1, 0, 1),
                   "gate": ((s_silu,), FFN_TILES, 0, 1), "up": ((s_h,), FFN_TILES, 0, 1),
                   "comb": ((s_hc,), FFN_TILES - 1, 1, 1)}
        W_ALL = 16 * 10

        def ring_bank(kind, n):
            return RING.index((kind, n)) % RING_BANKS

        def take_bank(pe, b, kind, n):
            at = RING.index((kind, n)) - RING_BANKS
            while True:
                turn, (kind0, n0) = b + at // len(RING), RING[at % len(RING)]
                sems, per, low_n, lag = READERS[kind0]
                if isinstance(b, int) and turn < -1:
                    break
                if exists(turn - lag):
                    for s in sems:
                        reads = 2 if kind0 == "kvw" else 1
                        wait(pe, s, turn - lag, per, reads * (n0 - low_n + 1), per * NB)
                    break
                at -= RING_BANKS
            return ps[:, ring_bank(kind, n), :]

        def turns(eng, body, weights=lambda: None):
            body(-1)
            weights()
            body(0)
            body(1)
            with eng.Fori(2, NB - 1) as b:
                body(b)
            body(NB - 1)
            body(NB)

        def low_half(eng, b, j):
            wait(eng, s_qh, b, 8, j + 1, 8 * NB)
            wait(eng, s_ao, b, 8, j + 1 - QN_SLOTS, 8 * NB)
            eng.tensor_tensor(qn_lo[:, j % QN_SLOTS, :], phi_q[:, j, :], qn_hi[:, j % QN_SLOTS, :].bitcast(F32),
                              ALU.subtract).then_inc(s_ql[j % 2], 1)

        block = ctx.enter_context(nc.Block())

        @block.sync
        def _(sp):
            sp.dma_start(b_o[:], dram["b_o1"]).then_inc(s_wb, 16)
            for dst, name in ((stage[:, 0], "w_gate1"), (stage[:, 1], "w_up1"), (w_rt_stage[:], "router1"),
                              (w_down[:], "w_down1"), (spread_stage[:, 0:PAIRS], "spread"),
                              (spread_stage[:, PAIRS:], "spread_e"), (low[:], "low"), (iota[:], "iota1"),
                              (own_head[:], "own_head"),
                              (iota64[:], "iota64")):
                sp.dma_start(dst, dram[name]).then_inc(s_w, 16)
            out_dram = out.rearrange("(b t p) d -> b p t d", p=P, t=NT)

            def body(b):
                f = b - 1
                if exists(f):
                    wait(sp, s_xo, f, 1, 1, NB)
                    sp.dma_start(out_dram[f], x_res[:, ds(f * NT, NT), :]).then_inc(s_out, 16)

            turns(sp, body)
            sp.wait_ge(s_out, 16 * NB)

        @block.tensor
        def _(pe):
            def three_passes(to, a, c):
                pe.matmul(to, a[0], c[0], start=True, stop=False)
                pe.matmul(to, a[1], c[0], start=False, stop=False)
                return pe.matmul(to, a[0], c[1], start=False, stop=True)

            def tile(t):
                return slice(t * P, (t + 1) * P)

            def gate_or_up(b, kind, i):
                w, done = {"gate": (w_gate, s_gate), "up": (w_up, s_up)}[kind]
                cols = slice(i * P, (i + 1) * P)
                bank = take_bank(pe, b, kind, i)
                three_passes(bank, (w[:, 0, cols], w[:, 1, cols]), (x4_hi[:], x4_lo[:])).then_inc(done, 1)

            def expert_tiles(b, tiles):
                f = b - 1
                if not exists(f):
                    return
                for i in tiles:
                    gate_or_up(b, "gate", i)
                for i in tiles:
                    if i:
                        bank = take_bank(pe, b, "comb", i)
                        wait(pe, s_ct, f, 1, 1, NB)
                        pe.matmul(bank, spread_e[:, i - 1, :], comb_t[:], start=True, stop=True).then_inc(s_cb, 1)
                    gate_or_up(b, "up", i)

            def phi_k_tile(b, n):
                bank = take_bank(pe, b, "phi_k", n)
                t, cols = n // 2, slice(n % 2 * 512, (n % 2 + 1) * 512)
                three_passes(bank, (x3_hi[:, tile(t)], x3_lo[:, tile(t)]),
                             (w_kf[:, 0, cols], w_kf[:, 1, cols])).then_inc(s_kps, 1)

            def phi_q_tile(b, j):
                bank = take_bank(pe, b, "phi_q", j)
                cols = slice(j * P, (j + 1) * P)
                three_passes(bank, (w_qf[:, 0, cols], w_qf[:, 1, cols]), (x3_hi[:], x3_lo[:])).then_inc(s_qps, 1)

            def body(b):
                f = b - 1
                if exists(b):
                    wait(pe, s_x3l, b, 1, 1, NB)
                    for n in range(2):
                        phi_k_tile(b, n)
                if exists(f):
                    wait(pe, s_at, f, 1, 1, NB)
                    for t in range(NT):
                        last = pe.transpose(ps[:, OUT, tile(t)], attn_t[:, tile(t)], ident[:])
                    last.then_inc(s_att, 1)
                if exists(b):
                    for n in range(2, 8):
                        phi_k_tile(b, n)
                if exists(b):
                    for j in range(4):
                        phi_q_tile(b, j)
                if exists(f):
                    bank = take_bank(pe, b, "x4t", 0)
                    wait(pe, s_xn4, f, 1, 1, NB)
                    for t in range(NT):
                        last = pe.transpose(bank[:, tile(t)], xn4[:, t, :], ident[:])
                    last.then_inc(s_x4t, 1)
                if exists(b):
                    for j in range(4, 8):
                        phi_q_tile(b, j)
                if exists(f):
                    wait(pe, s_x4l, f, 1, 1, NB)
                    wait(pe, s_ct, f, 1, 0, NB)
                    for t in range(NT):
                        last = three_passes(ps[:, ROUTE, E1 * t:E1 * (t + 1)], (x4_hi[:, tile(t)], x4_lo[:, tile(t)]),
                                            (w_rt[:, 0], w_rt[:, 1]))
                    last.then_inc(s_lg, 1)
                if exists(b):
                    wait(pe, s_k, b, 8, 8, 8 * NB)
                    for i in range(G_BANKS):
                        if i == 0:
                            wait(pe, s_x4, b, 1, 0, NB)
                        elif i == 1:
                            wait(pe, s_xo, b, 1, -1, NB)
                        else:
                            wait(pe, s_norm, b, 1, 0, NB)
                        for j in range(i * PER_BANK, min((i + 1) * PER_BANK, PAIRS)):
                            c = (j - i * PER_BANK) * (D + 2)
                            for t in range(NT):
                                last = pe.matmul(ps[:, OUT + i, c:c + D + 2], phi_k[:, t, tile(j)], xn3[:, t, :],
                                                 start=(t == 0), stop=(t == NT - 1))
                        last.then_inc(s_g, 1)
                if exists(f):
                    wait(pe, s_comb, f, COMB_STEPS, COMB_STEPS, COMB_STEPS * NB)
                    for t in range(NT):
                        last = pe.matmul(ps[:, ROUTE, tile(t)], comb[:, t, :], ident_r[:], start=True, stop=True)
                    last.then_inc(s_cps, 1)
                expert_tiles(b, (0,))
                if exists(b):
                    wait(pe, s_gsb, b, G_BANKS, G_BANKS, G_BANKS * NB)
                    for i in range(2):
                        for j in range(4):
                            last = pe.transpose(ps[:, OUT + i, tile(j)], g_sb[:, 4 * i + j, 0:D], ident[:])
                        last.then_inc(s_gt, 1)
                expert_tiles(b, (1, 2))
                if exists(b):
                    wait(pe, s_ksum, b, 1, 1, NB)
                    wait(pe, s_q, b, 8, 8, 8 * NB)
                    for j in range(PAIRS):
                        rows = slice(LOG_ROWS * (j % 4), LOG_ROWS * (j % 4 + 1))
                        last = pe.matmul(ps[rows, NORM, :], ksum[:, j, :], phi_q[:, j, :], start=(j < 4),
                                         stop=(j >= 4), skip_group_check=True)
                    last.then_inc(s_n, 1)
                if exists(b):
                    wait(pe, s_gtsb, b, 2, 2, 2 * NB)
                    for n in range(4):
                        bank = take_bank(pe, b, "kvw", n)
                        for c in range(2):
                            j = 2 * n + c
                            last = pe.matmul(bank[:, 2 * D * c:2 * D * (c + 1)], gt_sb[:, j, :],
                                             w_vo[:, 2 * j:2 * j + 2, :], start=True, stop=True)
                        last.then_inc(s_kv, 1)
                expert_tiles(b, (3, 4))
                for part in range(2):
                    if exists(b):
                        if part == 0:
                            if isinstance(b, int) and b == 0:
                                pe.wait_ge(s_w, W_ALL)
                                pe.wait_ge(s_split, 8)
                            wait(pe, s_ipk, b, 1, 1, NB)
                        for j in range(4 * part, 4 * part + 4):
                            bank = take_bank(pe, b, "inv", j)
                            pe.matmul(bank, spread[:, j, :], inv_pk[:], start=True, stop=True).then_inc(s_bc, 1)
                    if exists(f):
                        if part == 0:
                            wait(pe, s_h, f, FFN_TILES, FFN_TILES, FFN_TILES * NB)
                        for t in (2 * part, 2 * part + 1):
                            for i in range(FFN_TILES):
                                last = pe.matmul(ps[:, DOWN, tile(t)], h[:, i, tile(t)], w_down[:, i, :],
                                                 start=(i == 0), stop=(i == FFN_TILES - 1))
                        if part == 1:
                            last.then_inc(s_dn, 1)
                if exists(b + 1):
                    bank = take_bank(pe, b, "x3t", 0)
                    wait(pe, s_xn3, b, 1, 2, NB)
                    for t in range(NT):
                        last = pe.transpose(bank[:, tile(t)], xn3[:, t, 0:D], ident[:])
                    last.then_inc(s_x3t, 1)
                if exists(b):
                    wait(pe, s_kvl, b, 1, 1, NB)
                    for j in range(PAIRS):
                        wait(pe, s_ql[j % 2], b, 4, j // 2 + 1, 4 * NB)
                        q_hi, q_lo = qn_hi[:, j % QN_SLOTS, :], qn_lo[:, j % QN_SLOTS, :]
                        pe.matmul(ps[:, OUT, :], kvw_hi[:, j, :], q_hi, start=(j == 0), stop=False)
                        pe.matmul(ps[:, OUT, :], kvw_lo[:, j, :], q_hi, start=False, stop=False)
                        pe.matmul(ps[:, OUT, :], kvw_hi[:, j, :], q_lo, start=False,
                                  stop=(j == PAIRS - 1)).then_inc(s_ao, 1)

            turns(pe, body)

        @block.scalar
        def _(act):
            def expert_tile(b, i):
                f = b - 1
                if exists(f):
                    wait(act, s_gate, f, FFN_TILES, i + 1, FFN_TILES * NB)
                    wait(act, s_h, f, FFN_TILES, i - 1, FFN_TILES * NB)
                    act.activation(silu[:, i % 2, :], ps[:, ring_bank("gate", i), :], ACT.Silu).then_inc(s_silu, 1)

            def phi_q_tile(b, j):
                wait(act, s_qps, b, 8, j + 1, 8 * NB)
                wait(act, s_ql[j % 2], b, 4, 0, 4 * NB)
                act.activation(phi_q[:, j, :], ps[:, ring_bank("phi_q", j), :], ACT.Relu).then_inc(s_q, 1)

            def high_half(b, j):
                wait(act, s_qn, b, 8, j + 1, 8 * NB)
                wait(act, s_ao, b, 8, j + 1 - QN_SLOTS, 8 * NB)
                act.copy(qn_hi[:, j % QN_SLOTS, :], phi_q[:, j, :]).then_inc(s_qh, 1)

            def body(b):
                f = b - 1
                if exists(b):
                    for n in range(8):
                        wait(act, s_kps, b, 8, n + 1, 8 * NB)
                        wait(act, s_g, b, G_BANKS, 0, G_BANKS * NB)
                        act.activation(phi_k[:, n // 2, n % 2 * 512:(n % 2 + 1) * 512],
                                       ps[:, ring_bank("phi_k", n), :], ACT.Relu).then_inc(s_k, 1)
                if exists(b):
                    for j in range(4):
                        phi_q_tile(b, j)
                if exists(f):
                    wait(act, s_x4t, f, 1, 1, NB)
                    wait(act, s_up, f, FFN_TILES, 0, FFN_TILES * NB)
                    act.copy(x4_hi[:], ps[:, ring_bank("x4t", 0), :]).then_inc(s_x4h, 1)
                if exists(b):
                    for j in range(4, 8):
                        phi_q_tile(b, j)
                if exists(f):
                    wait(act, s_dif, f, 1, 1, NB)
                    wait(act, s_comb, f, COMB_STEPS, 0, COMB_STEPS * NB)
                    act.activation(expo[:], dif[:], ACT.Exp).then_inc(s_expo, 1)
                if exists(b):
                    for i in range(G_BANKS):
                        pairs = min((i + 1) * PER_BANK, PAIRS) - i * PER_BANK
                        wait(act, s_g, b, G_BANKS, i + 1, G_BANKS * NB)
                        wait(act, s_gt, b, 2, 0, 2 * NB)
                        wait(act, s_ksum, b, 1, 0, NB)
                        act.copy(g_sb[:, i * PER_BANK:i * PER_BANK + pairs, :],
                                 ps[:, OUT + i, 0:pairs * (D + 2)].rearrange("p (j c) -> p j c", j=pairs)
                                 ).then_inc(s_gsb, 1)
                if exists(f):
                    wait(act, s_cps, f, 1, 1, NB)
                    wait(act, s_cb, f, FFN_TILES - 1, 0, (FFN_TILES - 1) * NB)
                    act.copy(comb_t[:], ps[:, ROUTE, :]).then_inc(s_ct, 1)
                expert_tile(b, 0)
                if exists(b):
                    for i in range(2):
                        wait(act, s_gt, b, 2, i + 1, 2 * NB)
                        wait(act, s_kv, b, 4, 0, 4 * NB)
                        act.copy(gt_sb[:, 4 * i:4 * i + 4, :],
                                 ps[:, OUT + i, :].rearrange("p (j c) -> p j c", j=4)).then_inc(s_gtsb, 1)
                expert_tile(b, 1)
                expert_tile(b, 2)
                if exists(b):
                    for n in range(4):
                        wait(act, s_kv, b, 4, n + 1, 4 * NB)
                        wait(act, s_kvl, b, 1, 0, NB)
                        act.copy(kvw[0:HD1, 2 * n:2 * n + 2, :],
                                 ps[0:HD1, ring_bank("kvw", n), :].rearrange("p (j i d) -> p j i d", j=2, i=2)
                                 [:, :, 0, :]).then_inc(s_kva, 1)
                        act.copy(kvw[HD1:P, 2 * n:2 * n + 2, :],
                                 ps[HD1:P, ring_bank("kvw", n), :].rearrange("p (j i d) -> p j i d", j=2, i=2)
                                 [:, :, 1, :]).then_inc(s_kva, 1)
                    wait(act, s_inv, b, 1, 1, NB)
                    wait(act, s_ipk, b, 1, 0, NB)
                    act.activation(inv_half[:], inv[:], ACT.Identity, scale=low[:, 0:1]).then_inc(s_ihalf, 1)
                expert_tile(b, 3)
                expert_tile(b, 4)
                if exists(b):
                    wait(act, s_kva, b, 8, 8, 8 * NB)
                    wait(act, s_ao, b, 8, 0, 8 * NB)
                    act.copy(kvw_hi[:], kvw[:]).then_inc(s_kvh, 1)
                    for j in range(QN_SLOTS):
                        high_half(b, j)
                if exists(b + 1):
                    wait(act, s_x3t, b, 1, 2, NB)
                    if exists(b):
                        wait(act, s_qps, b, 8, 8, 8 * NB)
                    act.copy(x3_hi[:], ps[:, ring_bank("x3t", 0), :]).then_inc(s_x3h, 1)
                if exists(b):
                    for j in range(QN_SLOTS, PAIRS):
                        high_half(b, j)
                    wait(act, s_ao, b, 8, 8, 8 * NB)
                    wait(act, s_att, b, 1, 0, NB)
                    act.copy(attn_t[:], ps[:, OUT, :]).then_inc(s_at, 1)

            act.wait_ge(s_set, 4)
            act.activation(norm[:, 0:1], minus_half[:, 0:1], ACT.Silu).then_inc(s_tab, 1)
            turns(act, body, lambda: act.wait_ge(s_w, W_ALL))

        @block.vector
        def _(dve):
            def experts_tile(b, i):
                f = b - 1
                if not exists(f):
                    return
                wait(dve, s_silu, f, FFN_TILES, i + 1, FFN_TILES * NB)
                if i:
                    wait(dve, s_cb, f, FFN_TILES - 1, i, (FFN_TILES - 1) * NB)
                    dve.tensor_tensor(silu[:, i % 2, :], ps[:, ring_bank("comb", i), :], silu[:, i % 2, :],
                                      ALU.mult).then_inc(s_hc, 1)
                    wait(dve, s_hc, f, FFN_TILES - 1, i, (FFN_TILES - 1) * NB)
                wait(dve, s_up, f, FFN_TILES, i + 1, FFN_TILES * NB)
                wait(dve, s_dn, f, 1, 0, NB)
                dve.tensor_tensor(h[:, i, :], ps[:, ring_bank("up", i), :], silu[:, i % 2, :],
                                  ALU.mult).then_inc(s_h, 1)

            def comb_weights(f):
                done = [0]

                def then(ins):
                    done[0] += 1
                    ins.then_inc(s_comb, 1)
                    wait(dve, s_comb, f, COMB_STEPS, done[0], COMB_STEPS * NB)

                def wide(v):
                    return v[:].unsqueeze(2).broadcast_to(t_e)

                logits = ps[:, ROUTE, 0:NT * E1].rearrange("p (t e) -> p t e", e=E1)
                wait(dve, s_lg, f, 1, 1, NB)
                then(dve.tensor_reduce(top[0][:], logits, AX.X, ALU.max))
                wait(dve, s_expo, f, 1, 0, NB)
                dve.tensor_tensor(dif[:], logits, wide(top[0]), ALU.subtract).then_inc(s_dif, 1)
                then(dve.tensor_tensor(cand[:], logits, wide(top[0]), ALU.is_equal))
                then(dve.scalar_tensor_tensor(cand[:], cand[:], -64.0, iota[:], ALU.mult, ALU.add))
                then(dve.tensor_reduce(first[0][:], cand[:], AX.X, ALU.min))
                then(dve.tensor_tensor(hot[0][:], iota64[:], wide(first[0]), ALU.is_equal))
                wait(dve, s_dif, f, 1, 1, NB)
                then(dve.scalar_tensor_tensor(dif2[:], hot[0][:], -BIG, dif[:], ALU.mult, ALU.add))
                then(dve.tensor_reduce(top[1][:], dif2[:], AX.X, ALU.max))
                then(dve.tensor_tensor(cand[:], dif2[:], wide(top[1]), ALU.is_equal))
                then(dve.scalar_tensor_tensor(cand[:], cand[:], -64.0, iota[:], ALU.mult, ALU.add))
                then(dve.tensor_reduce(first[1][:], cand[:], AX.X, ALU.min))
                then(dve.tensor_tensor(hot[1][:], iota64[:], wide(first[1]), ALU.is_equal))
                then(dve.tensor_tensor(hot[1][:], hot[0][:], hot[1][:], ALU.add))
                wait(dve, s_expo, f, 1, 1, NB)
                then(dve.tensor_tensor(w12[:], hot[1][:], expo[:], ALU.mult))
                then(dve.tensor_reduce(s12[:], w12[:], AX.X, ALU.add))
                then(dve.tensor_reduce(z[:], expo[:], AX.X, ALU.add))
                then(dve.scalar_tensor_tensor(den[:], z[:], 1e-9, s12[:], ALU.mult, ALU.add))
                then(dve.reciprocal(den[:], den[:]))
                then(dve.tensor_tensor(w12[:], w12[:], wide(den), ALU.mult))
                wait(dve, s_cps, f, 1, 0, NB)
                then(dve.tensor_copy(comb[:, :, 0:E1], w12[:]))
                then(dve.tensor_tensor(comb[:, :, E1:2 * E1], w12[:], comb[:, :, 0:E1].bitcast(F32), ALU.subtract))
                assert done[0] == COMB_STEPS

            def layernorm_stats(batch, stat, mv, veps, s_x, s_bn, s_ve):
                wait_first(dve, mem["own_dve"], s_x, batch, 1, 1, NB)
                for t in range(NT):
                    dve.bn_stats(stat[:, t, :], x_res[:, batch * NT + t, :]).then_inc(s_bn, 1)
                wait_first(dve, mem["own_dve"], s_bn, batch, 2 * NT, NT, 2 * NT * NB)
                for t in range(NT):
                    dve.bn_aggr(mv[:, t, :], stat[:, t, :]).then_inc(s_bn, 1)
                wait(dve, s_bn, batch, 2 * NT, 2 * NT, 2 * NT * NB)
                dve.tensor_scalar(veps[:], mv[:, :, 1], EPS, None, ALU.add).then_inc(s_ve, 1)

            def body(b):
                f, nxt = b - 1, b + 1
                if exists(f):
                    wait(dve, s_att, f, 1, 1, NB)
                    wait(dve, s_bo, f, 1, 1, NB)
                    x_f = x_res[:, ds(f * NT, NT), :]
                    dve.tensor_tensor(x_f, ps[:, OUT, :].rearrange("p (t d) -> p t d", t=NT), x_f,
                                      ALU.add).then_inc(s_x4, 1)
                    layernorm_stats(f, stat4, mv4, veps4, s_x4, s_bn4, s_ve4)
                    wait(dve, s_rstd4, f, 1, 1, NB)
                    wait(dve, s_x4t, f, 1, 0, NB)
                    for t in range(NT):
                        last = dve.tensor_scalar(xn4[:, t, :], x_res[:, f * NT + t, :], mv4[:, t, 0:1],
                                                 rstd4[:, t:t + 1], ALU.subtract, ALU.mult)
                    last.then_inc(s_xn4, 1)
                    wait(dve, s_x4h, f, 1, 1, NB)
                    dve.tensor_tensor(x4_lo[:], ps[:, ring_bank("x4t", 0), :], x4_hi[:].bitcast(F32),
                                      ALU.subtract).then_inc(s_x4l, 1)
                if exists(nxt):
                    wait(dve, s_y, nxt, 16 * NT, 16 * NT, 16 * NT * NB)
                    x_n = x_res[:, ds(nxt * NT, NT), :]
                    dve.tensor_tensor(x_n, y[:], x_n, ALU.add).then_inc(s_x3, 1)
                    layernorm_stats(nxt, stat3, mv3, veps3, s_x3, s_bn3, s_ve3)
                if exists(f):
                    comb_weights(f)
                experts_tile(b, 0)
                if exists(nxt):
                    wait(dve, s_rstd3, nxt, 1, 1, NB)
                    if exists(b):
                        wait(dve, s_g, b, G_BANKS, G_BANKS, G_BANKS * NB)
                    for t in range(NT):
                        last = dve.tensor_scalar(xn3[:, t, 0:D], x_res[:, nxt * NT + t, :], mv3[:, t, 0:1],
                                                 rstd3[:, t:t + 1], ALU.subtract, ALU.mult)
                    last.then_inc(s_xn3, 1)
                experts_tile(b, 1)
                experts_tile(b, 2)
                if exists(b):
                    wait(dve, s_n, b, 1, 1, NB)
                    wait(dve, s_inv, b, 1, 0, NB)
                    dve.tensor_scalar(norm[:], ps[:, NORM, :], 1e-6, None, ALU.add).then_inc(s_norm, 1)
                    wait(dve, s_norm, b, 1, 1, NB)
                    wait(dve, s_ipk, b, 1, 0, NB)
                    dve.reciprocal(inv[:], norm[:]).then_inc(s_inv, 1)
                    wait(dve, s_ihalf, b, 1, 1, NB)
                    wait(dve, s_bc, b, 8, 0, 8 * NB)
                    dve.tensor_tensor(inv_pk[:], inv[:], inv_half[:].bitcast(F32), ALU.subtract).then_inc(s_ipk, 1)
                experts_tile(b, 3)
                experts_tile(b, 4)
                if exists(b):
                    for j in range(PAIRS):
                        if j in LOW_BEFORE:
                            low_half(dve, b, LOW_BEFORE[j])
                        wait(dve, s_bc, b, 8, j + 1, 8 * NB)
                        wait(dve, s_n, b, 1, 1, NB)
                        dve.tensor_tensor(phi_q[:, j, :], ps[:, ring_bank("inv", j), :], phi_q[:, j, :],
                                          ALU.mult).then_inc(s_qn, 1)
                if exists(f):
                    wait(dve, s_dn, f, 1, 1, NB)
                    x_f = x_res[:, ds(f * NT, NT), :]
                    dve.tensor_tensor(x_f, ps[:, DOWN, :].rearrange("p (t d) -> p t d", t=NT), x_f,
                                      ALU.add).then_inc(s_xo, 1)
                if exists(nxt):
                    wait(dve, s_x3h, nxt, 1, 1, NB)
                    dve.tensor_tensor(x3_lo[:], ps[:, ring_bank("x3t", 0), :], x3_hi[:].bitcast(F32),
                                      ALU.subtract).then_inc(s_x3l, 1)
                if exists(b):
                    for j in range(1, PAIRS, 2):
                        if j not in LOW_BEFORE.values():
                            low_half(dve, b, j)

            dve.memset(xn3[:, :, D:D + 2], 1.0).then_inc(s_set, 1)
            dve.memset(ksum[:], 0.0).then_inc(s_set, 1)
            dve.memset(comb[:].bitcast(F32), 0.0).then_inc(s_set, 1)
            dve.memset(minus_half[:], -0.5).then_inc(s_set, 1)
            def weights():
                dve.wait_ge(s_w, W_ALL)
                for n, (dst, src) in enumerate(((w_gate, stage[:, 0]), (w_up, stage[:, 1]), (w_rt, w_rt_stage[:]))):
                    dve.tensor_copy(dst[:, 0], src).then_inc(s_split, 1)
                    dve.wait_ge(s_split, 2 * n + 1)
                    dve.tensor_tensor(dst[:, 1], src, dst[:, 0].bitcast(F32), ALU.subtract).then_inc(s_split, 1)
                dve.tensor_copy(spread[:], spread_stage[:, 0:PAIRS]).then_inc(s_split, 1)
                dve.tensor_copy(spread_e[:], spread_stage[:, PAIRS:]).then_inc(s_split, 1)

            dve.wait_ge(s_set, 4)
            turns(dve, body, weights)

        @block.gpsimd
        def _(pool):
            def gather(batch):
                wait_first(pool, mem["own_pool"], s_y, batch, 16 * NT, 0, 16 * NT * NB)
                pool.tensor_copy(pos_y[:], pos[:, ds(batch * NT, NT)]).then_inc(s_posy, 1)
                wait(pool, s_x3, batch, 1, 0, NB)
                wait_first(pool, mem["own_pool"], s_posy, batch, 1, 1, NB)
                for t in range(NT):
                    pool.indirect_dma_start(y[:, t, :], None, y_sorted[:, :],
                                            bass.IndirectOffsetOnAxis(ap=pos_y[:, t:t + 1], axis=0)).then_inc(s_y, 16)

            def body(b):
                f, nxt = b - 1, b + 1
                if exists(nxt):
                    gather(nxt)
                if exists(f):
                    wait(pool, s_ve4, f, 1, 1, NB)
                    wait(pool, s_xn4, f, 1, 0, NB)
                    pool.tensor_tensor(rstd4[:], veps4[:], minus_half[:], ALU.pow).then_inc(s_rstd4, 1)
                if exists(nxt):
                    wait(pool, s_ve3, nxt, 1, 1, NB)
                    wait(pool, s_xn3, nxt, 1, 0, NB)
                    pool.tensor_tensor(rstd3[:], veps3[:], minus_half[:], ALU.pow).then_inc(s_rstd3, 1)
                if exists(b):
                    wait(pool, s_gsb, b, G_BANKS, G_BANKS, G_BANKS * NB)
                    wait(pool, s_n, b, 1, 0, NB)
                    pool.tensor_tensor(ksum[:, :, 0:8], g_sb[:, :, D:D + 1].broadcast_to([P, PAIRS, 8]), own_head[:],
                                       ALU.mult).then_inc(s_ksum, 1)
                if exists(nxt):
                    wait(pool, s_xn3, nxt, 1, 1, NB)
                    x_n = x_res[:, ds(nxt * NT, NT), :]
                    pool.tensor_tensor(x_n, x_n, b_o[:].unsqueeze(1).broadcast_to([P, NT, D]),
                                       ALU.add).then_inc(s_bo, 1)
                if exists(b):
                    wait(pool, s_kvh, b, 1, 1, NB)
                    wait(pool, s_ao, b, 8, 0, 8 * NB)
                    pool.tensor_tensor(kvw_lo[:], kvw[:], kvw_hi[:].bitcast(F32), ALU.subtract).then_inc(s_kvl, 1)
                    for j in range(0, PAIRS, 2):
                        low_half(pool, b, j)

            pool.wait_ge(s_set, 4)
            pool.wait_ge(s_wb, 16)
            turns(pool, body, lambda: pool.wait_ge(s_w, W_ALL))


def pairs_diagonal(w):
    import numpy as np

    heads, rows, cols = w.shape
    out = np.zeros((2 * rows, heads // 2, 2 * cols), np.float32)
    for i in range(2):
        out[i * rows:(i + 1) * rows, :, i * cols:(i + 1) * cols] = w[i::2].transpose(1, 0, 2)
    return out


def host_layouts(a):
    import numpy as np

    f = np.float32
    w_qkv, b_qkv = a["L0_attn_w_qkv"], a["L0_attn_b_qkv"]
    w4 = {n: np.zeros((D, H0, SLOT), f) for n in "qk"}
    b4 = {n: np.zeros((H0, SLOT), f) for n in "qk"}
    for i, n in enumerate("qk"):
        w = w_qkv[:, i * D:(i + 1) * D].reshape(D, H0, HD0)
        b = b_qkv[i * D:(i + 1) * D].reshape(H0, HD0)
        for c in range(3):
            w4[n][:, :, c * HD0:(c + 1) * HD0] = w
            b4[n][:, c * HD0:(c + 1) * HD0] = b
    b4["k"][:, MAXROW_HI] = 1.0
    b4["k"][:, MAXROW_LO] = 1.0
    b_qk = np.stack([b4["q"].reshape(GROUPS, P).T, b4["k"].reshape(GROUPS, P).T], axis=1)
    lo = np.zeros((P, 2), f)
    row = np.arange(P) % SLOT
    lo[:, 0] = (row >= 2 * HD0) & (row < 3 * HD0)
    lo[:, 1] = (row >= HD0) & (row < 2 * HD0)
    rep = lambda v: np.broadcast_to(v, (P, v.shape[0]))
    i = np.arange(P)
    by_middle = lambda w: w.transpose(1, 0, 2).reshape(D, -1)
    spread, own_head = np.zeros((P, PAIRS, P), f), np.zeros((P, PAIRS, 8), f)
    for j in range(PAIRS):
        for c in range(2):
            for half in range(2):
                spread[LOG_ROWS * (j % 4) + 2 * (j // 4) + c + 4 * half, j, HD1 * c:HD1 * (c + 1)] = 1.0
                own_head[HD1 * c:HD1 * (c + 1), j, 2 * (j // 4) + c + 4 * half] = 1.0
    low = np.zeros((P, 1), f)
    low[np.arange(P) % LOG_ROWS // 4 == 1] = 1.0
    spread_e = np.zeros((P, FFN_TILES - 1, P), f)
    for e in range(E1):
        for half in range(2):
            spread_e[e + E1 * half, e // 4, MID1 * (e % 4):MID1 * (e % 4 + 1)] = 1.0
    return {
        "x": a["L0_attn_x"].reshape(NB * SEQ, D),
        "w_q4": w4["q"].reshape(D, -1), "w_k4": w4["k"].reshape(D, -1), "w_v0": w_qkv[:, 2 * D:],
        "b_qk": b_qk, "lo_rows": lo, "b_v": rep(b_qkv[2 * D:]), "b_o0": rep(a["L0_attn_b_out"]),
        "w_o0": a["L0_attn_w_out"], "router0": a["L0_ffn_gate_w"],
        "iota_e": rep(np.arange(E0, dtype=f)), "iota_q": rep(np.arange(SLOTS, dtype=f)),
        "before": (i[:, None] < i[None, :]).astype(f),
        "w_qkv1_t": a["L1_attn_W_qkv"].reshape(D, 24, P).transpose(2, 1, 0),
        "rf1": pairs_diagonal(a["L1_attn_RF"]), "w_out1": pairs_diagonal(a["L1_attn_W_out"].reshape(H1, HD1, D)),
        "w_shared0": np.concatenate([a["L0_ffn_shared_gate_w"], a["L0_ffn_shared_up_w"]], axis=1),
        "w_shared_dn0": a["L0_ffn_shared_down_w"].reshape(2, P, D).transpose(1, 0, 2),
        "w_gate0": a["L0_ffn_routed_gate_w"].transpose(1, 0, 2), "w_up0": a["L0_ffn_routed_up_w"].transpose(1, 0, 2),
        "w_down0": a["L0_ffn_routed_down_w"].reshape(E0, 2, P, D).transpose(2, 0, 1, 3),
        "w_gate1": np.concatenate([by_middle(a["L1_ffn_wg_s"]), by_middle(a["L1_ffn_wg_r"])], axis=1),
        "w_up1": np.concatenate([by_middle(a["L1_ffn_wu_s"]), by_middle(a["L1_ffn_wu_r"])], axis=1),
        "w_down1": np.concatenate([a["L1_ffn_wd_s"].reshape(-1, D), a["L1_ffn_wd_r"].reshape(-1, D)])
                     .reshape(FFN_TILES, P, D).transpose(1, 0, 2),
        "router1": a["L1_ffn_router_w"], "b_o1": rep(a["L1_attn_b_out"]),
        "spread": spread, "spread_e": spread_e, "low": low, "own_head": own_head,
        "iota1": np.broadcast_to(np.arange(E1, dtype=f), (P, NT, E1)),
        "iota64": np.broadcast_to(np.arange(E1, dtype=f) - f(64), (P, NT, E1)),
        "mask": np.where(i[None, :] < i[:, None], f(-BIG), f(0)), "ident": np.eye(P, dtype=f),
    }


def two_layers(nc, dram, out):
    x_sorted = nc.dram_tensor("x_sorted", (SLOTS * P, D), F32, kind="Internal").ap()
    y_sorted = nc.dram_tensor("y_sorted", (SLOTS * P, D), F32, kind="Internal").ap()
    with ExitStack() as ctx:
        def sb(name, shape, dt=F32):
            return ctx.enter_context(nc.sbuf_tensor(name, shape, dt))

        mem = {"x_res": sb("x_res", [P, TILES, D]), "ident": sb("ident", [P, P]), "ident_r": sb("ident_r", [P, P], F32R),
               "mean2": sb("mean2", [P, TILES]), "rstd2": sb("rstd2", [P, TILES]),
               "pos": sb("pos", [P, TILES], I32), "score": sb("score", [P, TILES]),
               "slot_expert": sb("slot_expert", [P, SLOTS], I32), "slots_end": sb("slots_end", [P, E0]),
               "iota_q": sb("iota_q", [P, SLOTS]),
               "w_qf": sb("w_qf", [P, 2, H1 * HD1], F32R), "w_kf": sb("w_kf", [P, 2, H1 * HD1], F32R),
               "w_vo": sb("w_vo", [P, H1, D])}
        for name in ("own_sp", "own_act", "own_dve", "own_pool"):
            mem[name] = ctx.enter_context(nc.semaphore(name))
        mem["w_sh_stage"] = sb("w_sh_stage", [P, 2 * MID0])
        mem["w_sd"] = sb("w_sd", [P, 2, D])
        with ExitStack() as inner:
            for name, shape in (("logits", [P, TILES, E0]),
                                ("w_t", [P, 24, D]),
                                ("rf", [P, 8, P]),
                                ("w_out1", [P, 8, 2 * D]),
                                ("iota_e", [P, E0]),
                                ("before", [P, P])):
                mem[name] = inner.enter_context(nc.sbuf_tensor(name, shape, F32))
            mem["preload"] = [(mem[tensor][:], name) for tensor, name in (
                ("w_t", "w_qkv1_t"), ("rf", "rf1"), ("w_out1", "w_out1"), ("iota_e", "iota_e"),
                ("iota_q", "iota_q"), ("before", "before"), ("w_sh_stage", "w_shared0"), ("w_sd", "w_shared_dn0"))]
            layer0_attention(nc, mem, dram, x_sorted)
            routing(nc, mem, dram)
        layer0_experts(nc, mem, dram, x_sorted, y_sorted)
        layer1(nc, mem, dram, y_sorted, out)


def kernel(**inputs):
    import numpy as np
    import concourse.bacc as bacc
    from concourse.bass_utils import run_bass_kernel_spmd

    nc = bacc.Bacc("TRN2", target_bir_lowering=False, num_devices=1)
    arrays, dram = {}, {}
    for name, value in host_layouts({n: np.asarray(v) for n, v in inputs.items()}).items():
        value = np.ascontiguousarray(value)
        arrays["in_" + name] = value
        dram[name] = nc.dram_tensor("in_" + name, value.shape, mybir.dt.from_np(value.dtype), kind="ExternalInput").ap()
    out = nc.dram_tensor("out", (NB * SEQ, D), F32, kind="ExternalOutput").ap()
    two_layers(nc, dram, out)
    r = run_bass_kernel_spmd(nc, [arrays], core_ids=[0])
    return r.results[0]["out"].reshape(NB, SEQ, D)
```
